# Optimizing a Trainium2 kernel written in Bass

```python
import numpy as np
import jax
import jax.numpy as jnp

def _softmax(x, axis=-1):
    return jax.nn.softmax(x, axis=axis)

def _gelu(x):
    return jax.nn.gelu(x, approximate=True)

def _silu(x):
    return jax.nn.silu(x)

def _sigmoid(x):
    return jax.nn.sigmoid(x)

def _layernorm(x, axis=-1, eps=1e-05):
    m = jnp.mean(x, axis=axis, keepdims=True)
    v = jnp.var(x, axis=axis, keepdims=True)
    return (x - m) / jnp.sqrt(v + eps)

def _scatter_add(tgt, idx, src, axis=0):
    return tgt.at[idx].add(src)

def _segment_sum(src, seg, n):
    return jax.ops.segment_sum(src, seg, n)
kernel_name = 'mk_sandwich_d4_jaxref_r4_cbab62'

def setup_inputs(seed: int=0):
    np.random.seed(seed)
    _w = jnp.asarray

    def _L0_attn_setup():
        import jax, jax.numpy as jnp
        import numpy as np
        from jax.scipy.linalg import solve_triangular
        B, L, D, H = (1, 512, 256, 4)
        DK = DV = D // H
        CONV = 4
        FIR_S, FIR_M, FIR_L = (3, 15, 63)
        CHUNK = 32

        def _l2norm(x):
            return x * jax.lax.rsqrt(jnp.sum(x * x, -1, keepdims=True) + 1e-06)

        def _short_conv(x, w):
            K = w.shape[-1]
            l = x.shape[1]
            xp = jnp.pad(x, ((0, 0), (K - 1, 0), (0, 0)))
            y = sum((xp[:, j:j + l, :] * w[:, j] for j in range(K)))
            return jax.nn.silu(y)

        def _fir(x, filt):
            b, l, h, d = x.shape
            K = filt.shape[-1]
            xf = jnp.transpose(x.reshape(b, l, h * d), (0, 2, 1))
            y = jax.lax.conv_general_dilated(xf, filt.reshape(h * d, 1, K), (1,), [(K - 1, 0)], feature_group_count=h * d)
            return jnp.transpose(y, (0, 2, 1)).reshape(b, l, h, d)

        def _delta_rule_chunkwise(q, k, v, beta):
            b, h, Lq, dk = q.shape
            c = CHUNK
            n = Lq // c
            q = _l2norm(q)
            k = _l2norm(k)
            v = v * beta[..., None]
            kb = k * beta[..., None]
            rs = lambda t: t.reshape(b, h, n, c, t.shape[-1])
            qc, kc, vc, kbc = (rs(q), rs(k), rs(v), rs(kb))
            tri_strict = jnp.tril(jnp.ones((c, c), bool), -1)
            A = jnp.where(tri_strict, -(kbc @ jnp.swapaxes(kc, -1, -2)), 0.0)
            eye = jnp.eye(c, dtype=q.dtype)
            M = eye - A
            T = solve_triangular(M, jnp.broadcast_to(eye, M.shape), lower=True)
            u = T @ vc
            w = T @ kbc
            causal = jnp.tril(jnp.ones((c, c), bool))

            def step(S, inp):
                q_i, k_i, u_i, w_i = inp
                attn = jnp.where(causal, q_i @ jnp.swapaxes(k_i, -1, -2), 0.0)
                u_adj = u_i - w_i @ S
                o_i = q_i @ S + attn @ u_adj
                return (S + jnp.swapaxes(k_i, -1, -2) @ u_adj, o_i)
            S0 = jnp.zeros((b, h, dk, v.shape[-1]), q.dtype)
            mv = lambda t: jnp.moveaxis(t, 2, 0)
            _, o = jax.lax.scan(step, S0, (mv(qc), mv(kc), mv(u), mv(w)))
            return jnp.moveaxis(o, 0, 2).reshape(b, h, Lq, -1)

        def _rmsnorm(x, w, eps=1e-05):
            return x * jax.lax.rsqrt(jnp.mean(x * x, -1, keepdims=True) + eps) * w
        key = jax.random.key(seed)
        ks = jax.random.split(key, 16)
        wn = lambda k, shape, s: jax.random.normal(k, shape, jnp.float32) * s

        def fir_init(k, K):
            f = jnp.zeros((H, DV, K), jnp.float32).at[..., -1].set(1.0)
            return f + wn(k, (H, DV, K), 0.01)
        return {'hidden_states': jax.random.normal(ks[0], (B, L, D), jnp.float32), 'Wq': wn(ks[1], (D, D), 0.02), 'Wk': wn(ks[2], (D, D), 0.02), 'Wv': wn(ks[3], (D, D), 0.02), 'Wb': wn(ks[4], (H, D), 0.02), 'conv_q': wn(ks[5], (D, CONV), 0.1), 'conv_k': wn(ks[6], (D, CONV), 0.1), 'conv_v': wn(ks[7], (D, CONV), 0.1), 'fir_s': fir_init(ks[8], FIR_S), 'fir_m': fir_init(ks[9], FIR_M), 'fir_l': fir_init(ks[10], FIR_L), 'gate_w': wn(ks[11], (H, 5, D), 1.0 / np.sqrt(D)), 'gate_b': jnp.zeros((H, 5), jnp.float32), 'log_temp': jnp.zeros((H, 1), jnp.float32), 'eps_param': jnp.full((H, 1), 0.02, jnp.float32), 'norm_w': jnp.ones((DV,), jnp.float32), 'Wo': wn(ks[12], (D, D), 0.02)}
    _L0_attn_in = _L0_attn_setup()

    def _L0_ffn_setup():
        import jax, jax.numpy as jnp
        import numpy as np
        D_MODEL = 256
        key = jax.random.key(seed)
        k_x, k_w, k_a1, k_a2 = jax.random.split(key, 4)
        x = jax.random.normal(k_x, (4, 512, D_MODEL), dtype=jnp.float32)
        weight = jax.random.normal(k_w, (D_MODEL, D_MODEL), dtype=jnp.float32) * 0.02
        aux_weight1 = jax.random.normal(k_a1, (D_MODEL, D_MODEL), dtype=jnp.float32) * 0.02
        aux_weight2 = jax.random.normal(k_a2, (D_MODEL, D_MODEL), dtype=jnp.float32) * 0.02
        bias = jnp.zeros((D_MODEL,), dtype=jnp.float32)
        return {'x': x, 'weight': weight, 'aux_weight1': aux_weight1, 'aux_weight2': aux_weight2, 'bias': bias}
    _L0_ffn_in = _L0_ffn_setup()

    def _L1_attn_setup():
        import jax, jax.numpy as jnp
        import numpy as np
        import math
        NUM_HEADS = 8
        EMB = 256
        HEAD_DIM = 128
        B, T = (1, 1024)

        def sinusoidal_pe(T, d, dtype=jnp.float32):
            pos = jnp.arange(T, dtype=dtype)[:, None]
            inv_freq = jnp.exp(-math.log(10000.0) * jnp.arange(0, d, 2, dtype=dtype) / d)
            ang = pos * inv_freq[None, :]
            pe = jnp.zeros((T, d), dtype=dtype)
            pe = pe.at[:, 0::2].set(jnp.sin(ang))
            pe = pe.at[:, 1::2].set(jnp.cos(ang))
            return pe
        key = jax.random.key(seed)
        ks = jax.random.split(key, 6)
        s = lambda fan_in: 1.0 / math.sqrt(fan_in)
        x = jax.random.normal(ks[0], (B, T, EMB), dtype=jnp.float32)
        Wq = jax.random.normal(ks[1], (EMB, NUM_HEADS * HEAD_DIM), dtype=jnp.float32) * s(EMB)
        bq = jax.random.normal(ks[2], (NUM_HEADS * HEAD_DIM,), dtype=jnp.float32) * s(EMB)
        Wkv = jax.random.normal(ks[3], (EMB, 2 * HEAD_DIM), dtype=jnp.float32) * s(EMB)
        bkv = jax.random.normal(ks[4], (2 * HEAD_DIM,), dtype=jnp.float32) * s(EMB)
        Wo = jax.random.normal(ks[5], (NUM_HEADS * HEAD_DIM, EMB), dtype=jnp.float32) * s(NUM_HEADS * HEAD_DIM)
        return {'x': x, 'Wq': Wq, 'bq': bq, 'Wkv': Wkv, 'bkv': bkv, 'Wo': Wo}
    _L1_attn_in = _L1_attn_setup()

    def _L1_ffn_setup():
        import jax, jax.numpy as jnp
        import numpy as np
        CAP_FACTOR = 1.5
        key = jax.random.key(seed)
        ks = jax.random.split(key, 6)
        E, S, D, M = (48, 4, 256, 256)
        K = D // S
        x = jax.random.normal(ks[0], (4, 1024, D), dtype=jnp.float32)
        Wr = jax.random.normal(ks[1], (E, D), dtype=jnp.float32) * 0.02
        W1 = jax.random.normal(ks[2], (E, S, D, M), dtype=jnp.float32) * (1.0 / np.sqrt(D))
        b1 = jnp.zeros((E, S, M), dtype=jnp.float32)
        W2 = jax.random.normal(ks[3], (E, S, M, K), dtype=jnp.float32) * (1.0 / np.sqrt(M))
        b2 = jnp.zeros((E, S, K), dtype=jnp.float32)
        return {'x': x, 'Wr': Wr, 'W1': W1, 'b1': b1, 'W2': W2, 'b2': b2}
    _L1_ffn_in = _L1_ffn_setup()

    def _L2_attn_setup():
        import jax, jax.numpy as jnp
        import numpy as np
        N_HEADS = 16
        EPS = 1e-06
        key = jax.random.key(seed)
        ks = jax.random.split(key, 5)
        B, N, D, H = (4, 512, 256, N_HEADS)
        x = jax.random.normal(ks[0], (B, N, D), dtype=jnp.float32)
        Wq = jax.random.normal(ks[1], (D, D), dtype=jnp.float32) * D ** (-0.5)
        Wk = jax.random.normal(ks[2], (D, D), dtype=jnp.float32) * D ** (-0.5)
        Wv = jax.random.normal(ks[3], (D, D), dtype=jnp.float32) * D ** (-0.5)
        Wo = jax.random.normal(ks[4], (D, D), dtype=jnp.float32) * D ** (-0.5)
        q_scale = jnp.ones((H,), dtype=jnp.float32)
        k_scale = jnp.ones((H,), dtype=jnp.float32)
        return {'x': x, 'Wq': Wq, 'Wk': Wk, 'Wv': Wv, 'Wo': Wo, 'q_scale': q_scale, 'k_scale': k_scale}
    _L2_attn_in = _L2_attn_setup()

    def _L2_ffn_setup():
        import jax, jax.numpy as jnp
        import numpy as np
        DIM = 256
        HIDDEN = 768
        SCALE = 1.0 / 127.0

        def _dequant(w_int, dtype):
            return w_int.astype(dtype) * jnp.asarray(SCALE, dtype)
        key = jax.random.key(seed)
        k_x, k_g, k_u, k_d = jax.random.split(key, 4)
        x = jax.random.normal(k_x, (4, 512, DIM), dtype=jnp.float32)
        w_gate = jax.random.randint(k_g, (HIDDEN, DIM), -127, 128, dtype=jnp.int32)
        w_up = jax.random.randint(k_u, (HIDDEN, DIM), -127, 128, dtype=jnp.int32)
        w_down = jax.random.randint(k_d, (DIM, HIDDEN), -127, 128, dtype=jnp.int32)
        return {'x': x, 'w_gate': w_gate, 'w_up': w_up, 'w_down': w_down}
    _L2_ffn_in = _L2_ffn_setup()

    def _L3_attn_setup():
        import jax, jax.numpy as jnp
        import numpy as np
        from math import ceil
        DIM = 256
        D_STATE = 16
        D_CONV = 4
        EXPAND = 2
        DI = DIM * EXPAND
        DT_RANK = ceil(DIM / 16)

        def _mamba(x, W_in, W_conv, b_conv, W_xproj, W_dt, b_dt, A_log, D, W_out):
            b, l, _ = x.shape
            silu = jax.nn.silu
            xr = x @ W_in.T
            xc, res = (xr[..., :DI], xr[..., DI:])
            u = jnp.transpose(xc, (0, 2, 1))
            u = jax.lax.conv_general_dilated(u, W_conv, window_strides=(1,), padding=[(D_CONV - 1, 0)], dimension_numbers=('NCH', 'OIH', 'NCH'), feature_group_count=DI)
            u = silu(u + b_conv[None, :, None])
            x_dbl = jnp.einsum('bdl,ed->ble', u, W_xproj)
            dt = x_dbl[..., :DT_RANK]
            B = x_dbl[..., DT_RANK:DT_RANK + D_STATE]
            C = x_dbl[..., DT_RANK + D_STATE:]
            delta = jax.nn.softplus(dt @ W_dt.T + b_dt)
            A = -jnp.exp(A_log)
            dA = jnp.exp(jnp.einsum('bld,dn->lbdn', delta, A))
            dBu = jnp.einsum('bld,bln,bdl->lbdn', delta, B, u)
            Cl = jnp.transpose(C, (1, 0, 2))

            def step(h, inp):
                dA_t, dBu_t, c_t = inp
                h = dA_t * h + dBu_t
                return (h, jnp.einsum('bdn,bn->bd', h, c_t))
            h0 = jnp.zeros((b, DI, D_STATE), u.dtype)
            _, ys = jax.lax.scan(step, h0, (dA, dBu, Cl))
            y = jnp.transpose(ys, (1, 2, 0)) + u * D[None, :, None]
            y = jnp.transpose(y, (0, 2, 1)) * silu(res)
            return y @ W_out.T
        key = jax.random.key(seed)
        ks = jax.random.split(key, 8)
        b, l = (2, 256)
        sc = lambda k, shp, s=0.02: jax.random.normal(k, shp, jnp.float32) * s
        x = jax.random.normal(ks[0], (b, l, DIM), jnp.float32)
        W_in = sc(ks[1], (2 * DI, DIM))
        W_conv = sc(ks[2], (DI, 1, D_CONV), 0.1)
        b_conv = jnp.zeros((DI,), jnp.float32)
        W_xproj = sc(ks[3], (DT_RANK + 2 * D_STATE, DI))
        W_dt = sc(ks[4], (DI, DT_RANK), 0.1)
        b_dt = jnp.zeros((DI,), jnp.float32)
        A_log = jnp.log(jnp.tile(jnp.arange(1, D_STATE + 1, dtype=jnp.float32)[None, :], (DI, 1)))
        D = jnp.ones((DI,), jnp.float32)
        W_out = sc(ks[5], (DIM, DI))
        return dict(x=x, W_in=W_in, W_conv=W_conv, b_conv=b_conv, W_xproj=W_xproj, W_dt=W_dt, b_dt=b_dt, A_log=A_log, D=D, W_out=W_out)
    _L3_attn_in = _L3_attn_setup()

    def _L3_ffn_setup():
        import jax, jax.numpy as jnp
        import numpy as np
        D_MODEL = 256
        NUM_EXPERTS = 8
        HIDDEN = 512
        TOP_K = 2
        SHARED_HIDDEN = 512
        BATCH, SEQ = (4, 512)
        key = jax.random.key(seed)
        ks = jax.random.split(key, 8)
        s = 1.0 / np.sqrt(D_MODEL)
        sh = 1.0 / np.sqrt(HIDDEN)
        return {'x': jax.random.normal(ks[0], (BATCH, SEQ, D_MODEL), dtype=jnp.float32), 'w_router': jax.random.normal(ks[1], (D_MODEL, NUM_EXPERTS), dtype=jnp.float32) * s, 'w1': jax.random.normal(ks[2], (NUM_EXPERTS, D_MODEL, HIDDEN), dtype=jnp.float32) * s, 'w3': jax.random.normal(ks[3], (NUM_EXPERTS, D_MODEL, HIDDEN), dtype=jnp.float32) * s, 'w2': jax.random.normal(ks[4], (NUM_EXPERTS, HIDDEN, D_MODEL), dtype=jnp.float32) * sh, 'ws1': jax.random.normal(ks[5], (D_MODEL, SHARED_HIDDEN), dtype=jnp.float32) * s, 'ws3': jax.random.normal(ks[6], (D_MODEL, SHARED_HIDDEN), dtype=jnp.float32) * s, 'ws2': jax.random.normal(ks[7], (SHARED_HIDDEN, D_MODEL), dtype=jnp.float32) * sh}
    _L3_ffn_in = _L3_ffn_setup()
    _d = {'L0_attn_hidden_states': _L0_attn_in['hidden_states'], 'L0_attn_Wq': _L0_attn_in['Wq'], 'L0_attn_Wk': _L0_attn_in['Wk'], 'L0_attn_Wv': _L0_attn_in['Wv'], 'L0_attn_Wb': _L0_attn_in['Wb'], 'L0_attn_conv_q': _L0_attn_in['conv_q'], 'L0_attn_conv_k': _L0_attn_in['conv_k'], 'L0_attn_conv_v': _L0_attn_in['conv_v'], 'L0_attn_fir_s': _L0_attn_in['fir_s'], 'L0_attn_fir_m': _L0_attn_in['fir_m'], 'L0_attn_fir_l': _L0_attn_in['fir_l'], 'L0_attn_gate_w': _L0_attn_in['gate_w'], 'L0_attn_gate_b': _L0_attn_in['gate_b'], 'L0_attn_log_temp': _L0_attn_in['log_temp'], 'L0_attn_eps_param': _L0_attn_in['eps_param'], 'L0_attn_norm_w': _L0_attn_in['norm_w'], 'L0_attn_Wo': _L0_attn_in['Wo'], 'L0_ffn_weight': _L0_ffn_in['weight'], 'L0_ffn_aux_weight1': _L0_ffn_in['aux_weight1'], 'L0_ffn_aux_weight2': _L0_ffn_in['aux_weight2'], 'L0_ffn_bias': _L0_ffn_in['bias'], 'L1_attn_Wq': _L1_attn_in['Wq'], 'L1_attn_bq': _L1_attn_in['bq'], 'L1_attn_Wkv': _L1_attn_in['Wkv'], 'L1_attn_bkv': _L1_attn_in['bkv'], 'L1_attn_Wo': _L1_attn_in['Wo'], 'L1_ffn_Wr': _L1_ffn_in['Wr'], 'L1_ffn_W1': _L1_ffn_in['W1'], 'L1_ffn_b1': _L1_ffn_in['b1'], 'L1_ffn_W2': _L1_ffn_in['W2'], 'L1_ffn_b2': _L1_ffn_in['b2'], 'L2_attn_Wq': _L2_attn_in['Wq'], 'L2_attn_Wk': _L2_attn_in['Wk'], 'L2_attn_Wv': _L2_attn_in['Wv'], 'L2_attn_Wo': _L2_attn_in['Wo'], 'L2_attn_q_scale': _L2_attn_in['q_scale'], 'L2_attn_k_scale': _L2_attn_in['k_scale'], 'L2_ffn_w_gate': _L2_ffn_in['w_gate'], 'L2_ffn_w_up': _L2_ffn_in['w_up'], 'L2_ffn_w_down': _L2_ffn_in['w_down'], 'L3_attn_W_in': _L3_attn_in['W_in'], 'L3_attn_W_conv': _L3_attn_in['W_conv'], 'L3_attn_b_conv': _L3_attn_in['b_conv'], 'L3_attn_W_xproj': _L3_attn_in['W_xproj'], 'L3_attn_W_dt': _L3_attn_in['W_dt'], 'L3_attn_b_dt': _L3_attn_in['b_dt'], 'L3_attn_A_log': _L3_attn_in['A_log'], 'L3_attn_D': _L3_attn_in['D'], 'L3_attn_W_out': _L3_attn_in['W_out'], 'L3_ffn_w_router': _L3_ffn_in['w_router'], 'L3_ffn_w1': _L3_ffn_in['w1'], 'L3_ffn_w3': _L3_ffn_in['w3'], 'L3_ffn_w2': _L3_ffn_in['w2'], 'L3_ffn_ws1': _L3_ffn_in['ws1'], 'L3_ffn_ws3': _L3_ffn_in['ws3'], 'L3_ffn_ws2': _L3_ffn_in['ws2']}
    _x0 = _d['L0_attn_hidden_states']
    _d['L0_attn_hidden_states'] = jax.random.normal(jax.random.fold_in(jax.random.key(seed), 1), (8, 512, 256), dtype=_x0.dtype)
    del _x0
    return _d

def reference(L0_attn_hidden_states, L0_attn_Wq, L0_attn_Wk, L0_attn_Wv, L0_attn_Wb, L0_attn_conv_q, L0_attn_conv_k, L0_attn_conv_v, L0_attn_fir_s, L0_attn_fir_m, L0_attn_fir_l, L0_attn_gate_w, L0_attn_gate_b, L0_attn_log_temp, L0_attn_eps_param, L0_attn_norm_w, L0_attn_Wo, L0_ffn_weight, L0_ffn_aux_weight1, L0_ffn_aux_weight2, L0_ffn_bias, L1_attn_Wq, L1_attn_bq, L1_attn_Wkv, L1_attn_bkv, L1_attn_Wo, L1_ffn_Wr, L1_ffn_W1, L1_ffn_b1, L1_ffn_W2, L1_ffn_b2, L2_attn_Wq, L2_attn_Wk, L2_attn_Wv, L2_attn_Wo, L2_attn_q_scale, L2_attn_k_scale, L2_ffn_w_gate, L2_ffn_w_up, L2_ffn_w_down, L3_attn_W_in, L3_attn_W_conv, L3_attn_b_conv, L3_attn_W_xproj, L3_attn_W_dt, L3_attn_b_dt, L3_attn_A_log, L3_attn_D, L3_attn_W_out, L3_ffn_w_router, L3_ffn_w1, L3_ffn_w3, L3_ffn_w2, L3_ffn_ws1, L3_ffn_ws3, L3_ffn_ws2):

    def _L0_attn_ref(hidden_states, Wq, Wk, Wv, Wb, conv_q, conv_k, conv_v, fir_s, fir_m, fir_l, gate_w, gate_b, log_temp, eps_param, norm_w, Wo):
        import jax, jax.numpy as jnp
        import numpy as np
        from jax.scipy.linalg import solve_triangular
        B, L, D, H = (1, 512, 256, 4)
        DK = DV = D // H
        CONV = 4
        FIR_S, FIR_M, FIR_L = (3, 15, 63)
        CHUNK = 32

        def _l2norm(x):
            return x * jax.lax.rsqrt(jnp.sum(x * x, -1, keepdims=True) + 1e-06)

        def _short_conv(x, w):
            K = w.shape[-1]
            l = x.shape[1]
            xp = jnp.pad(x, ((0, 0), (K - 1, 0), (0, 0)))
            y = sum((xp[:, j:j + l, :] * w[:, j] for j in range(K)))
            return jax.nn.silu(y)

        def _fir(x, filt):
            b, l, h, d = x.shape
            K = filt.shape[-1]
            xf = jnp.transpose(x.reshape(b, l, h * d), (0, 2, 1))
            y = jax.lax.conv_general_dilated(xf, filt.reshape(h * d, 1, K), (1,), [(K - 1, 0)], feature_group_count=h * d)
            return jnp.transpose(y, (0, 2, 1)).reshape(b, l, h, d)

        def _delta_rule_chunkwise(q, k, v, beta):
            b, h, Lq, dk = q.shape
            c = CHUNK
            n = Lq // c
            q = _l2norm(q)
            k = _l2norm(k)
            v = v * beta[..., None]
            kb = k * beta[..., None]
            rs = lambda t: t.reshape(b, h, n, c, t.shape[-1])
            qc, kc, vc, kbc = (rs(q), rs(k), rs(v), rs(kb))
            tri_strict = jnp.tril(jnp.ones((c, c), bool), -1)
            A = jnp.where(tri_strict, -(kbc @ jnp.swapaxes(kc, -1, -2)), 0.0)
            eye = jnp.eye(c, dtype=q.dtype)
            M = eye - A
            T = solve_triangular(M, jnp.broadcast_to(eye, M.shape), lower=True)
            u = T @ vc
            w = T @ kbc
            causal = jnp.tril(jnp.ones((c, c), bool))

            def step(S, inp):
                q_i, k_i, u_i, w_i = inp
                attn = jnp.where(causal, q_i @ jnp.swapaxes(k_i, -1, -2), 0.0)
                u_adj = u_i - w_i @ S
                o_i = q_i @ S + attn @ u_adj
                return (S + jnp.swapaxes(k_i, -1, -2) @ u_adj, o_i)
            S0 = jnp.zeros((b, h, dk, v.shape[-1]), q.dtype)
            mv = lambda t: jnp.moveaxis(t, 2, 0)
            _, o = jax.lax.scan(step, S0, (mv(qc), mv(kc), mv(u), mv(w)))
            return jnp.moveaxis(o, 0, 2).reshape(b, h, Lq, -1)

        def _rmsnorm(x, w, eps=1e-05):
            return x * jax.lax.rsqrt(jnp.mean(x * x, -1, keepdims=True) + eps) * w
        b, l, d = hidden_states.shape
        q = _short_conv(hidden_states @ Wq.T, conv_q).reshape(b, l, H, DK)
        k = _short_conv(hidden_states @ Wk.T, conv_k).reshape(b, l, H, DK)
        v_direct = _short_conv(hidden_states @ Wv.T, conv_v).reshape(b, l, H, DV)
        beta = jax.nn.sigmoid(hidden_states @ Wb.T)
        tp = lambda t: jnp.transpose(t, (0, 2, 1, 3))
        delta_out = tp(_delta_rule_chunkwise(tp(q), tp(k), tp(v_direct), jnp.transpose(beta, (0, 2, 1))))
        local_s = _fir(v_direct, fir_s)
        local_m = _fir(v_direct, fir_m)
        local_l = _fir(v_direct, fir_l)
        logits = jnp.einsum('bld,hpd->blhp', hidden_states, gate_w) + gate_b
        temp = jnp.exp(log_temp).reshape(1, 1, H, 1)
        probs = jax.nn.softmax(logits / temp, -1)
        eps = jnp.clip(eps_param, 0.0, 0.2).reshape(1, 1, H, 1)
        probs = probs * (1.0 - 5.0 * eps) + eps
        o = probs[..., 0:1] * local_s + probs[..., 1:2] * local_m + probs[..., 2:3] * local_l + probs[..., 3:4] * delta_out + probs[..., 4:5] * v_direct
        o = _rmsnorm(o, norm_w)
        return o.reshape(b, l, H * DV) @ Wo.T

    def _L0_ffn_ref(x, weight, aux_weight1, aux_weight2, bias):
        import jax, jax.numpy as jnp
        import numpy as np
        D_MODEL = 256
        h = jnp.einsum('btc,cd->btd', x, weight)
        h = jnp.einsum('btc,cd->btd', h, aux_weight1)
        h = jnp.einsum('btc,cd->btd', h, aux_weight2)
        return jnp.tanh(h + bias)

    def _L1_attn_ref(x, Wq, bq, Wkv, bkv, Wo):
        import jax, jax.numpy as jnp
        import numpy as np
        import math
        NUM_HEADS = 8
        EMB = 256
        HEAD_DIM = 128
        B, T = (1, 1024)

        def sinusoidal_pe(T, d, dtype=jnp.float32):
            pos = jnp.arange(T, dtype=dtype)[:, None]
            inv_freq = jnp.exp(-math.log(10000.0) * jnp.arange(0, d, 2, dtype=dtype) / d)
            ang = pos * inv_freq[None, :]
            pe = jnp.zeros((T, d), dtype=dtype)
            pe = pe.at[:, 0::2].set(jnp.sin(ang))
            pe = pe.at[:, 1::2].set(jnp.cos(ang))
            return pe
        Bsz, Tlen, E = x.shape
        q = (x @ Wq + bq).reshape(Bsz, Tlen, NUM_HEADS, HEAD_DIM)
        kv = x @ Wkv + bkv
        k, v = (kv[..., :HEAD_DIM], kv[..., HEAD_DIM:])
        q = jnp.transpose(q, (0, 2, 1, 3))
        pe = sinusoidal_pe(Tlen, HEAD_DIM, x.dtype)
        q = q + pe[None, None, :, :]
        k = k + pe[None, :, :]
        scale = 1.0 / math.sqrt(HEAD_DIM)
        scores = jnp.einsum('bhqd,bkd->bhqk', q, k) * scale
        causal = jnp.tril(jnp.ones((Tlen, Tlen), dtype=bool))
        scores = jnp.where(causal[None, None, :, :], scores, jnp.finfo(scores.dtype).min)
        probs = jax.nn.softmax(scores, axis=-1)
        attn = jnp.einsum('bhqk,bkd->bhqd', probs, v)
        out = jnp.transpose(attn, (0, 2, 1, 3)).reshape(Bsz, Tlen, NUM_HEADS * HEAD_DIM)
        return out @ Wo

    def _L1_ffn_ref(x, Wr, W1, b1, W2, b2):
        import jax, jax.numpy as jnp
        import numpy as np
        CAP_FACTOR = 1.5
        orig_shape = x.shape
        D = x.shape[-1]
        E = Wr.shape[0]
        xf = x.reshape(-1, D)
        T = xf.shape[0]
        cap = int(CAP_FACTOR * T / E)
        logits = xf @ Wr.T
        vals, idx = jax.lax.top_k(logits.T, cap)
        w = jax.nn.softmax(vals, axis=-1)
        xg = xf[idx]
        h = jax.nn.gelu(jnp.einsum('ecd,esdm->ecsm', xg, W1) + b1[:, None], approximate=False)
        y = jnp.einsum('ecsm,esmk->ecsk', h, W2) + b2[:, None]
        y = y.reshape(E, cap, D) * w[..., None]
        out = jnp.zeros_like(xf).at[idx.reshape(-1)].add(y.reshape(-1, D))
        return out.reshape(orig_shape)

    def _L2_attn_ref(x, Wq, Wk, Wv, Wo, q_scale, k_scale):
        import jax, jax.numpy as jnp
        import numpy as np
        N_HEADS = 16
        EPS = 1e-06
        B, N, D = x.shape
        H = N_HEADS
        hd = D // H
        q = jax.nn.silu(x @ Wq.T)
        k = jax.nn.silu(x @ Wk.T)
        v = jax.nn.silu(x @ Wv.T)
        q = q.reshape(B, N, H, hd).transpose(0, 2, 1, 3)
        k = k.reshape(B, N, H, hd).transpose(0, 2, 1, 3)
        v = v.reshape(B, N, H, hd).transpose(0, 2, 1, 3)
        r_q = jnp.linalg.norm(q, axis=-1, keepdims=True)
        r_k = jnp.linalg.norm(k, axis=-1, keepdims=True)
        q_dir = q / (r_q + EPS)
        k_dir = k / (r_k + EPS)
        scores = jnp.einsum('bhnd,bhmd->bhnm', q_dir, k_dir)
        sq = q_scale[None, :, None, None]
        sk = k_scale[None, :, None, None]
        scores = scores * (r_q * sq) * (jnp.swapaxes(r_k, -2, -1) * sk)
        mask = jnp.tril(jnp.ones((N, N), dtype=bool))
        scores = jnp.where(mask, scores, -jnp.inf)
        probs = jax.nn.softmax(scores, axis=-1)
        out = jnp.einsum('bhnm,bhmd->bhnd', probs, v)
        out = out.transpose(0, 2, 1, 3).reshape(B, N, D)
        return out @ Wo.T

    def _L2_ffn_ref(x, w_gate, w_up, w_down):
        import jax, jax.numpy as jnp
        import numpy as np
        DIM = 256
        HIDDEN = 768
        SCALE = 1.0 / 127.0

        def _dequant(w_int, dtype):
            return w_int.astype(dtype) * jnp.asarray(SCALE, dtype)
        wg = _dequant(w_gate, x.dtype)
        wu = _dequant(w_up, x.dtype)
        wd = _dequant(w_down, x.dtype)
        gate = jnp.einsum('bsd,hd->bsh', x, wg)
        up = jnp.einsum('bsd,hd->bsh', x, wu)
        h = jax.nn.silu(gate) * up
        return jnp.einsum('bsh,dh->bsd', h, wd)

    def _L3_attn_ref(x, W_in, W_conv, b_conv, W_xproj, W_dt, b_dt, A_log, D, W_out):
        import jax, jax.numpy as jnp
        import numpy as np
        from math import ceil
        DIM = 256
        D_STATE = 16
        D_CONV = 4
        EXPAND = 2
        DI = DIM * EXPAND
        DT_RANK = ceil(DIM / 16)

        def _mamba(x, W_in, W_conv, b_conv, W_xproj, W_dt, b_dt, A_log, D, W_out):
            b, l, _ = x.shape
            silu = jax.nn.silu
            xr = x @ W_in.T
            xc, res = (xr[..., :DI], xr[..., DI:])
            u = jnp.transpose(xc, (0, 2, 1))
            u = jax.lax.conv_general_dilated(u, W_conv, window_strides=(1,), padding=[(D_CONV - 1, 0)], dimension_numbers=('NCH', 'OIH', 'NCH'), feature_group_count=DI)
            u = silu(u + b_conv[None, :, None])
            x_dbl = jnp.einsum('bdl,ed->ble', u, W_xproj)
            dt = x_dbl[..., :DT_RANK]
            B = x_dbl[..., DT_RANK:DT_RANK + D_STATE]
            C = x_dbl[..., DT_RANK + D_STATE:]
            delta = jax.nn.softplus(dt @ W_dt.T + b_dt)
            A = -jnp.exp(A_log)
            dA = jnp.exp(jnp.einsum('bld,dn->lbdn', delta, A))
            dBu = jnp.einsum('bld,bln,bdl->lbdn', delta, B, u)
            Cl = jnp.transpose(C, (1, 0, 2))

            def step(h, inp):
                dA_t, dBu_t, c_t = inp
                h = dA_t * h + dBu_t
                return (h, jnp.einsum('bdn,bn->bd', h, c_t))
            h0 = jnp.zeros((b, DI, D_STATE), u.dtype)
            _, ys = jax.lax.scan(step, h0, (dA, dBu, Cl))
            y = jnp.transpose(ys, (1, 2, 0)) + u * D[None, :, None]
            y = jnp.transpose(y, (0, 2, 1)) * silu(res)
            return y @ W_out.T
        return _mamba(x, W_in, W_conv, b_conv, W_xproj, W_dt, b_dt, A_log, D, W_out)

    def _L3_ffn_ref(x, w_router, w1, w3, w2, ws1, ws3, ws2):
        import jax, jax.numpy as jnp
        import numpy as np
        D_MODEL = 256
        NUM_EXPERTS = 8
        HIDDEN = 512
        TOP_K = 2
        SHARED_HIDDEN = 512
        BATCH, SEQ = (4, 512)
        orig_shape = x.shape
        xf = x.reshape(-1, D_MODEL)
        T = xf.shape[0]
        logits = xf @ w_router
        scores = jax.nn.softmax(logits, axis=-1)
        expert_weights, expert_indices = jax.lax.top_k(scores, TOP_K)
        cw = jnp.zeros((T, NUM_EXPERTS), dtype=xf.dtype)
        cw = cw.at[jnp.arange(T)[:, None], expert_indices].add(expert_weights)
        h = jax.nn.silu(jnp.einsum('td,edh->teh', xf, w1)) * jnp.einsum('td,edh->teh', xf, w3)
        y = jnp.einsum('teh,ehd->ted', h, w2)
        moe_out = jnp.einsum('te,ted->td', cw, y)
        shared = jax.nn.silu(xf @ ws1) * (xf @ ws3) @ ws2
        out = shared / (TOP_K + 1) + moe_out * (TOP_K / (TOP_K + 1))
        return out.reshape(orig_shape)
    x = L0_attn_hidden_states
    x = x + _layernorm(_L0_attn_ref(_layernorm(x, axis=-1), L0_attn_Wq, L0_attn_Wk, L0_attn_Wv, L0_attn_Wb, L0_attn_conv_q, L0_attn_conv_k, L0_attn_conv_v, L0_attn_fir_s, L0_attn_fir_m, L0_attn_fir_l, L0_attn_gate_w, L0_attn_gate_b, L0_attn_log_temp, L0_attn_eps_param, L0_attn_norm_w, L0_attn_Wo), axis=-1)
    x = x + _layernorm(_L0_ffn_ref(_layernorm(x, axis=-1), L0_ffn_weight, L0_ffn_aux_weight1, L0_ffn_aux_weight2, L0_ffn_bias), axis=-1)
    x = x + _layernorm(_L1_attn_ref(_layernorm(x, axis=-1), L1_attn_Wq, L1_attn_bq, L1_attn_Wkv, L1_attn_bkv, L1_attn_Wo), axis=-1)
    x = x + _layernorm(_L1_ffn_ref(_layernorm(x, axis=-1), L1_ffn_Wr, L1_ffn_W1, L1_ffn_b1, L1_ffn_W2, L1_ffn_b2), axis=-1)
    x = x + _layernorm(_L2_attn_ref(_layernorm(x, axis=-1), L2_attn_Wq, L2_attn_Wk, L2_attn_Wv, L2_attn_Wo, L2_attn_q_scale, L2_attn_k_scale), axis=-1)
    x = x + _layernorm(_L2_ffn_ref(_layernorm(x, axis=-1), L2_ffn_w_gate, L2_ffn_w_up, L2_ffn_w_down), axis=-1)
    x = x + _layernorm(_L3_attn_ref(_layernorm(x, axis=-1), L3_attn_W_in, L3_attn_W_conv, L3_attn_b_conv, L3_attn_W_xproj, L3_attn_W_dt, L3_attn_b_dt, L3_attn_A_log, L3_attn_D, L3_attn_W_out), axis=-1)
    x = x + _layernorm(_L3_ffn_ref(_layernorm(x, axis=-1), L3_ffn_w_router, L3_ffn_w1, L3_ffn_w3, L3_ffn_w2, L3_ffn_ws1, L3_ffn_ws3, L3_ffn_ws2), axis=-1)
    return x

_drawn_inputs = setup_inputs


def setup_inputs(seed=0):
    import zlib

    import numpy as np

    out = dict(_drawn_inputs(seed))
    spreads = {'L0_attn_gate_b': (0.0, 0.1),
     'L0_attn_log_temp': (0.0, 0.1),
     'L0_attn_eps_param': (0.019999999552965164, 0.2),
     'L0_attn_norm_w': (1.0, 0.2),
     'L0_ffn_bias': (0.0, 0.1),
     'L1_ffn_b1': (0.0, 0.1),
     'L1_ffn_b2': (0.0, 0.1),
     'L2_attn_q_scale': (1.0, 0.2),
     'L2_attn_k_scale': (1.0, 0.2),
     'L3_attn_b_conv': (0.0, 0.1),
     'L3_attn_b_dt': (0.0, 0.8),
     'L3_attn_D': (1.0, 0.2)}
    factors = {'L3_attn_W_xproj': 8.0, 'L3_attn_W_dt': 8.0, 'L3_attn_A_log': 8.0}
    for name, (base, spread) in spreads.items():
        noise = np.random.default_rng([zlib.crc32(name.encode()), seed]).standard_normal(out[name].shape)
        drawn = base * np.exp(spread * noise) if base else spread * noise
        out[name] = jnp.asarray(drawn.astype(out[name].dtype))
    for name, factor in factors.items():
        out[name] = (out[name] * factor).astype(out[name].dtype)
    return out
```

```python
from contextlib import ExitStack

import numpy as np

import concourse.bass as bass
from concourse import mybir

P = 128
NB = 8
L = 512
D = 256
NT = L // P
KD = D // P
EPS = 1e-5
MASKED = -1e30

ALU = mybir.AluOpType
ACT = mybir.ActivationFunctionType
AX = mybir.AxisListType
F32 = mybir.dt.float32
I32 = mybir.dt.int32
U32 = mybir.dt.uint32
BF16 = mybir.dt.bfloat16

STAGES = (0, 1, 2, 3, 4, 5, 6, 7)


class Scope:

    def __init__(self, nc, stage):
        self.nc, self.stage, self.ctx, self.sems = nc, stage, ExitStack(), []

    def __enter__(self):
        self.ctx.__enter__()
        return self

    def __exit__(self, *a):
        return self.ctx.__exit__(*a)

    def sb(self, name, shape, dt=F32):
        return self.ctx.enter_context(self.nc.sbuf_tensor(f"{self.stage}_{name}", shape, dt))

    def ps(self, name, shape, dt=F32):
        return self.ctx.enter_context(self.nc.psum_tensor(f"{self.stage}_{name}", shape, dt))

    def sem(self, name):
        s = self.ctx.enter_context(self.nc.semaphore(f"{self.stage}_{name}"))
        self.sems.append(s)
        return s

    def clear(self):
        for s in self.sems:
            self.nc.sync.sem_clear(s)
        self.nc.all_engine_barrier(sem_only=True)


class Chain:

    def __init__(self, eng, sem):
        self.eng, self.sem, self.n = eng, sem, 0

    def link(self, ins):
        self.n += 1
        ins.then_inc(self.sem, 1)
        self.eng.wait_ge(self.sem, self.n)


class Norm:

    def __init__(self, sc):
        self.x = sc.sb("x", [P, NT, D])
        self.xn = sc.sb("xn", [P, NT, D])
        self.xnT = sc.sb("xnT", [P, KD, L])
        self.stat = sc.sb("stat", [P, NT, 6])
        self.mv = sc.sb("mv", [P, NT, 2])
        self.rstd = sc.sb("rstd", [P, NT])
        self.ystat = sc.sb("ystat", [P, NT, 6])
        self.ymv = sc.sb("ymv", [P, NT, 2])
        self.yrstd = sc.sb("yrstd", [P, NT])
        self.ynm = sc.sb("ynm", [P, NT])
        self.yn = sc.sb("yn", [P, NT, D])
        self.x_in = sc.sem("x_in")
        self.var_ready = sc.sem("var_ready")
        self.rstd_ready = sc.sem("rstd_ready")
        self.xn_ready = sc.sem("xn_ready")
        self.xnT_ready = sc.sem("xnT_ready")
        self.y_var_ready = sc.sem("y_var_ready")
        self.y_scale_ready = sc.sem("y_scale_ready")
        self.yn_ready = sc.sem("yn_ready")
        self.x_out = sc.sem("x_out")
        self.x_stored = sc.sem("x_stored")
        self.xT_ps_ready = sc.sem("xT_ps_ready")


def rows(x):
    return x.rearrange("b (t p) d -> b p t d", p=P)


def norm_in_vector(nc, dve, n, link):
    dve.wait_ge(n.x_in, 16)
    for t in range(NT):
        last = nc.vector.bn_stats(n.stat[:, t, :], n.x[:, t, :])
    link(last)
    for t in range(NT):
        last = nc.vector.bn_aggr(n.mv[:, t, :], n.stat[:, t, :])
    last.then_inc(n.var_ready, 1)
    dve.wait_ge(n.rstd_ready, 2)
    for t in range(NT):
        nc.vector.tensor_scalar(n.xn[:, t, :], n.x[:, t, :], n.mv[:, t, 0:1], n.rstd[:, t:t + 1],
                                ALU.subtract, ALU.mult).then_inc(n.xn_ready, 1)


def norm_in_pool(nc, pool, n, eps):
    pool.wait_ge(n.var_ready, 1)
    nc.gpsimd.tensor_scalar(n.rstd[:, :], n.mv[:, :, 1], EPS, None, ALU.add).then_inc(n.rstd_ready, 1)
    pool.wait_ge(n.rstd_ready, 1)
    nc.gpsimd.tensor_tensor(n.rstd[:, :], n.rstd[:, :], eps.minus_half[:, 0:NT], ALU.pow).then_inc(n.rstd_ready, 1)


def norm_in_tensor(nc, pe, n, xT_ps, ident):
    for t in range(NT):
        pe.wait_ge(n.xn_ready, t + 1)
        for k in range(KD):
            last = nc.tensor.transpose(xT_ps[k][:, t * P:(t + 1) * P], n.xn[:, t, k * P:(k + 1) * P], ident[:, :])
    last.then_inc(n.xT_ps_ready, 1)


def norm_in_evacuate(nc, act, n, xT_ps):
    act.wait_ge(n.xT_ps_ready, 1)
    for k in range(KD):
        nc.scalar.activation(n.xnT[:, k, :], xT_ps[k][:, :], ACT.Copy).then_inc(n.xnT_ready, 1)


def norm_out_vector(nc, dve, n, link, y):
    for t in range(NT):
        last = nc.vector.bn_stats(n.ystat[:, t, :], y(t))
    link(last)
    for t in range(NT):
        last = nc.vector.bn_aggr(n.ymv[:, t, :], n.ystat[:, t, :])
    last.then_inc(n.y_var_ready, 1)


def norm_out_scalar(nc, act, n, y):
    act.wait_ge(n.y_scale_ready, 3)
    for t in range(NT):
        nc.scalar.activation(n.yn[:, t, :], y(t), ACT.Identity, bias=n.ynm[:, t:t + 1],
                             scale=n.yrstd[:, t:t + 1]).then_inc(n.yn_ready, 1)


def norm_out_pool(nc, pool, n, eps):
    pool.wait_ge(n.y_var_ready, 1)
    nc.gpsimd.tensor_scalar(n.yrstd[:, :], n.ymv[:, :, 1], EPS, None, ALU.add)
    nc.gpsimd.tensor_scalar(n.ynm[:, :], n.ymv[:, :, 0], -1.0, None, ALU.mult).then_inc(n.y_scale_ready, 1)
    pool.wait_ge(n.y_scale_ready, 1)
    nc.gpsimd.tensor_tensor(n.yrstd[:, :], n.yrstd[:, :], eps.minus_half[:, 0:NT], ALU.pow)\
        .then_inc(n.y_scale_ready, 1)
    pool.wait_ge(n.y_scale_ready, 2)
    nc.gpsimd.tensor_tensor(n.ynm[:, :], n.ynm[:, :], n.yrstd[:, :], ALU.mult).then_inc(n.y_scale_ready, 1)
    for t in range(NT):
        pool.wait_ge(n.yn_ready, t + 1)
        nc.gpsimd.tensor_tensor(n.yn[:, t, :], n.yn[:, t, :], n.x[:, t, :], ALU.add).then_inc(n.x_out, 1)


def norm_out_store(sp, n, dst, b):
    sp.wait_ge(n.x_out, NT)
    sp.dma_start(rows(dst)[b], n.yn[:, :, :]).then_inc(n.x_stored, 16)
    sp.wait_ge(n.x_stored, 16)


class Consts:
    pass


def constants(nc, ctx):
    c = Consts()
    c.ident = ctx.enter_context(nc.sbuf_tensor("ident", [P, P], F32))
    c.minus_half = ctx.enter_context(nc.sbuf_tensor("minus_half", [P, 64], F32))
    c.causal = ctx.enter_context(nc.sbuf_tensor("causal", [P, P], F32))
    c.gathered = ctx.enter_context(nc.semaphore("gathered"))
    c.added = ctx.enter_context(nc.semaphore("added"))
    c.iota8 = ctx.enter_context(nc.sbuf_tensor("iota8", [P, 8], F32))
    with nc.semaphore("const_done") as const_done, nc.Block() as block:
        @block.gpsimd
        def _(pool):
            nc.gpsimd.memset(c.ident[:, :], 0.0)
            nc.gpsimd.memset(c.causal[:, :], 0.0)
            nc.gpsimd.iota(c.iota8[:, :], [[1, 8]], base=0, channel_multiplier=0,
                           allow_small_or_imprecise_dtypes=True)
            nc.gpsimd.memset(c.minus_half[:, :], -0.5).then_inc(const_done, 1)
            pool.wait_ge(const_done, 1)
            nc.gpsimd.affine_select(out=c.ident[:, :], in_=c.ident[:, :], compare_op=ALU.not_equal, fill=1.0,
                                    base=0, pattern=[[-1, P]], channel_multiplier=1).then_inc(const_done, 1)
            nc.gpsimd.affine_select(out=c.causal[:, :], in_=c.causal[:, :], compare_op=ALU.is_ge, fill=MASKED,
                                    base=0, pattern=[[-1, P]], channel_multiplier=1).then_inc(const_done, 1)
            pool.wait_ge(const_done, 3)
    return c


def stage_tanh_mlp(nc, w, src, dst, c):
    with Scope(nc, "mlp") as sc:
        n = Norm(sc)
        wt = [sc.sb(f"w{i}", [P, KD, D]) for i in range(3)]
        bias = sc.sb("bias", [P, D])
        hT = [sc.sb(f"hT{i}", [P, KD, L]) for i in range(2)]
        y = sc.sb("y", [P, NT, D])
        pA = [sc.ps(f"pA{k}", [P, L]) for k in range(KD)]
        pB = [sc.ps(f"pB{k}", [P, L]) for k in range(KD)]
        pY = sc.ps("pY", [P, NT, D])
        w_in = sc.sem("w_in")
        with nc.Block() as block:
            @block.sync
            def _(sp):
                for i, name in enumerate(("L0_ffn_weight", "L0_ffn_aux_weight1", "L0_ffn_aux_weight2")):
                    sp.dma_start(wt[i][:, :, :], w[name].rearrange("(k p) d -> p k d", p=P)).then_inc(w_in, 16)
                sp.dma_start(bias[:, :], w["L0_ffn_bias"][None, :].to_broadcast([P, D])).then_inc(w_in, 16)
                sp.wait_ge(w_in, 64)
        h_ps = sc.sem("h_ps")
        h_ready = sc.sem("h_ready")
        yb_ready = sc.sem("yb_ready")
        y_ready = sc.sem("y_ready")
        dch = sc.sem("dch")
        with nc.Fori(0, NB) as b:
            with nc.Block() as block:
                @block.sync
                def _(sp):
                    sp.dma_start(n.x[:, :, :], rows(src)[b]).then_inc(n.x_in, 16)
                    norm_out_store(sp, n, dst, b)

                @block.vector
                def _(dve):
                    link = Chain(dve, dch).link
                    norm_in_vector(nc, dve, n, link)
                    dve.wait_ge(h_ps, 3)
                    for t in range(NT):
                        nc.vector.tensor_tensor(y[:, t, :], pY[:, t, :], bias[:, :], ALU.add).then_inc(yb_ready, 1)
                    dve.wait_ge(y_ready, 1)
                    norm_out_vector(nc, dve, n, link, lambda t: y[:, t, :])

                @block.scalar
                def _(act):
                    norm_in_evacuate(nc, act, n, pA)
                    for i, ps in enumerate((pB, pA)):
                        act.wait_ge(h_ps, i + 1)
                        for k in range(KD):
                            nc.scalar.activation(hT[i][:, k, :], ps[k][:, :], ACT.Copy).then_inc(h_ready, 1)
                    act.wait_ge(yb_ready, NT)
                    nc.scalar.activation(y[:, :, :], y[:, :, :], ACT.Tanh).then_inc(y_ready, 1)
                    act.wait_ge(y_ready, 1)
                    norm_out_scalar(nc, act, n, lambda t: y[:, t, :])

                @block.tensor
                def _(pe):
                    norm_in_tensor(nc, pe, n, pA, c.ident)
                    pe.wait_ge(n.xnT_ready, KD)
                    for i, (a, ps) in enumerate(((n.xnT, pB), (hT[0], pA))):
                        if i == 1:
                            pe.wait_ge(h_ready, KD)
                        for m in range(KD):
                            for k in range(KD):
                                last = nc.tensor.matmul(ps[m][:, :], wt[i][:, k, m * P:(m + 1) * P], a[:, k, :],
                                                        start=(k == 0), stop=(k == KD - 1))
                        last.then_inc(h_ps, 1)
                    pe.wait_ge(h_ready, 2 * KD)
                    for t in range(NT):
                        for k in range(KD):
                            last = nc.tensor.matmul(pY[:, t, :], hT[1][:, k, t * P:(t + 1) * P], wt[2][:, k, :],
                                                    start=(k == 0), stop=(k == KD - 1))
                    last.then_inc(h_ps, 1)

                @block.gpsimd
                def _(pool):
                    norm_in_pool(nc, pool, n, c)
                    norm_out_pool(nc, pool, n, c)
            sc.clear()


def stage_int_swiglu(nc, w, src, dst, c):
    H = w["L2_ffn_w_gate"].shape[1]
    JH = H // P
    scale = float(np.float32(1.0 / 127.0))
    with Scope(nc, "isw") as sc:
        n = Norm(sc)
        raw = sc.sb("raw", [P, KD * H], I32)
        wg = sc.sb("wg", [P, KD, H])
        wu = sc.sb("wu", [P, KD, H])
        wd = sc.sb("wd", [P, JH, D])
        g = sc.sb("g", [P, 2, L])
        hT = sc.sb("hT", [P, JH, L])
        pX = [sc.ps(f"pX{k}", [P, L]) for k in range(KD)]
        pG = [sc.ps(f"pG{k}", [P, L]) for k in range(2)]
        pU = [sc.ps(f"pU{k}", [P, L]) for k in range(2)]
        pY = sc.ps("pY", [P, NT, D])
        w_in, w_ready = sc.sem("w_in"), sc.sem("w_ready")
        gu_ps, g_ready, h_ready, y_ps, dch = (sc.sem(s) for s in ("gu_ps", "g_ready", "h_ready", "y_ps", "dch"))
        sources = ((wg, w["L2_ffn_w_gate"]), (wu, w["L2_ffn_w_up"]), (wd, w["L2_ffn_w_down"]))
        with nc.Block() as block:
            @block.sync
            def _(sp):
                for i, (t, a) in enumerate(sources):
                    if i:
                        sp.wait_ge(w_ready, i)
                    sp.dma_start(raw[:, :].rearrange("p (k d) -> p k d", d=a.shape[1]),
                                 a.rearrange("(k p) d -> p k d", p=P)).then_inc(w_in, 16)

            @block.vector
            def _(dve):
                for i, (t, a) in enumerate(sources):
                    dve.wait_ge(w_in, 16 * (i + 1))
                    nc.vector.tensor_scalar(t[:, :, :].rearrange("p k d -> p (k d)"), raw[:, :], scale, None,
                                            ALU.mult).then_inc(w_ready, 1)
                dve.wait_ge(w_ready, 3)
        sc.clear()
        with nc.Fori(0, NB) as b:
            with nc.Block() as block:
                @block.sync
                def _(sp):
                    sp.dma_start(n.x[:, :, :], rows(src)[b]).then_inc(n.x_in, 16)
                    norm_out_store(sp, n, dst, b)

                @block.vector
                def _(dve):
                    link = Chain(dve, dch).link
                    norm_in_vector(nc, dve, n, link)
                    for j in range(JH):
                        dve.wait_ge(g_ready, j + 1)
                        nc.vector.tensor_tensor(hT[:, j, :], g[:, j % 2, :], pU[j % 2][:, :], ALU.mult)\
                            .then_inc(h_ready, 1)
                    dve.wait_ge(y_ps, 1)
                    norm_out_vector(nc, dve, n, link, lambda t: pY[:, t, :])

                @block.scalar
                def _(act):
                    norm_in_evacuate(nc, act, n, pX)
                    for j in range(JH):
                        act.wait_ge(gu_ps, j + 1)
                        if j >= 2:
                            act.wait_ge(h_ready, j - 1)
                        nc.scalar.activation(g[:, j % 2, :], pG[j % 2][:, :], ACT.Silu).then_inc(g_ready, 1)
                    norm_out_scalar(nc, act, n, lambda t: pY[:, t, :])

                @block.tensor
                def _(pe):
                    norm_in_tensor(nc, pe, n, pX, c.ident)
                    pe.wait_ge(n.xnT_ready, KD)

                    def down(j):
                        pe.wait_ge(h_ready, j + 1)
                        for t in range(NT):
                            last = nc.tensor.matmul(pY[:, t, :], hT[:, j, t * P:(t + 1) * P], wd[:, j, :],
                                                    start=(j == 0 and t % 2 == 0), stop=(j == JH - 1),
                                                    skip_group_check=True)
                        return last

                    for j in range(JH):
                        if j >= 2:
                            pe.wait_ge(h_ready, j - 1)
                        for wt, ps in ((wg, pG), (wu, pU)):
                            for k in range(KD):
                                last = nc.tensor.matmul(ps[j % 2][:, :], wt[:, k, j * P:(j + 1) * P], n.xnT[:, k, :],
                                                        start=(k == 0), stop=(k == KD - 1))
                        last.then_inc(gu_ps, 1)
                        if j >= 1:
                            down(j - 1)
                    down(JH - 1).then_inc(y_ps, 1)

                @block.gpsimd
                def _(pool):
                    norm_in_pool(nc, pool, n, c)
                    norm_out_pool(nc, pool, n, c)
            sc.clear()


def stage_moe_top2(nc, w, src, dst, c):
    E, H = w["L3_ffn_w1"].shape[0], w["L3_ffn_w1"].shape[2]
    TOP = 2
    JH = H // P
    NE = E + 1
    units = [(e, j) for e in range(NE) for j in range(JH)]
    with Scope(nc, "top2") as sc:
        n = Norm(sc)
        w1 = sc.sb("w1", [P, NE * KD, H])
        w3 = sc.sb("w3", [P, NE * KD, H])
        w2 = sc.sb("w2", [P, NE * JH, D])
        wr = sc.sb("wr", [P, KD, E])
        g = sc.sb("g", [P, 2, L])
        hT = sc.sb("hT", [P, 2, L])
        acc = sc.sb("acc", [P, NT, D])
        sub = sc.sb("sub", [P, NT, E])
        prob = sc.sb("prob", [P, NT, E])
        best = sc.sb("best", [P, NT, 8])
        best_i = sc.sb("best_i", [P, NT, 8], U32)
        best_f = sc.sb("best_f", [P, NT, 8])
        cw = sc.sb("cw", [P, NT, E])
        red = sc.sb("red", [P, NT])
        pG = [sc.ps(f"pG{k}", [P, L]) for k in range(2)]
        pU = [sc.ps(f"pU{k}", [P, L]) for k in range(2)]
        pY = [sc.ps(f"pY{k}", [P, NT, D]) for k in range(2)]
        pX = [pY[1][:, 0:2, :].rearrange("p t d -> p (t d)"), pY[1][:, 2:4, :].rearrange("p t d -> p (t d)")]
        pR = pG[0][:, 0:NT * E].rearrange("p (t e) -> p t e", e=E)
        w_in = sc.sem("w_in")
        gu_ps, g_ready, h_ready, y_ps, dch, r_ps, sub_ready, exp_ready, acc_ready = (
            sc.sem(s) for s in ("gu_ps", "g_ready", "h_ready", "y_ps", "dch", "r_ps", "sub_ready", "exp_ready",
                                "acc_ready"))
        with nc.Block() as block:
            @block.sync
            def _(sp):
                sp.dma_start(wr[:, :, :], w["L3_ffn_w_router"].rearrange("(k p) e -> p k e", p=P)).then_inc(w_in, 16)
                for t, many, one, k in ((w1, "L3_ffn_w1", "L3_ffn_ws1", KD), (w3, "L3_ffn_w3", "L3_ffn_ws3", KD),
                                        (w2, "L3_ffn_w2", "L3_ffn_ws2", JH)):
                    for e in range(E):
                        sp.dma_start(t[:, e * k:(e + 1) * k, :],
                                     w[many][e].rearrange("(k p) h -> p k h", p=P)).then_inc(w_in, 16)
                    sp.dma_start(t[:, E * k:, :], w[one].rearrange("(k p) h -> p k h", p=P)).then_inc(w_in, 16)
                sp.wait_ge(w_in, 16 * (3 * NE + 1))
        with nc.Fori(0, NB) as b:
            with nc.Block() as block:
                @block.sync
                def _(sp):
                    sp.dma_start(n.x[:, :, :], rows(src)[b]).then_inc(n.x_in, 16)
                    norm_out_store(sp, n, dst, b)

                @block.vector
                def _(dve):
                    link = Chain(dve, dch).link
                    norm_in_vector(nc, dve, n, link)
                    dve.wait_ge(r_ps, 1)
                    link(nc.vector.tensor_reduce(red[:, :], pR, AX.X, ALU.max))
                    nc.vector.tensor_tensor(sub[:, :, :], pR, red[:, :].unsqueeze(2).to_broadcast([P, NT, E]),
                                            ALU.subtract).then_inc(sub_ready, 1)
                    dve.wait_ge(exp_ready, 1)
                    link(nc.vector.tensor_reduce(red[:, :], sub[:, :, :], AX.X, ALU.add))
                    link(nc.vector.reciprocal(red[:, :], red[:, :]))
                    link(nc.vector.tensor_tensor(prob[:, :, :], sub[:, :, :],
                                                 red[:, :].unsqueeze(2).to_broadcast([P, NT, E]), ALU.mult))
                    for t in range(NT):
                        last = nc.vector.max(best[:, t, :], prob[:, t, :])
                    link(last)
                    for t in range(NT):
                        last = nc.vector.max_index(best_i[:, t, :], best[:, t, :], prob[:, t, :])
                    link(last)
                    link(nc.vector.tensor_copy(best_f[:, :, :], best_i[:, :, :]))
                    for t in range(NT):
                        last = nc.vector.tensor_scalar(cw[:, t, :], c.iota8[:, :], best_f[:, t, 0:1], None, ALU.is_equal)
                    link(last)
                    for t in range(NT):
                        last = nc.vector.scalar_tensor_tensor(cw[:, t, :], c.iota8[:, :], best_f[:, t, 1:2], cw[:, t, :],
                                                              ALU.is_equal, ALU.add)
                    link(last)
                    link(nc.vector.scalar_tensor_tensor(cw[:, :, :], prob[:, :, :], TOP / (TOP + 1.0), cw[:, :, :],
                                                        ALU.mult, ALU.mult))

                    def add_expert(e):
                        dve.wait_ge(y_ps, e + 1)
                        if e:
                            dve.wait_ge(acc_ready, e)
                        for t in range(NT):
                            if e == 0:
                                last = nc.vector.tensor_scalar(acc[:, t, :], pY[0][:, t, :], cw[:, t, 0:1], None,
                                                               ALU.mult)
                            else:
                                weight = cw[:, t, e:e + 1] if e < E else 1.0 / (TOP + 1.0)
                                last = nc.vector.scalar_tensor_tensor(acc[:, t, :], pY[e % 2][:, t, :], weight,
                                                                      acc[:, t, :], ALU.mult, ALU.add)
                        last.then_inc(acc_ready, 1)

                    for u, (e, j) in enumerate(units):
                        dve.wait_ge(g_ready, u + 1)
                        if u >= 2:
                            dve.wait_ge(gu_ps, u + 1)
                        nc.vector.tensor_tensor(hT[:, u % 2, :], g[:, u % 2, :], pU[u % 2][:, :], ALU.mult)\
                            .then_inc(h_ready, 1)
                        if j == 1 and e >= 1:
                            add_expert(e - 1)
                    add_expert(E)
                    dve.wait_ge(acc_ready, NE)
                    norm_out_vector(nc, dve, n, link, lambda t: acc[:, t, :])

                @block.scalar
                def _(act):
                    norm_in_evacuate(nc, act, n, pX)
                    act.wait_ge(sub_ready, 1)
                    nc.scalar.activation(sub[:, :, :], sub[:, :, :], ACT.Exp).then_inc(exp_ready, 1)
                    for u in range(len(units)):
                        act.wait_ge(gu_ps, u + 1)
                        if u >= 2:
                            act.wait_ge(h_ready, u - 1)
                        nc.scalar.activation(g[:, u % 2, :], pG[u % 2][:, :], ACT.Silu).then_inc(g_ready, 1)
                    norm_out_scalar(nc, act, n, lambda t: acc[:, t, :])

                @block.tensor
                def _(pe):
                    norm_in_tensor(nc, pe, n, pX, c.ident)
                    pe.wait_ge(n.xnT_ready, KD)
                    for t in range(NT):
                        for k in range(KD):
                            last = nc.tensor.matmul(pR[:, t, :], n.xnT[:, k, t * P:(t + 1) * P], wr[:, k, :],
                                                    start=(k == 0), stop=(k == KD - 1))
                    last.then_inc(r_ps, 1)

                    def down(u):
                        e, j = units[u]
                        pe.wait_ge(h_ready, u + 1)
                        if j == 0 and e >= 2:
                            pe.wait_ge(acc_ready, e - 1)
                        for t in range(NT):
                            last = nc.tensor.matmul(pY[e % 2][:, t, :], hT[:, u % 2, t * P:(t + 1) * P],
                                                    w2[:, e * JH + j, :], start=(j == 0 and t % 2 == 0),
                                                    stop=(j == JH - 1), skip_group_check=True)
                        if j == JH - 1:
                            last.then_inc(y_ps, 1)

                    for u, (e, j) in enumerate(units):
                        if u == 0:
                            pe.wait_ge(sub_ready, 1)
                        if u >= 2:
                            pe.wait_ge(h_ready, u - 1)
                        for wt, ps in ((w1, pG), (w3, pU)):
                            for k in range(KD):
                                last = nc.tensor.matmul(ps[u % 2][:, :], wt[:, e * KD + k, j * P:(j + 1) * P],
                                                        n.xnT[:, k, :], start=(k == 0), stop=(k == KD - 1))
                        last.then_inc(gu_ps, 1)
                        if u >= 1:
                            down(u - 1)
                    down(len(units) - 1)

                @block.gpsimd
                def _(pool):
                    norm_in_pool(nc, pool, n, c)
                    norm_out_pool(nc, pool, n, c)
            sc.clear()


def stage_mqa(nc, w, src, dst, c):
    DH = w["L1_attn_Wkv"].shape[1] // 2
    H = w["L1_attn_Wq"].shape[1] // DH
    SCALE = float(np.float32(1.0 / np.sqrt(DH)))
    units = [(h, q) for h in range(H) for q in range(NT)]
    with Scope(nc, "mqa") as sc:
        n = Norm(sc)
        wq = sc.sb("wq", [P, KD, H * DH])
        wkv = sc.sb("wkv", [P, KD, 2 * DH])
        wo = sc.sb("wo", [P, H, D])
        bq = sc.sb("bq", [P, H])
        bk = sc.sb("bk", [P, 1])
        bv = sc.sb("bv", [P, DH])
        peT = sc.sb("peT", [P, L])
        qT = sc.sb("qT", [P, H, L])
        kT = sc.sb("kT", [P, L])
        v = sc.sb("v", [P, NT, DH])
        prob = sc.sb("prob", [P, 3, L])
        probT = sc.sb("probT", [P, 2, NT, L])
        oT = sc.sb("oT", [P, H, L])
        nmax = sc.sb("nmax", [P, len(units)])
        rsum = sc.sb("rsum", [P, len(units)])
        rinv = sc.sb("rinv", [P, len(units)])
        pS = [sc.ps(f"pS{k}", [P, L]) for k in range(2)]
        pT = [sc.ps(f"pT{k}", [P, L]) for k in range(2)]
        pO = [sc.ps(f"pO{k}", [P, L]) for k in range(2)]
        pY = sc.ps("pY", [P, NT, D])
        w_in = sc.sem("w_in")
        (proj_ps, proj_used, k_sum, s_ps, max_ready, exp_ready, inv_ready, prob_ready, t_ps, t_used, o_ps, o_used, y_ps,
         dch) = (sc.sem(s) for s in ("proj_ps", "proj_used", "k_sum", "s_ps", "max_ready", "exp_ready", "inv_ready",
                                     "prob_ready", "t_ps", "t_used", "o_ps", "o_used", "y_ps", "dch"))
        with nc.Block() as block:
            @block.sync
            def _(sp):
                sp.dma_start(wq[:, :, :], w["L1_attn_Wq"].rearrange("(k p) d -> p k d", p=P)).then_inc(w_in, 16)
                sp.dma_start(wkv[:, :, :], w["L1_attn_Wkv"].rearrange("(k p) d -> p k d", p=P)).then_inc(w_in, 16)
                sp.dma_start(wo[:, :, :], w["L1_attn_Wo"].rearrange("(h p) d -> p h d", p=P)).then_inc(w_in, 16)
                with nc.allow_non_contiguous_dma(reason="biases, a few values each"):
                    sp.dma_start(bq[:, :], w["L1_attn_bq"].rearrange("(h p) -> p h", p=P)).then_inc(w_in, 16)
                    sp.dma_start(bk[:, :], w["L1_attn_bkv"].rearrange("(a p) -> p a", p=P)[:, 0:1]).then_inc(w_in, 16)
                sp.dma_start(bv[:, :], w["L1_attn_bkv"][None, DH:].to_broadcast([P, DH])).then_inc(w_in, 16)
                sp.dma_start(peT[:, :], w["positions"]).then_inc(w_in, 16)
                sp.wait_ge(w_in, 16 * 7)
        with nc.Fori(0, NB) as b:
            with nc.Block() as block:
                @block.sync
                def _(sp):
                    sp.dma_start(n.x[:, :, :], rows(src)[b]).then_inc(n.x_in, 16)
                    norm_out_store(sp, n, dst, b)

                @block.vector
                def _(dve):
                    link = Chain(dve, dch).link
                    norm_in_vector(nc, dve, n, link)
                    for i in range(H + 1):
                        dve.wait_ge(proj_ps, i + 1)
                        out, bias = (kT[:, :], bk[:, 0:1]) if i == 0 else (qT[:, i - 1, :], bq[:, i - 1:i])
                        nc.vector.scalar_tensor_tensor(out, pO[i % 2][:, :], bias, peT[:, :], ALU.add, ALU.add)\
                            .then_inc(proj_used, 1)
                        if i == 1:
                            dve.wait_ge(proj_used, 1)
                            nc.vector.tensor_scalar(kT[:, :], kT[:, :], SCALE, None, ALU.mult).then_inc(k_sum, 1)
                    dve.wait_ge(proj_ps, H + 2)
                    nc.vector.tensor_tensor(v[:, :, :], pT[0][:, :].rearrange("p (t d) -> p t d", d=DH),
                                            bv[:, :].unsqueeze(1).to_broadcast([P, NT, DH]), ALU.add)\
                        .then_inc(proj_used, 1)

                    def neg_max(u):
                        dve.wait_ge(s_ps, u + 1)
                        nc.vector.tensor_reduce(nmax[:, u:u + 1], pS[u % 2][:, 0:(units[u][1] + 1) * P], AX.X, ALU.max,
                                                negate=True).then_inc(max_ready, 1)

                    def inverse(u):
                        dve.wait_ge(exp_ready, u + 1)
                        nc.vector.reciprocal(rinv[:, u:u + 1], rsum[:, u:u + 1]).then_inc(inv_ready, 1)

                    def evacuate(u):
                        h, q = units[u]
                        dve.wait_ge(t_ps, u + 1)
                        if h >= 2:
                            dve.wait_ge(o_ps, h - 1)
                        nc.vector.tensor_copy(probT[:, h % 2, 0:q + 1, q * P:(q + 1) * P],
                                              pT[u % 2][:, 0:(q + 1) * P].rearrange("p (k q) -> p k q", q=P))\
                            .then_inc(t_used, 1)

                    for u in range(len(units) + 2):
                        if u < len(units):
                            neg_max(u)
                        if 1 <= u <= len(units):
                            inverse(u - 1)
                        if u >= 2:
                            evacuate(u - 2)
                    dve.wait_ge(y_ps, 1)
                    norm_out_vector(nc, dve, n, link, lambda t: pY[:, t, :])

                @block.scalar
                def _(act):
                    norm_in_evacuate(nc, act, n, pT)

                    def output(h):
                        act.wait_ge(o_ps, h + 1)
                        nc.scalar.activation(oT[:, h, :], pO[h % 2][:, :], ACT.Copy).then_inc(o_used, 1)

                    for u, (h, q) in enumerate(units):
                        act.wait_ge(max_ready, u + 1)
                        if u >= 3:
                            act.wait_ge(t_ps, u - 2)
                        nc.scalar.activation(prob[:, u % 3, 0:(q + 1) * P], pS[u % 2][:, 0:(q + 1) * P], ACT.Exp,
                                             bias=nmax[:, u:u + 1], accum_out=rsum[:, u:u + 1]).then_inc(exp_ready, 1)
                        if q == NT - 1 and h >= 2:
                            output(h - 2)
                    output(H - 2)
                    output(H - 1)
                    norm_out_scalar(nc, act, n, lambda t: pY[:, t, :])

                @block.tensor
                def _(pe):
                    norm_in_tensor(nc, pe, n, pT, c.ident)
                    pe.wait_ge(n.xnT_ready, KD)
                    for i in range(H + 1):
                        if i >= 2:
                            pe.wait_ge(proj_used, i - 1)
                        for k in range(KD):
                            wt = wkv[:, k, 0:DH] if i == 0 else wq[:, k, (i - 1) * DH:i * DH]
                            last = nc.tensor.matmul(pO[i % 2][:, :], wt, n.xnT[:, k, :], start=(k == 0), stop=(k == KD - 1))
                        last.then_inc(proj_ps, 1)
                    for t in range(NT):
                        for k in range(KD):
                            last = nc.tensor.matmul(pT[0][:, t * DH:(t + 1) * DH], n.xnT[:, k, t * P:(t + 1) * P],
                                                    wkv[:, k, DH:], start=(k == 0), stop=(k == KD - 1))
                    last.then_inc(proj_ps, 1)
                    pe.wait_ge(proj_used, H + 2)
                    pe.wait_ge(k_sum, 1)

                    def scores(u):
                        h, q = units[u]
                        if u >= 2:
                            pe.wait_ge(exp_ready, u - 1)
                        nc.tensor.matmul(pS[u % 2][:, 0:(q + 1) * P], qT[:, h, q * P:(q + 1) * P], kT[:, 0:(q + 1) * P],
                                         start=True, stop=False, skip_group_check=True)
                        nc.tensor.matmul(pS[u % 2][:, q * P:(q + 1) * P], c.ident[:, :], c.causal[:, :],
                                         start=False, stop=True, skip_group_check=True).then_inc(s_ps, 1)

                    def turn(u):
                        pe.wait_ge(prob_ready, u + 1)
                        if u >= 2:
                            pe.wait_ge(t_used, u - 1)
                        for k in range(units[u][1] + 1):
                            last = nc.tensor.transpose(pT[u % 2][:, k * P:(k + 1) * P], prob[:, u % 3, k * P:(k + 1) * P],
                                                       c.ident[:, :])
                        last.then_inc(t_ps, 1)

                    def weigh(h):
                        pe.wait_ge(t_used, NT * (h + 1))
                        if h >= 2:
                            pe.wait_ge(o_used, h - 1)
                        for k in range(NT):
                            last = nc.tensor.matmul(pO[h % 2][:, k * P:], v[:, k, :], probT[:, h % 2, k, k * P:],
                                                    start=(k == 0), stop=(k == NT - 1), skip_group_check=True)
                        last.then_inc(o_ps, 1)

                    for u in range(len(units) + 3):
                        if u < len(units):
                            scores(u)
                        if 2 <= u < len(units) + 2:
                            turn(u - 2)
                        if u >= 3 and (u - 3) % NT == NT - 1:
                            weigh((u - 3) // NT)
                    pe.wait_ge(o_used, H)
                    for t in range(NT):
                        for h in range(H):
                            last = nc.tensor.matmul(pY[:, t, :], oT[:, h, t * P:(t + 1) * P], wo[:, h, :],
                                                    start=(h == 0), stop=(h == H - 1))
                    last.then_inc(y_ps, 1)

                @block.gpsimd
                def _(pool):
                    norm_in_pool(nc, pool, n, c)
                    for u, (h, q) in enumerate(units):
                        pool.wait_ge(inv_ready, u + 1)
                        nc.gpsimd.tensor_scalar(prob[:, u % 3, 0:(q + 1) * P], prob[:, u % 3, 0:(q + 1) * P],
                                                rinv[:, u:u + 1], 1.0, ALU.mult, ALU.mult).then_inc(prob_ready, 1)
                    norm_out_pool(nc, pool, n, c)
            sc.clear()


def stage_silu_mha(nc, w, src, dst, c):
    H = w["L2_attn_q_scale"].shape[0]
    DH = D // H
    PAD = 32
    HQ = P // PAD
    G = H // HQ
    EPS_LEN = 1e-6
    units = [(q, h) for q in range(NT) for h in range(H)]
    with Scope(nc, "mha") as sc:
        n = Norm(sc)
        wt = {s: sc.sb("w" + s, [P, KD, D]) for s in "qkvo"}
        hs = {s: sc.sb("hs" + s, [P, H]) for s in "qk"}
        half = sc.sb("half", [P, NT * H])
        r = {s: sc.sb("r" + s, [P, NT, D]) for s in "qk"}
        sq = sc.sb("sq", [P, NT, D])
        ss = {s: sc.sb("ss" + s, [P, NT, H]) for s in "qk"}
        ln = {s: sc.sb("ln" + s, [P, NT, H]) for s in "qk"}
        inv = {s: sc.sb("inv" + s, [P, NT, H]) for s in "qk"}
        padded = {s: sc.sb("pad" + s, [P, NT, G * P]) for s in "qk"}
        qkT = {s: sc.sb(s + "T", [P, G, L]) for s in "qk"}
        v = sc.sb("v", [P, NT, D])
        prob = sc.sb("prob", [P, 3, L])
        probT = sc.sb("probT", [P, 2, L])
        o = sc.sb("o", [P, NT, D])
        oT = sc.sb("oT", [P, KD, L])
        nmax = sc.sb("nmax", [P, len(units)])
        rsum = sc.sb("rsum", [P, len(units)])
        rinv = sc.sb("rinv", [P, len(units)])
        pS = [sc.ps(f"pS{k}", [P, L]) for k in range(2)]
        pT = [sc.ps(f"pT{k}", [P, L]) for k in range(2)]
        pO = [sc.ps(f"pO{k}", [P, L]) for k in range(2)]
        pY = sc.ps("pY", [P, NT, D])
        (w_in, row_ps, row_ready, sq_ready, len_ready, fac_ready, pad_ready, padT_ps, padT_ready, s_ps, max_ready,
         exp_ready, t_ps, t_used, o_ps, o_ready, oT_ps, oT_ready, y_ps, dch, pz) = (
            sc.sem(s) for s in ("w_in", "row_ps", "row_ready", "sq_ready", "len_ready", "fac_ready", "pad_ready",
                                "padT_ps", "padT_ready", "s_ps", "max_ready", "exp_ready", "t_ps", "t_used", "o_ps",
                                "o_ready", "oT_ps", "oT_ready", "y_ps", "dch", "pz"))

        def heads(a):
            return a.rearrange("p t (h d) -> p (t h) d", d=DH)

        with nc.Block() as block:
            @block.sync
            def _(sp):
                for s in "qkvo":
                    sp.dma_start(wt[s][:, :, :], w["L2_attn_W" + s].rearrange("(k p) d -> p k d", p=P)).then_inc(w_in, 16)
                for s in "qk":
                    sp.dma_start(hs[s][:, :], w[f"L2_attn_{s}_scale"][None, :].to_broadcast([P, H])).then_inc(w_in, 16)
                sp.wait_ge(w_in, 16 * 6)

            @block.gpsimd
            def _(pool):
                nc.gpsimd.memset(half[:, :], 0.5)
                for s in "qk":
                    nc.gpsimd.memset(padded[s][:, :, :], 0.0).then_inc(pz, 1)
                pool.wait_ge(pz, 2)
        sc.clear()
        with nc.Fori(0, NB) as b:
            with nc.Block() as block:
                @block.sync
                def _(sp):
                    sp.dma_start(n.x[:, :, :], rows(src)[b]).then_inc(n.x_in, 16)
                    norm_out_store(sp, n, dst, b)

                @block.vector
                def _(dve):
                    link = Chain(dve, dch).link
                    norm_in_vector(nc, dve, n, link)
                    for i, s in enumerate("qk"):
                        dve.wait_ge(sq_ready, i + 1)
                        nc.vector.tensor_reduce(ss[s][:, :, :].rearrange("p t h -> p (t h)"), heads(sq[:, :, :]), AX.X,
                                                ALU.add).then_inc(len_ready, 1)
                    for i, s in enumerate("qk"):
                        dve.wait_ge(fac_ready, 2 * i + 2)
                        link(nc.vector.reciprocal(inv[s][:, :, :], inv[s][:, :, :]))
                        link(nc.vector.tensor_tensor(inv[s][:, :, :], inv[s][:, :, :], ln[s][:, :, :], ALU.mult))
                        link(nc.vector.tensor_tensor(inv[s][:, :, :], inv[s][:, :, :],
                                                     hs[s][:, :].unsqueeze(1).to_broadcast([P, NT, H]), ALU.mult))
                        dst_p = padded[s][:, :, :].rearrange("p t (h d) -> p (t h) d", d=PAD)[:, :, 0:DH]
                        fac = inv[s][:, :, :].rearrange("p t h -> p (t h)").unsqueeze(2).to_broadcast([P, NT * H, DH])
                        nc.vector.tensor_tensor(dst_p, heads(r[s][:, :, :]), fac, ALU.mult).then_inc(pad_ready, 1)

                    def neg_max(u):
                        dve.wait_ge(s_ps, u + 1)
                        nc.vector.tensor_reduce(nmax[:, u:u + 1], pS[u % 2][:, 0:(units[u][0] + 1) * P], AX.X, ALU.max,
                                                negate=True).then_inc(max_ready, 1)

                    def evacuate(u):
                        dve.wait_ge(t_ps, u + 1)
                        if u >= 2:
                            dve.wait_ge(o_ps, u - 1)
                        m = (units[u][0] + 1) * P
                        nc.vector.tensor_copy(probT[:, u % 2, 0:m], pT[u % 2][:, 0:m]).then_inc(t_used, 1)

                    def normalize(q):
                        dve.wait_ge(exp_ready, H * (q + 1))
                        cols = slice(q * H, (q + 1) * H)
                        link(nc.vector.reciprocal(rinv[:, cols], rsum[:, cols]))
                        dve.wait_ge(o_ps, H * (q + 1))
                        nc.vector.tensor_tensor(o[:, q, :].rearrange("p (h d) -> p h d", d=DH),
                                                pO[q % 2][:, 0:D].rearrange("p (h d) -> p h d", d=DH),
                                                rinv[:, cols].unsqueeze(2).to_broadcast([P, H, DH]), ALU.mult)\
                            .then_inc(o_ready, 1)

                    for u in range(len(units) + 2):
                        if u < len(units):
                            neg_max(u)
                        if u >= 2:
                            evacuate(u - 2)
                        if u >= 8 and (u - 8) % H == H - 1:
                            normalize((u - 8) // H)
                    normalize(NT - 1)
                    dve.wait_ge(y_ps, 1)
                    norm_out_vector(nc, dve, n, link, lambda t: pY[:, t, :])

                @block.scalar
                def _(act):
                    norm_in_evacuate(nc, act, n, pT)
                    for i, s in enumerate("qkv"):
                        out = v if s == "v" else r[s]
                        for t in range(NT):
                            act.wait_ge(row_ps, NT * i + t + 1)
                            nc.scalar.activation(out[:, t, :], pO[t % 2][:, 0:D], ACT.Silu).then_inc(row_ready, 1)
                        if s != "v":
                            act.wait_ge(row_ready, NT * (i + 1))
                            if i:
                                act.wait_ge(len_ready, i)
                            nc.scalar.activation(sq[:, :, :], r[s][:, :, :], ACT.Square).then_inc(sq_ready, 1)
                    for g in range(2 * G):
                        act.wait_ge(padT_ps, g + 1)
                        nc.scalar.activation(qkT["qk"[g // G]][:, g % G, :], pS[g % 2][:, :], ACT.Copy)\
                            .then_inc(padT_ready, 1)
                    for u, (q, h) in enumerate(units):
                        act.wait_ge(max_ready, u + 1)
                        if u >= 3:
                            act.wait_ge(t_ps, u - 2)
                        nc.scalar.activation(prob[:, u % 3, 0:(q + 1) * P], pS[u % 2][:, 0:(q + 1) * P], ACT.Exp,
                                             bias=nmax[:, u:u + 1], accum_out=rsum[:, u:u + 1]).then_inc(exp_ready, 1)
                    for k in range(KD):
                        act.wait_ge(oT_ps, k + 1)
                        nc.scalar.activation(oT[:, k, :], pS[k][:, :], ACT.Copy).then_inc(oT_ready, 1)
                    norm_out_scalar(nc, act, n, lambda t: pY[:, t, :])

                @block.tensor
                def _(pe):
                    norm_in_tensor(nc, pe, n, pT, c.ident)
                    pe.wait_ge(n.xnT_ready, KD)
                    for i, s in enumerate("qkv"):
                        for t in range(NT):
                            if NT * i + t >= 2:
                                pe.wait_ge(row_ready, NT * i + t - 1)
                            for k in range(KD):
                                last = nc.tensor.matmul(pO[t % 2][:, 0:D], n.xnT[:, k, t * P:(t + 1) * P], wt[s][:, k, :],
                                                        start=(k == 0), stop=(k == KD - 1))
                            last.then_inc(row_ps, 1)
                    for g in range(2 * G):
                        pe.wait_ge(pad_ready, g // G + 1)
                        if g >= 2:
                            pe.wait_ge(padT_ready, g - 1)
                        for t in range(NT):
                            last = nc.tensor.transpose(pS[g % 2][:, t * P:(t + 1) * P],
                                                       padded["qk"[g // G]][:, t, (g % G) * P:(g % G + 1) * P],
                                                       c.ident[:, :])
                        last.then_inc(padT_ps, 1)
                    pe.wait_ge(padT_ready, 2 * G)
                    pe.wait_ge(row_ready, 3 * NT)

                    def scores(u):
                        q, h = units[u]
                        at = slice(h % HQ * PAD, (h % HQ + 1) * PAD)
                        if u >= 2:
                            pe.wait_ge(exp_ready, u - 1)
                        nc.tensor.matmul(pS[u % 2][:, 0:(q + 1) * P], qkT["q"][at, h // HQ, q * P:(q + 1) * P],
                                         qkT["k"][at, h // HQ, 0:(q + 1) * P], start=True, stop=False,
                                         skip_group_check=True)
                        nc.tensor.matmul(pS[u % 2][:, q * P:(q + 1) * P], c.ident[:, :], c.causal[:, :],
                                         start=False, stop=True, skip_group_check=True).then_inc(s_ps, 1)

                    def turn(u):
                        pe.wait_ge(exp_ready, u + 1)
                        if u >= 2:
                            pe.wait_ge(t_used, u - 1)
                        for k in range(units[u][0] + 1):
                            last = nc.tensor.transpose(pT[u % 2][:, k * P:(k + 1) * P], prob[:, u % 3, k * P:(k + 1) * P],
                                                       c.ident[:, :])
                        last.then_inc(t_ps, 1)

                    def weigh(u):
                        q, h = units[u]
                        pe.wait_ge(t_used, u + 1)
                        if h == 0 and q >= 2:
                            pe.wait_ge(o_ready, q - 1)
                        for k in range(q + 1):
                            last = nc.tensor.matmul(pO[q % 2][:, h * DH:(h + 1) * DH], probT[:, u % 2, k * P:(k + 1) * P],
                                                    v[:, k, h * DH:(h + 1) * DH], start=(k == 0), stop=(k == q))
                        last.then_inc(o_ps, 1)

                    for u in range(len(units) + 3):
                        if u < len(units):
                            scores(u)
                        if 2 <= u < len(units) + 2:
                            turn(u - 2)
                        if u >= 3:
                            weigh(u - 3)
                    pe.wait_ge(o_ready, NT)
                    for k in range(KD):
                        for t in range(NT):
                            last = nc.tensor.transpose(pS[k][:, t * P:(t + 1) * P], o[:, t, k * P:(k + 1) * P],
                                                       c.ident[:, :])
                        last.then_inc(oT_ps, 1)
                    pe.wait_ge(oT_ready, KD)
                    for t in range(NT):
                        for k in range(KD):
                            last = nc.tensor.matmul(pY[:, t, :], oT[:, k, t * P:(t + 1) * P], wt["o"][:, k, :],
                                                    start=(k == 0), stop=(k == KD - 1))
                    last.then_inc(y_ps, 1)

                @block.gpsimd
                def _(pool):
                    norm_in_pool(nc, pool, n, c)
                    for i, s in enumerate("qk"):
                        pool.wait_ge(len_ready, i + 1)
                        flat = lambda a: a[:, :, :].rearrange("p t h -> p (t h)")
                        nc.gpsimd.tensor_tensor(flat(ln[s]), flat(ss[s]), half[:, :], ALU.pow).then_inc(fac_ready, 1)
                        pool.wait_ge(fac_ready, 2 * i + 1)
                        nc.gpsimd.tensor_scalar(flat(inv[s]), flat(ln[s]), EPS_LEN, None, ALU.add).then_inc(fac_ready, 1)
                    norm_out_pool(nc, pool, n, c)
            sc.clear()


def stage_mamba(nc, w, src, dst, c):
    DI, NS = w["L3_attn_A_log"].shape
    R = w["L3_attn_W_dt"].shape[0]
    CONV = w["L3_attn_W_conv"].shape[2]
    CT = DI // P
    X = R + 2 * NS
    units = [(ct, s) for ct in range(CT) for s in range(NS)]
    with Scope(nc, "mamba") as sc:
        n = Norm(sc)
        w_in_t = sc.sb("w_in_t", [P, KD, 2 * DI])
        w_conv = sc.sb("w_conv", [P, CT, CONV])
        b_conv = sc.sb("b_conv", [P, CT])
        w_x = sc.sb("w_x", [P, CT, X])
        w_dt = sc.sb("w_dt", [R, DI])
        b_dt = sc.sb("b_dt", [P, CT])
        a_neg = sc.sb("a_neg", [P, CT, NS])
        d_skip = sc.sb("d_skip", [P, CT])
        w_out = sc.sb("w_out", [P, CT, D])
        sel = sc.sb("sel", [X, 2 * NS, P])
        xc = sc.sb("xc", [P, CT, CONV - 1 + L])
        conv = sc.sb("conv", [P, CT, L])
        u_t = sc.sb("u_t", [P, CT, L])
        res = sc.sb("res", [P, CT, L])
        xdbl = sc.sb("xdbl", [X, L])
        delta = sc.sb("delta", [P, CT, L])
        e_t = sc.sb("e_t", [P, CT, L])
        bc = sc.sb("bc", [P, 2 * NS, L])
        dA = sc.sb("dA", [P, 3, L])
        dB = sc.sb("dB", [P, 3, L])
        h_t = sc.sb("h_t", [P, 3, L])
        hC = sc.sb("hC", [P, 3, L])
        pA = sc.ps("pA", [P, CT, L])
        pS = [sc.ps(f"pS{k}", [P, L]) for k in range(2)]
        pY = sc.ps("pY", [P, NT, D])
        (w_in, pz, xr_ps, xr_used, conv_ready, u_ready, xd_ps, xd_ready, dt_ps, z_ready, soft_ready, delta_ready, du_ready,
         bc_ps, bc_ready, da_ready, db_ready, scan_ready, hc_ready, s_ps, s_sum, y_ready, y_ps, dch, pch) = (
            sc.sem(s) for s in ("w_in", "pz", "xr_ps", "xr_used", "conv_ready", "u_ready", "xd_ps", "xd_ready", "dt_ps",
                                "z_ready", "soft_ready", "delta_ready", "du_ready", "bc_ps", "bc_ready", "da_ready",
                                "db_ready", "scan_ready", "hc_ready", "s_ps", "s_sum", "y_ready", "y_ps", "dch", "pch"))
        ln1 = conv
        with nc.Block() as block:
            @block.sync
            def _(sp):
                with nc.allow_non_contiguous_dma(reason="per-channel parameters, a few values each"):
                    sp.dma_start(w_in_t[:, :, :], w["L3_attn_W_in"].rearrange("(k p) d -> p k d", p=P)).then_inc(w_in, 16)
                    sp.dma_start(w_conv[:, :, :], w["L3_attn_W_conv"].rearrange("(c p) a j -> p c (a j)", p=P))\
                        .then_inc(w_in, 16)
                    sp.dma_start(w_x[:, :, :], w["L3_attn_W_xproj"].rearrange("(c p) e -> p c e", p=P)).then_inc(w_in, 16)
                    sp.dma_start(w_dt[:, :], w["L3_attn_W_dt"]).then_inc(w_in, 16)
                    sp.dma_start(a_neg[:, :, :], w["L3_attn_A_log"].rearrange("(c p) s -> p c s", p=P)).then_inc(w_in, 16)
                    sp.dma_start(w_out[:, :, :], w["L3_attn_W_out"].rearrange("(c p) d -> p c d", p=P)).then_inc(w_in, 16)
                    for t, name in ((b_conv, "b_conv"), (b_dt, "b_dt"), (d_skip, "D")):
                        sp.dma_start(t[:, :], w["L3_attn_" + name].rearrange("(c p) -> p c", p=P)).then_inc(w_in, 16)
                sp.wait_ge(w_in, 16 * 9)

            @block.scalar
            def _(act):
                act.wait_ge(w_in, 16 * 9)
                nc.scalar.activation(a_neg[:, :, :], a_neg[:, :, :], ACT.Exp).then_inc(u_ready, 1)

            @block.gpsimd
            def _(pool):
                nc.gpsimd.memset(xc[:, :, :], 0.0).then_inc(pz, 1)
                nc.gpsimd.memset(sel[:, :, :], 0.0).then_inc(pz, 1)
                pool.wait_ge(pz, 2)
                nc.gpsimd.affine_select(out=sel[:, :, :], in_=sel[:, :, :], compare_op=ALU.not_equal, fill=1.0,
                                        base=-R, pattern=[[-1, 2 * NS], [0, P]], channel_multiplier=1).then_inc(pz, 1)
                pool.wait_ge(pz, 3)
                pool.wait_ge(u_ready, 1)
                nc.gpsimd.tensor_scalar(a_neg[:, :, :].rearrange("p c s -> p (c s)"),
                                        a_neg[:, :, :].rearrange("p c s -> p (c s)"), -1.0, None, ALU.mult)\
                    .then_inc(pz, 1)
                pool.wait_ge(pz, 4)
        sc.clear()
        with nc.Fori(0, NB) as b:
            with nc.Block() as block:
                @block.sync
                def _(sp):
                    sp.dma_start(n.x[:, :, :], rows(src)[b]).then_inc(n.x_in, 16)
                    norm_out_store(sp, n, dst, b)

                @block.vector
                def _(dve):
                    link = Chain(dve, dch).link
                    norm_in_vector(nc, dve, n, link)
                    for j in range(CONV):
                        for ct in range(CT):
                            if j == 0:
                                dve.wait_ge(xr_used, ct + 1)
                                last = nc.vector.tensor_scalar(conv[:, ct, :], xc[:, ct, 0:L], w_conv[:, ct, 0:1], None,
                                                               ALU.mult)
                            else:
                                last = nc.vector.scalar_tensor_tensor(conv[:, ct, :], xc[:, ct, j:j + L],
                                                                      w_conv[:, ct, j:j + 1], conv[:, ct, :],
                                                                      ALU.mult, ALU.add)
                            if j == CONV - 1:
                                last.then_inc(conv_ready, 1)
                        if j < CONV - 1:
                            link(last)
                    for ct in range(CT):
                        dve.wait_ge(dt_ps, ct + 1)
                        last = nc.vector.tensor_scalar(delta[:, ct, :], pA[:, ct, :], b_dt[:, ct:ct + 1], None, ALU.add)
                        last.then_inc(z_ready, 1)
                    dve.wait_ge(soft_ready, 3)
                    for ct in range(CT):
                        nc.vector.scalar_tensor_tensor(bc[:, ct, :], e_t[:, ct, :], -0.5, e_t[:, ct, :],
                                                       ALU.mult, ALU.mult)
                        last = nc.vector.tensor_tensor(ln1[:, ct, :], ln1[:, ct, :], e_t[:, ct, :], ALU.min)
                    link(last)
                    for ct in range(CT):
                        last = nc.vector.tensor_tensor(bc[:, ct, :], bc[:, ct, :], e_t[:, ct, :], ALU.add)
                    link(last)
                    for ct in range(CT):
                        last = nc.vector.tensor_tensor(ln1[:, ct, :], ln1[:, ct, :], bc[:, ct, :], ALU.max)
                    link(last)
                    for ct in range(CT):
                        last = nc.vector.scalar_tensor_tensor(delta[:, ct, :], delta[:, ct, :], 0.0, ln1[:, ct, :],
                                                              ALU.max, ALU.add)
                        last.then_inc(delta_ready, 1)

                    def finish(ct):
                        dve.wait_ge(s_ps, ct + 1)
                        nc.vector.scalar_tensor_tensor(u_t[:, ct, :], u_t[:, ct, :], d_skip[:, ct:ct + 1],
                                                       pS[ct % 2][:, :], ALU.mult, ALU.add).then_inc(s_sum, 1)

                    for u, (ct, s) in enumerate(units):
                        dve.wait_ge(da_ready, u + 1)
                        dve.wait_ge(db_ready, u + 1)
                        if u >= 3:
                            dve.wait_ge(hc_ready, u - 2)
                        nc.vector.tensor_tensor_scan(h_t[:, u % 3, :], dA[:, u % 3, :], dB[:, u % 3, :], 0.0,
                                                     ALU.mult, ALU.add).then_inc(scan_ready, 1)
                        if s == 3 and ct >= 1:
                            finish(ct - 1)
                    finish(CT - 1)
                    dve.wait_ge(y_ps, 1)
                    norm_out_vector(nc, dve, n, link, lambda t: pY[:, t, :])

                @block.scalar
                def _(act):
                    norm_in_evacuate(nc, act, n, pS)
                    for i in range(2 * CT):
                        act.wait_ge(xr_ps, i + 1)
                        if i < CT:
                            nc.scalar.activation(xc[:, i, CONV - 1:], pA[:, i % CT, :], ACT.Copy).then_inc(xr_used, 1)
                        else:
                            nc.scalar.activation(res[:, i - CT, :], pA[:, i % CT, :], ACT.Silu).then_inc(xr_used, 1)
                    for ct in range(CT):
                        act.wait_ge(conv_ready, ct + 1)
                        nc.scalar.activation(u_t[:, ct, :], conv[:, ct, :], ACT.Silu, bias=b_conv[:, ct:ct + 1])\
                            .then_inc(u_ready, 1)
                    act.wait_ge(xd_ps, 1)
                    nc.scalar.activation(xdbl[:, :], pS[0][0:X, :], ACT.Copy).then_inc(xd_ready, 1)
                    act.wait_ge(z_ready, CT)
                    nc.scalar.activation(e_t[:, :, :], delta[:, :, :], ACT.Abs).then_inc(soft_ready, 1)
                    act.wait_ge(soft_ready, 1)
                    nc.scalar.activation(e_t[:, :, :], e_t[:, :, :], ACT.Exp, scale=-1.0).then_inc(soft_ready, 1)
                    act.wait_ge(soft_ready, 2)
                    act.wait_ge(u_ready, CT)
                    nc.scalar.activation(ln1[:, :, :], e_t[:, :, :], ACT.Ln, bias=1.0).then_inc(soft_ready, 1)
                    act.wait_ge(delta_ready, 4)
                    for i in range(2 * NS):
                        act.wait_ge(bc_ps, i + 1)
                        nc.scalar.activation(bc[:, i, :], pA[:, i % CT, :], ACT.Copy).then_inc(bc_ready, 1)
                    for u, (ct, s) in enumerate(units):
                        if u >= 3:
                            act.wait_ge(scan_ready, u - 2)
                        nc.scalar.activation(dA[:, u % 3, :], delta[:, ct, :], ACT.Exp, scale=a_neg[:, ct, s:s + 1])\
                            .then_inc(da_ready, 1)
                    norm_out_scalar(nc, act, n, lambda t: pY[:, t, :])

                @block.tensor
                def _(pe):
                    norm_in_tensor(nc, pe, n, pS, c.ident)
                    pe.wait_ge(n.xnT_ready, KD)
                    for i in range(2 * CT):
                        if i >= CT:
                            pe.wait_ge(xr_used, i - CT + 1)
                        for k in range(KD):
                            last = nc.tensor.matmul(pA[:, i % CT, :], w_in_t[:, k, i * P:(i + 1) * P], n.xnT[:, k, :],
                                                    start=(k == 0), stop=(k == KD - 1))
                        last.then_inc(xr_ps, 1)
                    for ct in range(CT):
                        pe.wait_ge(u_ready, ct + 1)
                        last = nc.tensor.matmul(pS[0][0:X, :], w_x[:, ct, :], u_t[:, ct, :], start=(ct == 0),
                                                stop=(ct == CT - 1))
                    last.then_inc(xd_ps, 1)
                    pe.wait_ge(xd_ready, 1)
                    pe.wait_ge(xr_used, 2 * CT)
                    for ct in range(CT):
                        nc.tensor.matmul(pA[:, ct, :], w_dt[:, ct * P:(ct + 1) * P], xdbl[0:R, :], start=True, stop=True)\
                            .then_inc(dt_ps, 1)
                    for i in range(2 * NS):
                        if i < CT:
                            pe.wait_ge(z_ready, i + 1)
                        else:
                            pe.wait_ge(bc_ready, i - CT + 1)
                        nc.tensor.matmul(pA[:, i % CT, :], sel[:, i, :], xdbl[:, :], start=True, stop=True)\
                            .then_inc(bc_ps, 1)
                    for u, (ct, s) in enumerate(units):
                        if s == 0 and ct >= 2:
                            pe.wait_ge(s_sum, ct - 1)
                        pe.wait_ge(hc_ready, u + 1)
                        last = nc.tensor.matmul(pS[ct % 2][:, :], c.ident[:, :], hC[:, u % 3, :], start=(s == 0),
                                                stop=(s == NS - 1))
                        last.then_inc(bc_ps, 1)
                        if s == NS - 1:
                            last = None
                            pe.wait_ge(bc_ps, 2 * NS + u + 1)
                            pe.sem_inc(s_ps, 1)
                    for ct in range(CT):
                        pe.wait_ge(y_ready, ct + 1)
                    for t in range(NT):
                        for ct in range(CT):
                            last = nc.tensor.matmul(pY[:, t, :], res[:, ct, t * P:(t + 1) * P], w_out[:, ct, :],
                                                    start=(ct == 0), stop=(ct == CT - 1))
                    last.then_inc(y_ps, 1)

                @block.gpsimd
                def _(pool):
                    norm_in_pool(nc, pool, n, c)
                    pool.wait_ge(delta_ready, CT)
                    pool.wait_ge(u_ready, CT)
                    for ct in range(CT):
                        nc.gpsimd.tensor_tensor(e_t[:, ct, :], delta[:, ct, :], u_t[:, ct, :], ALU.mult)\
                            .then_inc(du_ready, 1)

                    def state_in(u):
                        ct, s = units[u]
                        pool.wait_ge(du_ready, ct + 1)
                        pool.wait_ge(bc_ready, NS if u else 2 * NS)
                        if u >= 3:
                            pool.wait_ge(scan_ready, u - 2)
                        nc.gpsimd.tensor_tensor(dB[:, u % 3, :], e_t[:, ct, :], bc[:, s, :], ALU.mult)\
                            .then_inc(db_ready, 1)

                    def state_out(u):
                        ct, s = units[u]
                        pool.wait_ge(scan_ready, u + 1)
                        if u >= 3:
                            pool.wait_ge(bc_ps, 2 * NS + u - 2)
                        nc.gpsimd.tensor_tensor(hC[:, u % 3, :], h_t[:, u % 3, :], bc[:, NS + s, :], ALU.mult)\
                            .then_inc(hc_ready, 1)

                    def gate(ct):
                        pool.wait_ge(s_sum, ct + 1)
                        nc.gpsimd.tensor_tensor(res[:, ct, :], res[:, ct, :], u_t[:, ct, :], ALU.mult)\
                            .then_inc(y_ready, 1)

                    for u in range(len(units) + 1):
                        if u < len(units):
                            state_in(u)
                        if u >= 1:
                            state_out(u - 1)
                        if u >= 8 and (u - 8) % NS == NS - 1:
                            gate((u - 8) // NS)
                    gate(CT - 1)
                    norm_out_pool(nc, pool, n, c)
            sc.clear()


def stage_expert_choice(nc, w, src, dst, c):
    E, S, _, M = w["L1_ffn_W1"].shape
    K = w["L1_ffn_W2"].shape[3]
    T = NB * L
    CAP = int(1.5 * T / E)
    assert CAP == P and D == 2 * P and M == 2 * P
    GE = 4
    MT = M // P
    TAKEN = -3.0e38
    normed = nc.dram_tensor("normed", [T, D], F32, kind="Internal").ap()
    logit_d = nc.dram_tensor("router_logits", [E, T], F32, kind="Internal").ap()
    moe_sum = nc.dram_tensor("moe_sum", [T, D], F32, kind="Internal").ap()

    with Scope(nc, "route") as sc:
        n = Norm(sc)
        wr = sc.sb("wr", [P, KD, E])
        lg = sc.sb("lg", [E, L])
        zero = sc.sb("zero", [P, NT, D])
        pX = [sc.ps(f"pX{k}", [P, L]) for k in range(KD)]
        pL = sc.ps("pL", [E, L])
        w_in, z_ready, lg_ps, lg_ready, stored, dch = (
            sc.sem(s) for s in ("w_in", "z_ready", "lg_ps", "lg_ready", "stored", "dch"))
        with nc.Block() as block:
            @block.sync
            def _(sp):
                sp.dma_start(wr[:, :, :], w["L1_ffn_Wr"].rearrange("(k p) e -> p k e", p=P)).then_inc(w_in, 16)
                sp.wait_ge(w_in, 16)

            @block.vector
            def _(dve):
                nc.vector.memset(zero[:, :, :], 0.0).then_inc(z_ready, 1)
                dve.wait_ge(z_ready, 1)
        sc.clear()
        with nc.Fori(0, NB) as b:
            with nc.Block() as block:
                @block.sync
                def _(sp):
                    sp.dma_start(n.x[:, :, :], rows(src)[b]).then_inc(n.x_in, 16)
                    sp.dma_start(moe_sum.rearrange("(b t p) d -> b p t d", t=NT, p=P)[b], zero[:, :, :])\
                        .then_inc(stored, 16)
                    sp.wait_ge(n.xn_ready, NT)
                    sp.dma_start(normed.rearrange("(b t p) d -> b p t d", t=NT, p=P)[b], n.xn[:, :, :])\
                        .then_inc(stored, 16)
                    sp.wait_ge(lg_ready, 1)
                    sp.dma_start(logit_d.rearrange("e (b l) -> b e l", l=L)[b], lg[:, :]).then_inc(stored, 16)
                    sp.wait_ge(stored, 48)

                @block.vector
                def _(dve):
                    norm_in_vector(nc, dve, n, Chain(dve, dch).link)

                @block.scalar
                def _(act):
                    norm_in_evacuate(nc, act, n, pX)
                    act.wait_ge(lg_ps, 1)
                    nc.scalar.activation(lg[:, :], pL[:, :], ACT.Copy).then_inc(lg_ready, 1)

                @block.tensor
                def _(pe):
                    norm_in_tensor(nc, pe, n, pX, c.ident)
                    pe.wait_ge(n.xnT_ready, KD)
                    for k in range(KD):
                        last = nc.tensor.matmul(pL[:, :], wr[:, k, :], n.xnT[:, k, :], start=(k == 0), stop=(k == KD - 1))
                    last.then_inc(lg_ps, 1)

                @block.gpsimd
                def _(pool):
                    norm_in_pool(nc, pool, n, c)
            sc.clear()

    with Scope(nc, "expert") as sc:
        lg = sc.sb("lg", [E, T])
        vals = sc.sb("vals", [E, CAP])
        idx = sc.sb("idx", [E, CAP], U32)
        idx_f = sc.sb("idx_f", [E, CAP])
        nmax = sc.sb("nmax", [E, 1])
        rsum = sc.sb("rsum", [E, 1])
        idxT = sc.sb("idxT", [P, E], U32)
        wgtT = sc.sb("wgtT", [P, E])
        ES = E * S // 2
        b1r = sc.sb("b1r", [ES, 2, M])
        b1T = sc.sb("b1T", [P, E * S, MT])
        ones = sc.sb("ones", [1, P])
        w1 = [sc.sb(f"w1_{g}", [P, GE, S, 2, M]) for g in range(2)]
        w2 = [sc.sb(f"w2_{g}", [P, GE, S, 2, K]) for g in range(2)]
        b2 = [sc.sb(f"b2_{g}", [1, GE, S * K]) for g in range(2)]
        xg = [sc.sb(f"xg_{g}", [P, GE, D]) for g in range(2)]
        col = [sc.sb(f"col_{g}", [P, GE], U32) for g in range(2)]
        xgT = sc.sb("xgT", [P, 2, KD, P])
        hT = sc.sb("hT", [P, 2, S * MT, P])
        y = sc.sb("y", [P, 2, D])
        pX = [sc.ps(f"pX{k}", [P, L]) for k in range(2)]
        pH = [sc.ps(f"pH{k}", [P, S * MT, P]) for k in range(2)]
        pY = [sc.ps(f"pY{k}", [P, L]) for k in range(2)]
        (lg_in, b1_in, w_in, dch, max_ready, exp_ready, wgt_ready, t_ps, t_ready, col_ready, x_ps, x_ready, h_ps, hb_ready,
         h_ready, y_ps, y_ready, one_ready) = (
            sc.sem(s) for s in ("lg_in", "b1_in", "w_in", "dch", "max_ready", "exp_ready", "wgt_ready", "t_ps",
                                "t_ready", "col_ready", "x_ps", "x_ready", "h_ps", "hb_ready", "h_ready", "y_ps",
                                "y_ready", "one_ready"))

        def load_group(sp, g, e0):
            for j in range(GE):
                sp.dma_start(w1[g][:, j, :, :, :].rearrange("p s k m -> p s (k m)"),
                             w["L1_ffn_W1"][bass.ds(e0 + j, 1)].rearrange("e s (p k) m -> p (e s) (k m)", k=2))\
                    .then_inc(w_in, 16)
                sp.dma_start(w2[g][:, j, :, :, :].rearrange("p s k m -> p s (k m)"),
                             w["L1_ffn_W2"][bass.ds(e0 + j, 1)].rearrange("e s (p k) m -> p (e s) (k m)", k=2))\
                    .then_inc(w_in, 16)
            sp.dma_start(b2[g][:, :, :], w["L1_ffn_b2"].rearrange("(a e) s k -> a e (s k)", a=1)[:, bass.ds(e0, GE), :])\
                .then_inc(w_in, 16)

        LOADS = 16 * (2 * GE + 1)

        def gather_group(pool, g):
            for j in range(GE):
                pool.indirect_dma_start(out=xg[g][:, j, :], out_offset=None, in_=normed,
                                        in_offset=bass.IndirectOffsetOnAxis(ap=col[g][:, j:j + 1], axis=0))\
                    .then_inc(c.gathered, 16)

        with nc.Block() as block:
            @block.sync
            def _(sp):
                sp.dma_start(lg[:, :], logit_d).then_inc(lg_in, 16)
                sp.dma_start(b1r[:, :, :], w["L1_ffn_b1"].rearrange("(a e) s m -> (e s) a m", a=2)).then_inc(b1_in, 16)
                load_group(sp, 0, 0)
                sp.wait_ge(w_in, LOADS)

            @block.vector
            def _(dve):
                link = Chain(dve, dch).link
                nc.vector.memset(ones[:, :], 1.0).then_inc(one_ready, 1)
                dve.wait_ge(lg_in, 16)
                for i in range(CAP // 8):
                    eight = slice(8 * i, 8 * i + 8)
                    link(nc.vector.max(vals[:, eight], lg[:, :]))
                    link(nc.vector.max_index(idx[:, eight], vals[:, eight], lg[:, :]))
                    link(nc.vector.match_replace(lg[:, :], vals[:, eight], lg[:, :], TAKEN))
                link(nc.vector.tensor_copy(idx_f[:, :], idx[:, :]))
                nc.vector.tensor_scalar(nmax[:, :], vals[:, 0:1], -1.0, None, ALU.mult).then_inc(max_ready, 1)
                dve.wait_ge(exp_ready, 1)
                link(nc.vector.reciprocal(rsum[:, :], rsum[:, :]))
                nc.vector.tensor_scalar(vals[:, :], vals[:, :], rsum[:, 0:1], None, ALU.mult).then_inc(wgt_ready, 1)
                dve.wait_ge(t_ps, 1)
                nc.vector.tensor_copy(b1T[:, :, :].rearrange("p (a e) k -> p a k e", a=2),
                                      pX[1][:, 0:2 * MT * ES].rearrange("p (a k e) -> p a k e", a=2, k=MT))\
                    .then_inc(t_ready, 1)
                dve.wait_ge(t_ps, 2)
                link(nc.vector.tensor_copy(idxT[:, :], pX[0][:, 0:E]))
                nc.vector.tensor_copy(wgtT[:, :], pX[0][:, E:2 * E]).then_inc(t_ready, 1)
                nc.vector.tensor_copy(col[0][:, :], idxT[:, 0:GE]).then_inc(col_ready, 1)
                dve.wait_ge(t_ready, 2)

            @block.scalar
            def _(act):
                act.wait_ge(max_ready, 1)
                nc.scalar.activation(vals[:, :], vals[:, :], ACT.Exp, bias=nmax[:, 0:1], accum_out=rsum[:, 0:1])\
                    .then_inc(exp_ready, 1)

            @block.tensor
            def _(pe):
                pe.wait_ge(b1_in, 16)
                for a in range(2):
                    for k in range(MT):
                        at = (a * MT + k) * ES
                        last = nc.tensor.transpose(pX[1][:, at:at + ES], b1r[:, a, k::MT], c.ident[0:ES, 0:ES])
                last.then_inc(t_ps, 1)
                pe.wait_ge(wgt_ready, 1)
                nc.tensor.transpose(pX[0][:, 0:E], idx_f[:, :], c.ident[0:E, 0:E])
                nc.tensor.transpose(pX[0][:, E:2 * E], vals[:, :], c.ident[0:E, 0:E]).then_inc(t_ps, 1)

            @block.gpsimd
            def _(pool):
                pool.wait_ge(col_ready, 1)
                gather_group(pool, 0)
                pool.wait_ge(c.gathered, 16 * GE)
        sc.clear()

        def half(g, e0, more):
            with nc.Block() as block:
                @block.sync
                def _(sp):
                    if more:
                        load_group(sp, 1 - g, e0 + GE)
                        sp.wait_ge(w_in, LOADS)

                @block.vector
                def _(dve):
                    if more:
                        nc.vector.tensor_copy(col[1 - g][:, :], idxT[:, bass.ds(e0 + GE, GE)]).then_inc(col_ready, 1)

                    def add_b1(j):
                        dve.wait_ge(h_ps, j + 1)
                        if j >= 2:
                            dve.wait_ge(y_ps, j - 1)
                        bias = b1T[:, bass.ds((e0 + j) * S, S), :].rearrange("p s k -> p (s k)")
                        nc.vector.tensor_tensor(hT[:, j % 2, :, :], pH[j % 2][:, :, :],
                                                bias.unsqueeze(2).to_broadcast([P, S * MT, P]), ALU.add)\
                            .then_inc(hb_ready, 1)

                    def weigh(j):
                        dve.wait_ge(y_ps, j + 1)
                        if j:
                            dve.wait_ge(c.added, (e0 + j) * 16)
                        nc.vector.tensor_tensor(y[:, j % 2, :], pY[j % 2][:, 0:D],
                                                wgtT[:, bass.ds(e0 + j, 1)].to_broadcast([P, D]), ALU.mult)\
                            .then_inc(y_ready, 1)

                    for j in range(GE + 1):
                        if j < GE:
                            add_b1(j)
                        if j >= 1:
                            weigh(j - 1)

                @block.scalar
                def _(act):
                    def turned(j):
                        act.wait_ge(x_ps, j + 1)
                        if j >= 2:
                            act.wait_ge(h_ps, j - 1)
                        nc.scalar.activation(xgT[:, j % 2, :, :].rearrange("p k t -> p (k t)"), pX[j % 2][:, 0:D], ACT.Copy)\
                            .then_inc(x_ready, 1)

                    turned(0)
                    for j in range(GE):
                        if j + 1 < GE:
                            turned(j + 1)
                        act.wait_ge(hb_ready, j + 1)
                        nc.scalar.activation(hT[:, j % 2, :, :], hT[:, j % 2, :, :], ACT.Gelu).then_inc(h_ready, 1)

                @block.tensor
                def _(pe):
                    def turn(j):
                        if j >= 2:
                            pe.wait_ge(x_ready, j - 1)
                        for k in range(KD):
                            last = nc.tensor.transpose(pX[j % 2][:, k * P:(k + 1) * P], xg[g][:, j, k::KD], c.ident[:, :])
                        last.then_inc(x_ps, 1)

                    def hidden(j):
                        pe.wait_ge(x_ready, j + 1)
                        if j >= 2:
                            pe.wait_ge(hb_ready, j - 1)
                        for s in range(S):
                            for m in range(MT):
                                for k in range(KD):
                                    last = nc.tensor.matmul(pH[j % 2][:, s * MT + m, :], w1[g][:, j, s, k, m::MT],
                                                            xgT[:, j % 2, k, :], start=(k == 0), stop=(k == KD - 1))
                        last.then_inc(h_ps, 1)

                    def output(j):
                        pe.wait_ge(h_ready, j + 1)
                        if j >= 2:
                            pe.wait_ge(y_ready, j - 1)
                        nc.tensor.matmul(pY[j % 2][:, 0:D], ones[:, :], b2[g][:, j, :], start=True, stop=False,
                                         skip_group_check=True)
                        for s in range(S):
                            for m in range(MT):
                                last = nc.tensor.matmul(pY[j % 2][:, s * K:(s + 1) * K], hT[:, j % 2, s * MT + m, :],
                                                        w2[g][:, j, s, m, :], start=False, stop=(m == MT - 1),
                                                        skip_group_check=True)
                        last.then_inc(y_ps, 1)

                    turn(0)
                    for j in range(GE + 1):
                        if j + 1 < GE:
                            turn(j + 1)
                        if j < GE:
                            hidden(j)
                        if j >= 1:
                            output(j - 1)

                @block.gpsimd
                def _(pool):
                    if more:
                        pool.wait_ge(col_ready, 1)
                        gather_group(pool, 1 - g)
                    for j in range(GE):
                        pool.wait_ge(y_ready, j + 1)
                        pool.indirect_dma_start(out=moe_sum, in_=y[:, j % 2, :], in_offset=None,
                                                out_offset=bass.IndirectOffsetOnAxis(ap=col[g][:, j:j + 1], axis=0),
                                                compute_op=ALU.add).then_inc(c.added, 16)
                    pool.wait_ge(c.added, (e0 + GE) * 16)
                    if more:
                        pool.wait_ge(c.gathered, (e0 + 2 * GE) * 16)
            sc.clear()

        with nc.Fori(0, E // (2 * GE) - 1) as i:
            half(0, i * (2 * GE), True)
            half(1, i * (2 * GE) + GE, True)
        half(0, E - 2 * GE, True)
        half(1, E - GE, False)

    with Scope(nc, "moe_out") as sc:
        n = Norm(sc)
        y = sc.sb("y", [P, NT, D])
        y_in, dch = sc.sem("y_in"), sc.sem("dch")
        with nc.Fori(0, NB) as b:
            with nc.Block() as block:
                @block.sync
                def _(sp):
                    sp.dma_start(y[:, :, :], moe_sum.rearrange("(b t p) d -> b p t d", t=NT, p=P)[b]).then_inc(y_in, 16)
                    sp.dma_start(n.x[:, :, :], rows(src)[b]).then_inc(n.x_in, 16)
                    norm_out_store(sp, n, dst, b)

                @block.vector
                def _(dve):
                    dve.wait_ge(y_in, 16)
                    norm_out_vector(nc, dve, n, Chain(dve, dch).link, lambda t: y[:, t, :])

                @block.scalar
                def _(act):
                    norm_out_scalar(nc, act, n, lambda t: y[:, t, :])

                @block.gpsimd
                def _(pool):
                    pool.wait_ge(n.x_in, 16)
                    norm_out_pool(nc, pool, n, c)
            sc.clear()


def stage_delta(nc, w, src, dst, c):
    H = w["L0_attn_Wb"].shape[1]
    DH = D // H
    CONV = w["L0_attn_conv_q"].shape[1]
    TAPS = [w["L0_attn_fir_" + f].shape[2] for f in "sml"]
    PAST = max(TAPS) - 1
    NG = w["L0_attn_gate_w"].shape[2]
    CH = 32
    NC = P // CH
    PE_TAPS = 24
    LEVELS = 4
    with Scope(nc, "delta") as sc:
        n = Norm(sc)
        wt = {s: sc.sb("w" + s, [P, KD, D]) for s in "qkvo"}
        wg = sc.sb("wg", [P, KD, H * NG + H])
        wconv = {s: sc.sb("wconv" + s, [P, KD, CONV]) for s in "qkv"}
        fir = {f: sc.sb("fir" + f, [P, KD, k]) for f, k in zip("sml", TAPS)}
        diag = sc.sb("diag", [P, KD, PE_TAPS, P])
        masks = sc.sb("masks", [P, LEVELS + 3, P])
        gate_b = sc.sb("gate_b", [P, H, NG])
        itemp = sc.sb("itemp", [P, H])
        geps = sc.sb("geps", [P, H])
        gscale = sc.sb("gscale", [P, H])
        norm_w = sc.sb("norm_w", [P, DH])
        xc = {s: sc.sb("xc" + s, [P, KD, CONV - 1 + L]) for s in "qkv"}
        cT = {s: sc.sb("c" + s, [P, KD, (PAST if s == "v" else 0) + L]) for s in "qkv"}
        r = {s: sc.sb("r" + s, [P, NT, D]) for s in "qkv"}
        kb = sc.sb("kb", [P, NT, D])
        vb = sc.sb("vb", [P, NT, D])
        sq = sc.sb("sq", [P, NT, D])
        ss = {s: sc.sb("ss" + s, [P, NT * H]) for s in "qko"}
        beta = sc.sb("beta", [P, NT, H])
        gl = sc.sb("gl", [P, NT, H, NG])
        gred = sc.sb("gred", [P, NT * H])
        hT = {s: sc.sb("hT" + s, [DH, H, L]) for s in ("q", "k", "kb")}
        facc = {f: sc.sb("facc" + f, [P, KD, L]) for f in "sml"}
        GT = sc.sb("GT", [P, H, P])
        Tm = sc.sb("Tm", [P, H, P])
        TT = sc.sb("TT", [P, H, P])
        X = sc.sb("X", [P, H, P])
        attnT = sc.sb("attnT", [P, H, P])
        u_t = sc.sb("u_t", [P, D])
        ua = sc.sb("ua", [P, D])
        wT = sc.sb("wT", [DH, H, P])
        S = sc.sb("S", [DH, D])
        do = sc.sb("do", [P, NT, D])
        o = sc.sb("o", [P, NT, D])
        oT = sc.sb("oT", [P, KD, L])
        pb = [sc.ps(f"pb{k}", [P, L]) for k in range(6)]
        pY = sc.ps("pY", [P, NT, D])
        pW, pS = pY[:, 0, :], pY[0:DH, 2, :]
        NAMES = ("w_in", "zeroed", "proj_ps", "xc_ready", "conv_ready", "c_ready", "gate_ps", "beta_ready", "gate_sub",
                 "gate_exp", "row_ps", "row_ready", "sq_ready", "ss_ready", "ilen_ready", "rows_ready", "firp_ps",
                 "firp_ready", "hT_ps", "hT_ready", "g_ps", "gt_ready", "t_ready", "x_ps", "x_masked", "tx_ps",
                 "attn_ready", "uw_ps", "uw_ready", "ws_ps", "ua_ready", "ks_ps", "s_ready", "do_ps", "do_ready",
                 "s_zero", "fir_done", "fir_ps", "fir_used", "o_sq", "o_ss", "o_ilen", "o_ready", "oT_ps", "oT_ready",
                 "y_ps", "dch", "pch", "setup")
        z = {name: sc.sem(name) for name in NAMES}

        def xc_out(s, k):
            return facc[{"q": "s", "k": "m", "v": "l"}[s]][:, k, :]

        def xc_silu(s, k):
            return cT[s][:, k, (PAST if s == "v" else 0):]

        def hd(a):
            return a[:, :, :].rearrange("p t (h d) -> p (t h) d", d=DH)

        def per_head(a):
            return a.unsqueeze(2).to_broadcast([P, NT * H, DH])

        with nc.Block() as block:
            @block.sync
            def _(sp):
                def load(out, in_):
                    sp.dma_start(out, in_).then_inc(z["w_in"], 16)

                for s in "qkvo":
                    load(wt[s][:, :, :], w["L0_attn_W" + s].rearrange("(k p) d -> p k d", p=P))
                with nc.allow_non_contiguous_dma(reason="small weights"):
                    for h in range(H):
                        load(wg[:, :, h * NG:(h + 1) * NG], w["L0_attn_gate_w"][h].rearrange("(k p) g -> p k g", p=P))
                    load(wg[:, :, H * NG:], w["L0_attn_Wb"].rearrange("(k p) h -> p k h", p=P))
                    for s in "qkv":
                        load(wconv[s][:, :, :], w["L0_attn_conv_" + s].rearrange("(k p) j -> p k j", p=P))
                    for f in "sml":
                        load(fir[f][:, :, :], w["L0_attn_fir_" + f].rearrange("(k h) d j -> (h d) k j", k=KD))
                load(masks[:, :, :], w["chunk_masks"])
                load(gate_b[:, :, :], w["L0_attn_gate_b"][None, :, :].to_broadcast([P, H, NG]))
                for t, name in ((itemp, "log_temp"), (geps, "eps_param")):
                    load(t[:, :], w["L0_attn_" + name].rearrange("h a -> a h").to_broadcast([P, H]))
                load(norm_w[:, :], w["L0_attn_norm_w"][None, :].to_broadcast([P, DH]))
                sp.wait_ge(z["w_in"], 16 * (4 + H + 1 + 3 + 3 + 1 + 1 + 2 + 1))

            @block.scalar
            def _(act):
                act.wait_ge(z["w_in"], 16 * (4 + H + 1 + 3 + 3 + 1 + 1 + 2 + 1))
                nc.scalar.activation(itemp[:, :], itemp[:, :], ACT.Exp, scale=-1.0).then_inc(z["setup"], 1)
                act.wait_ge(z["setup"], 1)

            @block.vector
            def _(dve):
                link = Chain(dve, z["dch"]).link
                dve.wait_ge(z["w_in"], 16 * (4 + H + 1 + 3 + 3 + 1 + 1 + 2 + 1))
                link(nc.vector.tensor_scalar(geps[:, :], geps[:, :], 0.0, 0.2, ALU.max, ALU.min))
                link(nc.vector.tensor_scalar(gscale[:, :], geps[:, :], -float(NG), 1.0, ALU.mult, ALU.add))
                for k in range(KD):
                    for j in range(PE_TAPS):
                        last = nc.vector.tensor_scalar(diag[:, k, j, :], c.ident[:, :], fir["l"][:, k, j:j + 1], None,
                                                       ALU.mult)
                link(last)

            @block.gpsimd
            def _(pool):
                for s in "qkv":
                    nc.gpsimd.memset(xc[s][:, :, :], 0.0)
                nc.gpsimd.memset(cT["v"][:, :, :], 0.0).then_inc(z["zeroed"], 1)
                pool.wait_ge(z["zeroed"], 1)
        sc.clear()
        with nc.Fori(0, NB) as b:
            with nc.Block() as block:
                @block.sync
                def _(sp):
                    sp.dma_start(n.x[:, :, :], rows(src)[b]).then_inc(n.x_in, 16)
                    norm_out_store(sp, n, dst, b)

                @block.vector
                def _(dve):
                    link = Chain(dve, z["dch"]).link
                    norm_in_vector(nc, dve, n, link)
                    for i, s in enumerate("qkv"):
                        for j in range(CONV):
                            for k in range(KD):
                                if j == 0:
                                    dve.wait_ge(z["xc_ready"], KD * i + k + 1)
                                    last = nc.vector.tensor_scalar(xc_out(s, k), xc[s][:, k, 0:L], wconv[s][:, k, 0:1],
                                                                   None, ALU.mult)
                                else:
                                    last = nc.vector.scalar_tensor_tensor(xc_out(s, k), xc[s][:, k, j:j + L],
                                                                          wconv[s][:, k, j:j + 1], xc_out(s, k),
                                                                          ALU.mult, ALU.add)
                            if j < CONV - 1:
                                link(last)
                        last.then_inc(z["conv_ready"], 1)
                    flat = gl[:, :, :, :].rearrange("p t h g -> p (t h) g")
                    gps = pb[5][:, 0:NT * (NG + 1) * H].rearrange("p (t x) -> p t x", t=NT)
                    dve.wait_ge(z["gate_ps"], 1)
                    dve.wait_ge(z["beta_ready"], 1)
                    for t in range(NT):
                        last = nc.vector.tensor_tensor(gl[:, t, :, :], gps[:, t, 0:H * NG].rearrange("p (h g) -> p h g", g=NG),
                                                       gate_b[:, :, :], ALU.add)
                    link(last)
                    for t in range(NT):
                        last = nc.vector.tensor_tensor(gl[:, t, :, :], gl[:, t, :, :],
                                                       itemp[:, :].unsqueeze(2).to_broadcast([P, H, NG]), ALU.mult)
                    link(last)
                    link(nc.vector.tensor_reduce(gred[:, :], flat, AX.X, ALU.max))
                    nc.vector.tensor_tensor(flat, flat, gred[:, :].unsqueeze(2).to_broadcast([P, NT * H, NG]),
                                            ALU.subtract).then_inc(z["gate_sub"], 1)
                    for i, s in enumerate("qk"):
                        dve.wait_ge(z["sq_ready"], i + 1)
                        nc.vector.tensor_reduce(ss[s][:, :], hd(sq), AX.X, ALU.add).then_inc(z["ss_ready"], 1)
                    for i, s in enumerate("qk"):
                        dve.wait_ge(z["ilen_ready"], 2 * i + 2)
                        last = nc.vector.tensor_tensor(hd(r[s]), hd(r[s]), per_head(ss[s][:, :]), ALU.mult)
                        last.then_inc(z["rows_ready"], 1)
                    bflat = beta[:, :, :].rearrange("p t h -> p (t h)")
                    dve.wait_ge(z["rows_ready"], 2)
                    nc.vector.tensor_tensor(hd(kb), hd(r["k"]), per_head(bflat), ALU.mult).then_inc(z["rows_ready"], 1)
                    dve.wait_ge(z["row_ready"], 6)
                    nc.vector.tensor_tensor(hd(vb), hd(r["v"]), per_head(bflat), ALU.mult).then_inc(z["rows_ready"], 1)
                    dve.wait_ge(z["gate_exp"], 1)
                    link(nc.vector.tensor_reduce(gred[:, :], flat, AX.X, ALU.add))
                    link(nc.vector.reciprocal(gred[:, :], gred[:, :]))
                    link(nc.vector.tensor_tensor(flat, flat, gred[:, :].unsqueeze(2).to_broadcast([P, NT * H, NG]), ALU.mult))
                    for t in range(NT):
                        last = nc.vector.tensor_tensor(gl[:, t, :, :], gl[:, t, :, :],
                                                       gscale[:, :].unsqueeze(2).to_broadcast([P, H, NG]), ALU.mult)
                    link(last)
                    for t in range(NT):
                        last = nc.vector.tensor_tensor(gl[:, t, :, :], gl[:, t, :, :],
                                                       geps[:, :].unsqueeze(2).to_broadcast([P, H, NG]), ALU.add)
                    last.then_inc(z["gate_sub"], 1)

                    def tap(f, k, j, first):
                        at = PAST - (TAPS["sml".index(f)] - 1) + j
                        v_in, acc, wj = cT["v"][:, k, at:at + L], facc[f][:, k, :], fir[f][:, k, j:j + 1]
                        if first:
                            return nc.vector.tensor_scalar(acc, v_in, wj, None, ALU.mult)
                        return nc.vector.scalar_tensor_tensor(acc, v_in, wj, acc, ALU.mult, ALU.add)

                    steps = [(f, j) for f in "sm" for j in range(TAPS["sml".index(f)])]
                    steps += [("l", j) for j in range(PE_TAPS, TAPS[2])]
                    done = [0]

                    def taps(count):
                        for _ in range(count):
                            if done[0] == len(steps):
                                return
                            f, j = steps[done[0]]
                            if (f, j) == ("l", PE_TAPS):
                                dve.wait_ge(z["firp_ready"], KD)
                            for k in range(KD):
                                last = tap(f, k, j, j == 0)
                            done[0] += 1
                            link(last)

                    taps(16)

                    def all_heads(a):
                        return a.unsqueeze(1).to_broadcast([P, H, P])

                    def bank(i):
                        return pb[i][:, :].rearrange("p (h j) -> p h j", h=H)

                    for t in range(NT):
                        dve.wait_ge(z["g_ps"], t + 1)
                        nc.vector.tensor_tensor(Tm[:, :, :], bank(0), all_heads(masks[:, 0, :]), ALU.mult)
                        link(nc.vector.tensor_tensor(TT[:, :, :], bank(1), all_heads(masks[:, 1, :]), ALU.mult))
                        nc.vector.tensor_tensor(Tm[:, :, :], Tm[:, :, :], all_heads(c.ident[:, :]), ALU.add)
                        nc.vector.tensor_tensor(TT[:, :, :], TT[:, :, :], all_heads(c.ident[:, :]), ALU.add)\
                            .then_inc(z["t_ready"], 1)
                        if t:
                            dve.wait_ge(z["do_ps"], t)
                        nc.vector.tensor_tensor(attnT[:, :, :], bank(2), all_heads(masks[:, 6, :]), ALU.mult)\
                            .then_inc(z["attn_ready"], 1)
                        for lv in range(LEVELS):
                            at = LEVELS * t + lv
                            dve.wait_ge(z["x_ps"], at + 1)
                            nc.vector.tensor_tensor(X[:, :, :], bank(0), all_heads(masks[:, 2 + lv, :]), ALU.mult)\
                                .then_inc(z["x_masked"], 1)
                            dve.wait_ge(z["tx_ps"], at + 1)
                            if lv < LEVELS - 1:
                                nc.vector.tensor_tensor(Tm[:, :, :], Tm[:, :, :], bank(1), ALU.subtract)
                            nc.vector.tensor_tensor(TT[:, :, :], TT[:, :, :], bank(2), ALU.subtract)\
                                .then_inc(z["t_ready"], 1)
                        for i in range(NC):
                            at = NC * t + i
                            lanes = slice(i * CH, (i + 1) * CH)
                            dve.wait_ge(z["ws_ps"], at + 1)
                            dve.wait_ge(z["uw_ready"], 2 * t + 2)
                            nc.vector.tensor_tensor(ua[lanes, :], u_t[lanes, :], pW[lanes, :], ALU.subtract)\
                                .then_inc(z["ua_ready"], 1)
                            taps(2 if i % 2 else 3)
                            dve.wait_ge(z["ks_ps"], at + 1)
                            if at == 0:
                                dve.wait_ge(z["s_zero"], 1)
                            nc.vector.tensor_tensor(S[:, :], S[:, :], pS, ALU.add).then_inc(z["s_ready"], 1)
                            taps(1)
                    taps(len(steps))
                    nc.vector.engine_nop().then_inc(z["fir_done"], 1)
                    first = True
                    for f in range(3):
                        for t2 in range(2):
                            at = 2 * f + t2
                            dve.wait_ge(z["fir_ps"], at + 1)
                            for t in (2 * t2, 2 * t2 + 1):
                                fp = pb[at % 2][:, (t % 2) * D:(t % 2 + 1) * D].rearrange("p (h d) -> p h d", d=DH)
                                last = nc.vector.tensor_tensor(sq[:, t, :].rearrange("p (h d) -> p h d", d=DH), fp,
                                                               gl[:, t, :, f:f + 1].to_broadcast([P, H, DH]), ALU.mult)
                            last.then_inc(z["fir_used"], 1)
                            if at == 0:
                                dve.wait_ge(z["o_ready"], 2)
                            dve.wait_ge(z["fir_used"], at + 1)
                            link(nc.vector.tensor_tensor(o[:, 2 * t2:2 * t2 + 2, :], o[:, 2 * t2:2 * t2 + 2, :],
                                                         sq[:, 2 * t2:2 * t2 + 2, :], ALU.add))
                    nc.vector.engine_nop().then_inc(z["o_ready"], 1)
                    dve.wait_ge(z["o_sq"], 1)
                    nc.vector.tensor_reduce(ss["o"][:, :], hd(sq), AX.X, ALU.add).then_inc(z["o_ss"], 1)
                    dve.wait_ge(z["o_ilen"], 2)
                    link(nc.vector.tensor_tensor(hd(o), hd(o), per_head(ss["o"][:, :]), ALU.mult))
                    nc.vector.tensor_tensor(hd(o), hd(o), norm_w[:, :].unsqueeze(1).to_broadcast([P, NT * H, DH]), ALU.mult)\
                        .then_inc(z["o_ready"], 1)
                    dve.wait_ge(z["y_ps"], 1)
                    norm_out_vector(nc, dve, n, link, lambda t: pY[:, t, :])

                @block.scalar
                def _(act):
                    norm_in_evacuate(nc, act, n, pb)
                    for i, s in enumerate("qkv"):
                        for k in range(KD):
                            act.wait_ge(z["proj_ps"], KD * i + k + 1)
                            nc.scalar.activation(xc[s][:, k, CONV - 1:], pb[2 + k][:, :], ACT.Copy).then_inc(z["xc_ready"], 1)
                    for i, s in enumerate("qkv"):
                        act.wait_ge(z["conv_ready"], i + 1)
                        for k in range(KD):
                            nc.scalar.activation(xc_silu(s, k), xc_out(s, k), ACT.Silu).then_inc(z["c_ready"], 1)
                    act.wait_ge(z["gate_ps"], 1)
                    gps = pb[5][:, 0:NT * (NG + 1) * H].rearrange("p (t x) -> p t x", t=NT)
                    nc.scalar.activation(beta[:, :, :], gps[:, :, H * NG:], ACT.Sigmoid).then_inc(z["beta_ready"], 1)
                    for i in range(6):
                        act.wait_ge(z["row_ps"], i + 1)
                        s, t2 = "qkv"[i // 2], i % 2
                        nc.scalar.activation(r[s][:, 2 * t2:2 * t2 + 2, :].rearrange("p t d -> p (t d)"),
                                             pb[i % 2][:, :], ACT.Copy).then_inc(z["row_ready"], 1)
                    for i, s in enumerate("qk"):
                        act.wait_ge(z["row_ready"], 2 * (i + 1))
                        if i:
                            act.wait_ge(z["ss_ready"], 1)
                        nc.scalar.activation(sq[:, :, :], r[s][:, :, :], ACT.Square).then_inc(z["sq_ready"], 1)
                    act.wait_ge(z["gate_sub"], 1)
                    nc.scalar.activation(gl[:, :, :, :], gl[:, :, :, :], ACT.Exp).then_inc(z["gate_exp"], 1)
                    for k in range(KD):
                        act.wait_ge(z["firp_ps"], k + 1)
                        nc.scalar.activation(facc["l"][:, k, :], pb[3 + k][:, :], ACT.Copy).then_inc(z["firp_ready"], 1)
                    for i in range(3 * H):
                        act.wait_ge(z["hT_ps"], i + 1)
                        nc.scalar.activation(hT[("q", "k", "kb")[i // H]][:, i % H, :], pb[i % 2][0:DH, :], ACT.Copy)\
                            .then_inc(z["hT_ready"], 1)
                    for t in range(NT):
                        act.wait_ge(z["g_ps"], t + 1)
                        nc.scalar.activation(GT[:, :, :].rearrange("p h j -> p (h j)"), pb[3][:, :], ACT.Copy)\
                            .then_inc(z["gt_ready"], 1)
                        act.wait_ge(z["uw_ps"], t + 1)
                        nc.scalar.activation(u_t[:, :], pb[3][:, 0:D], ACT.Copy).then_inc(z["uw_ready"], 1)
                        nc.scalar.activation(wT[:, :, :].rearrange("p h j -> p (h j)"), pb[4][0:DH, :], ACT.Copy)\
                            .then_inc(z["uw_ready"], 1)
                        act.wait_ge(z["do_ps"], t + 1)
                        nc.scalar.activation(do[:, t, :], pb[5][:, 0:D], ACT.Copy).then_inc(z["do_ready"], 1)
                    act.wait_ge(z["o_ready"], 3)
                    nc.scalar.activation(sq[:, :, :], o[:, :, :], ACT.Square).then_inc(z["o_sq"], 1)
                    for k in range(KD):
                        act.wait_ge(z["oT_ps"], k + 1)
                        nc.scalar.activation(oT[:, k, :], pb[k][:, :], ACT.Copy).then_inc(z["oT_ready"], 1)
                    norm_out_scalar(nc, act, n, lambda t: pY[:, t, :])

                @block.tensor
                def _(pe):
                    norm_in_tensor(nc, pe, n, pb, c.ident)
                    pe.wait_ge(n.xnT_ready, KD)
                    for i, s in enumerate("qkv"):
                        for m in range(KD):
                            if i:
                                pe.wait_ge(z["xc_ready"], KD * (i - 1) + m + 1)
                            for k in range(KD):
                                last = nc.tensor.matmul(pb[2 + m][:, :], wt[s][:, k, m * P:(m + 1) * P], n.xnT[:, k, :],
                                                        start=(k == 0), stop=(k == KD - 1))
                            last.then_inc(z["proj_ps"], 1)
                    NGH = H * (NG + 1)
                    for t in range(NT):
                        for k in range(KD):
                            last = nc.tensor.matmul(pb[5][:, t * NGH:(t + 1) * NGH], n.xnT[:, k, t * P:(t + 1) * P],
                                                    wg[:, k, :], start=(k == 0), stop=(k == KD - 1))
                    last.then_inc(z["gate_ps"], 1)
                    for i in range(6):
                        s, t2 = "qkv"[i // 2], i % 2
                        past = PAST if s == "v" else 0
                        pe.wait_ge(z["c_ready"], KD * (i // 2) + KD)
                        if i >= 2:
                            pe.wait_ge(z["row_ready"], i - 1)
                        for t in (2 * t2, 2 * t2 + 1):
                            for k in range(KD):
                                at = (t % 2) * D + k * P
                                last = nc.tensor.transpose(pb[i % 2][:, at:at + P],
                                                           cT[s][:, k, past + t * P:past + (t + 1) * P], c.ident[:, :])
                        last.then_inc(z["row_ps"], 1)
                    pe.wait_ge(z["xc_ready"], 3 * KD)
                    for k in range(KD):
                        for j in range(PE_TAPS):
                            last = nc.tensor.matmul(pb[3 + k][:, :], diag[:, k, j, :], cT["v"][:, k, j:j + L],
                                                    start=(j == 0), stop=(j == PE_TAPS - 1))
                        last.then_inc(z["firp_ps"], 1)
                    pe.wait_ge(z["row_ready"], 6)
                    for i in range(3 * H):
                        rows_of, done = ((r["q"], 1), (r["k"], 2), (kb, 3))[i // H]
                        pe.wait_ge(z["rows_ready"], done)
                        if i >= 2:
                            pe.wait_ge(z["hT_ready"], i - 1)
                        for t in range(NT):
                            last = nc.tensor.transpose(pb[i % 2][0:DH, t * P:(t + 1) * P],
                                                       rows_of[:, t, (i % H) * DH:(i % H + 1) * DH], c.ident[:, :])
                        last.then_inc(z["hT_ps"], 1)
                    pe.wait_ge(z["hT_ready"], 3 * H)
                    pe.wait_ge(z["firp_ready"], KD)
                    pe.wait_ge(z["rows_ready"], 4)
                    pe.wait_ge(z["s_zero"], 1)
                    pe.wait_ge(z["beta_ready"], 1)
                    pe.wait_ge(z["gate_sub"], 1)
                    for t in range(NT):
                        tok = slice(t * P, (t + 1) * P)
                        if t:
                            pe.wait_ge(z["uw_ready"], 2 * t)
                            pe.wait_ge(z["t_ready"], (LEVELS + 1) * t)
                        for h in range(H):
                            out = slice(h * P, (h + 1) * P)
                            q, k, kbh = (hT[s][:, h, tok] for s in ("q", "k", "kb"))
                            nc.tensor.matmul(pb[0][:, out], kbh, k, start=True, stop=True)
                            nc.tensor.matmul(pb[1][:, out], k, kbh, start=True, stop=True)
                            nc.tensor.matmul(pb[3][:, out], k, kbh, start=True, stop=True)
                            last = nc.tensor.matmul(pb[2][:, out], k, q, start=True, stop=True)
                        last.then_inc(z["g_ps"], 1)
                        pe.wait_ge(z["gt_ready"], t + 1)
                        pe.wait_ge(z["attn_ready"], t + 1)
                        for lv in range(LEVELS):
                            at = LEVELS * t + lv
                            pe.wait_ge(z["t_ready"], (LEVELS + 1) * t + lv + 1)
                            for h in range(H):
                                last = nc.tensor.matmul(pb[0][:, h * P:(h + 1) * P], GT[:, h, :], Tm[:, h, :],
                                                        start=True, stop=True)
                            last.then_inc(z["x_ps"], 1)
                            pe.wait_ge(z["x_masked"], at + 1)
                            for h in range(H):
                                if lv < LEVELS - 1:
                                    nc.tensor.matmul(pb[1][:, h * P:(h + 1) * P], TT[:, h, :], X[:, h, :],
                                                     start=True, stop=True)
                                last = nc.tensor.matmul(pb[2][:, h * P:(h + 1) * P], X[:, h, :], TT[:, h, :],
                                                        start=True, stop=True)
                            last.then_inc(z["tx_ps"], 1)
                        pe.wait_ge(z["t_ready"], (LEVELS + 1) * (t + 1))
                        for h in range(H):
                            cols = slice(h * DH, (h + 1) * DH)
                            nc.tensor.matmul(pb[3][:, cols], TT[:, h, :], vb[:, t, cols], start=True, stop=True)
                            last = nc.tensor.matmul(pb[4][0:DH, h * P:(h + 1) * P], kb[:, t, cols], TT[:, h, :],
                                                    start=True, stop=True)
                        last.then_inc(z["uw_ps"], 1)
                        pe.wait_ge(z["uw_ready"], 2 * t + 2)
                        for i in range(NC):
                            at = NC * t + i
                            lanes = slice(i * CH, (i + 1) * CH)
                            if at:
                                pe.wait_ge(z["s_ready"], at)
                            for h in range(H):
                                cols = slice(h * DH, (h + 1) * DH)
                                last = nc.tensor.matmul(pW[lanes, cols], wT[:, h, lanes], S[:, cols], start=True, stop=True)
                            last.then_inc(z["ws_ps"], 1)
                            if t and i == 0:
                                pe.wait_ge(z["do_ready"], t)
                            for h in range(H):
                                cols = slice(h * DH, (h + 1) * DH)
                                nc.tensor.matmul(pb[5][lanes, cols], hT["q"][:, h, t * P + i * CH:t * P + (i + 1) * CH],
                                                 S[:, cols], start=(h == 0), stop=False, skip_group_check=True)
                            pe.wait_ge(z["ua_ready"], at + 1)
                            for h in range(H):
                                cols = slice(h * DH, (h + 1) * DH)
                                last = nc.tensor.matmul(pS[:, cols], r["k"][lanes, t, cols], ua[lanes, cols],
                                                        start=True, stop=True)
                            last.then_inc(z["ks_ps"], 1)
                        for h in range(H):
                            cols = slice(h * DH, (h + 1) * DH)
                            last = nc.tensor.matmul(pb[5][:, cols], attnT[:, h, :], ua[:, cols], start=False, stop=True,
                                                    skip_group_check=True)
                        last.then_inc(z["do_ps"], 1)
                    pe.wait_ge(z["fir_done"], 1)
                    for i in range(6):
                        f, t2 = "sml"[i // 2], i % 2
                        if i >= 2:
                            pe.wait_ge(z["fir_used"], i - 1)
                        for t in (2 * t2, 2 * t2 + 1):
                            for k in range(KD):
                                at = (t % 2) * D + k * P
                                last = nc.tensor.transpose(pb[i % 2][:, at:at + P], facc[f][:, k, t * P:(t + 1) * P],
                                                           c.ident[:, :])
                        last.then_inc(z["fir_ps"], 1)
                    pe.wait_ge(z["o_ready"], 4)
                    for k in range(KD):
                        for t in range(NT):
                            last = nc.tensor.transpose(pb[k][:, t * P:(t + 1) * P], o[:, t, k * P:(k + 1) * P], c.ident[:, :])
                        last.then_inc(z["oT_ps"], 1)
                    pe.wait_ge(z["oT_ready"], KD)
                    pe.wait_ge(z["s_ready"], NT * NC)
                    for t in range(NT):
                        for k in range(KD):
                            last = nc.tensor.matmul(pY[:, t, :], oT[:, k, t * P:(t + 1) * P], wt["o"][:, k, :],
                                                    start=(k == 0), stop=(k == KD - 1))
                    last.then_inc(z["y_ps"], 1)

                @block.gpsimd
                def _(pool):
                    link = Chain(pool, z["pch"]).link
                    nc.gpsimd.memset(S[:, :], 0.0).then_inc(z["s_zero"], 1)
                    norm_in_pool(nc, pool, n, c)
                    for i, s in enumerate("qk"):
                        pool.wait_ge(z["ss_ready"], i + 1)
                        nc.gpsimd.tensor_scalar(ss[s][:, :], ss[s][:, :], 1e-6, None, ALU.add).then_inc(z["ilen_ready"], 1)
                        pool.wait_ge(z["ilen_ready"], 2 * i + 1)
                        nc.gpsimd.tensor_tensor(ss[s][:, :], ss[s][:, :], c.minus_half[:, 0:NT * H], ALU.pow)\
                            .then_inc(z["ilen_ready"], 1)
                    pool.wait_ge(z["gate_sub"], 2)
                    pool.wait_ge(z["do_ready"], NT)
                    pool.wait_ge(z["rows_ready"], 4)
                    for t in range(NT):
                        for a, g in ((do, 3), (r["v"], 4)):
                            a3 = a[:, t, :].rearrange("p (h d) -> p h d", d=DH)
                            out = o[:, t, :].rearrange("p (h d) -> p h d", d=DH) if g == 3 else a3
                            last = nc.gpsimd.tensor_tensor(out, a3, gl[:, t, :, g:g + 1].to_broadcast([P, H, DH]), ALU.mult)
                    last.then_inc(z["o_ready"], 1)
                    pool.wait_ge(z["o_ready"], 1)
                    nc.gpsimd.tensor_tensor(o[:, :, :], o[:, :, :], r["v"][:, :, :], ALU.add).then_inc(z["o_ready"], 1)
                    pool.wait_ge(z["o_ss"], 1)
                    nc.gpsimd.tensor_scalar(ss["o"][:, :], ss["o"][:, :], 1.0 / DH, 1e-5, ALU.mult, ALU.add)\
                        .then_inc(z["o_ilen"], 1)
                    pool.wait_ge(z["o_ilen"], 1)
                    nc.gpsimd.tensor_tensor(ss["o"][:, :], ss["o"][:, :], c.minus_half[:, 0:NT * H], ALU.pow)\
                        .then_inc(z["o_ilen"], 1)
                    norm_out_pool(nc, pool, n, c)
            sc.clear()


_TRANSPOSED = ("L2_ffn_w_gate", "L2_ffn_w_up", "L2_ffn_w_down", "L2_attn_Wq", "L2_attn_Wk", "L2_attn_Wv", "L2_attn_Wo",
               "L3_attn_W_in", "L3_attn_W_xproj", "L3_attn_W_dt", "L3_attn_W_out", "L1_ffn_Wr",
               "L0_attn_Wq", "L0_attn_Wk", "L0_attn_Wv", "L0_attn_Wo", "L0_attn_Wb", "L0_attn_gate_w")


def positions(tokens, d):
    pos = np.arange(tokens, dtype=np.float32)[None, :]
    freq = np.exp((-np.log(10000.0) * np.arange(0, d, 2) / d).astype(np.float32)).astype(np.float32)
    out = np.zeros((d, tokens), np.float32)
    out[0::2] = np.sin(freq[:, None] * pos)
    out[1::2] = np.cos(freq[:, None] * pos)
    return out


def chunk_masks(chunk):
    i, j = np.arange(P)[:, None], np.arange(P)[None, :]

    def lower(s):
        return ((i // (2 * s) == j // (2 * s)) & (i // s % 2 == 1) & (j // s % 2 == 0)).astype(np.float32)

    s, m = 2, [-lower(1), -lower(1).T]
    while s < chunk:
        m.append(lower(s))
        s *= 2
    m.append(((i // chunk == j // chunk) & (i <= j)).astype(np.float32))
    return np.ascontiguousarray(np.stack(m, 1))


def build(nc, w, out):
    ctx = ExitStack()
    with ctx:
        c = constants(nc, ctx)
        stages = {0: stage_delta, 1: stage_tanh_mlp, 2: stage_mqa, 3: stage_expert_choice, 4: stage_silu_mha, 5: stage_int_swiglu, 6: stage_mamba, 7: stage_moe_top2}
        res = nc.dram_tensor("residual", [NB, L, D], F32, kind="Internal").ap()
        src = w["L0_attn_hidden_states"]
        for s in STAGES:
            dst = out if s == STAGES[-1] else res
            stages[s](nc, w, src, dst, c)
            src = dst


def kernel(**inputs):
    import numpy as _np
    import concourse.bacc as _bacc
    from concourse import mybir as _mybir
    from concourse.bass_utils import run_bass_kernel_spmd as _run

    nc = _bacc.Bacc("TRN2", target_bir_lowering=False, num_devices=1)
    arrays, w = {}, {}
    for name, v in inputs.items():
        a = _np.asarray(v)
        if name in _TRANSPOSED:
            a = _np.swapaxes(a, -1, -2)
        a = _np.ascontiguousarray(a)
        arrays["in_" + name] = a
        w[name] = nc.dram_tensor("in_" + name, a.shape, _mybir.dt.from_np(a.dtype), kind="ExternalInput").ap()
    constants_of_shapes = {"positions": positions(L, P), "chunk_masks": chunk_masks(32)}
    for name, a in constants_of_shapes.items():
        arrays[name] = a
        w[name] = nc.dram_tensor(name, a.shape, _mybir.dt.float32, kind="ExternalInput").ap()
    out = nc.dram_tensor("out_0", (NB, L, D), _mybir.dt.float32, kind="ExternalOutput").ap()
    build(nc, w, out)
    r = _run(nc, [arrays], core_ids=[0])
    return r.results[0]["out_0"]
```

```python
from contextlib import ExitStack

import numpy as np

import concourse.bass as bass
from concourse import mybir

P = 128
NB = 8
L = 512
D = 256
NT = L // P
KD = D // P
EPS = 1e-5
MASKED = -1e30

ALU = mybir.AluOpType
ACT = mybir.ActivationFunctionType
AX = mybir.AxisListType
F32 = mybir.dt.float32
I32 = mybir.dt.int32
U32 = mybir.dt.uint32
BF16 = mybir.dt.bfloat16

STAGES = (0, 1, 2, 3, 4, 5, 6, 7)


class Scope:

    def __init__(self, nc, stage):
        self.nc, self.stage, self.ctx, self.sems = nc, stage, ExitStack(), []

    def __enter__(self):
        self.ctx.__enter__()
        return self

    def __exit__(self, *a):
        return self.ctx.__exit__(*a)

    def sb(self, name, shape, dt=F32):
        return self.ctx.enter_context(self.nc.sbuf_tensor(f"{self.stage}_{name}", shape, dt))

    def ps(self, name, shape, dt=F32):
        return self.ctx.enter_context(self.nc.psum_tensor(f"{self.stage}_{name}", shape, dt))

    def sem(self, name):
        s = self.ctx.enter_context(self.nc.semaphore(f"{self.stage}_{name}"))
        self.sems.append(s)
        return s

    def clear(self):
        for s in self.sems:
            self.nc.sync.sem_clear(s)
        self.nc.all_engine_barrier(sem_only=True)


class Chain:

    def __init__(self, eng, sem):
        self.eng, self.sem, self.n = eng, sem, 0

    def link(self, ins):
        self.n += 1
        ins.then_inc(self.sem, 1)
        self.eng.wait_ge(self.sem, self.n)


class Norm:

    def __init__(self, sc):
        self.x = sc.sb("x", [P, NT, D])
        self.xr = sc.sb("xr", [P, NT, D])
        self.xn = sc.sb("xn", [P, NT, D])
        self.xnT = sc.sb("xnT", [P, KD, L])
        self.stat = sc.sb("stat", [P, NT, 6])
        self.mv = sc.sb("mv", [P, NT, 2])
        self.rstd = sc.sb("rstd", [P, NT])
        self.ystat = sc.sb("ystat", [P, NT, 6])
        self.ymv = sc.sb("ymv", [P, NT, 2])
        self.yrstd = sc.sb("yrstd", [P, NT])
        self.ynm = sc.sb("ynm", [P, NT])
        self.yn = sc.sb("yn", [P, NT, D])
        self.x_in = sc.sem("x_in")
        self.xr_in = sc.sem("xr_in")
        self.var_ready = sc.sem("var_ready")
        self.rstd_ready = sc.sem("rstd_ready")
        self.xn_ready = sc.sem("xn_ready")
        self.xnT_ready = sc.sem("xnT_ready")
        self.y_var_ready = sc.sem("y_var_ready")
        self.y_scale_ready = sc.sem("y_scale_ready")
        self.yn_ready = sc.sem("yn_ready")
        self.x_out = sc.sem("x_out")
        self.x_stored = sc.sem("x_stored")
        self.xT_ps_ready = sc.sem("xT_ps_ready")


def rows(x):
    return x.rearrange("b (t p) d -> b p t d", p=P)


def norm_in_vector(nc, dve, n, link):
    dve.wait_ge(n.x_in, 16)
    for t in range(NT):
        last = nc.vector.bn_stats(n.stat[:, t, :], n.x[:, t, :])
    link(last)
    for t in range(NT):
        last = nc.vector.bn_aggr(n.mv[:, t, :], n.stat[:, t, :])
    last.then_inc(n.var_ready, 1)
    dve.wait_ge(n.rstd_ready, 2)
    for t in range(NT):
        nc.vector.tensor_scalar(n.xn[:, t, :], n.x[:, t, :], n.mv[:, t, 0:1], n.rstd[:, t:t + 1],
                                ALU.subtract, ALU.mult).then_inc(n.xn_ready, 1)


def norm_in_pool(nc, pool, n, eps):
    pool.wait_ge(n.var_ready, 1)
    nc.gpsimd.tensor_scalar(n.rstd[:, :], n.mv[:, :, 1], EPS, None, ALU.add).then_inc(n.rstd_ready, 1)
    pool.wait_ge(n.rstd_ready, 1)
    nc.gpsimd.tensor_tensor(n.rstd[:, :], n.rstd[:, :], eps.minus_half[:, 0:NT], ALU.pow).then_inc(n.rstd_ready, 1)


def norm_in_tensor(nc, pe, n, xT_ps, ident):
    for t in range(NT):
        pe.wait_ge(n.xn_ready, t + 1)
        for k in range(KD):
            last = nc.tensor.transpose(xT_ps[k][:, t * P:(t + 1) * P], n.xn[:, t, k * P:(k + 1) * P], ident[:, :])
    last.then_inc(n.xT_ps_ready, 1)


def norm_in_evacuate(nc, act, n, xT_ps):
    act.wait_ge(n.xT_ps_ready, 1)
    for k in range(KD):
        nc.scalar.activation(n.xnT[:, k, :], xT_ps[k][:, :], ACT.Copy).then_inc(n.xnT_ready, 1)


def norm_out_vector(nc, dve, n, link, y):
    for t in range(NT):
        last = nc.vector.bn_stats(n.ystat[:, t, :], y(t))
    link(last)
    for t in range(NT):
        last = nc.vector.bn_aggr(n.ymv[:, t, :], n.ystat[:, t, :])
    last.then_inc(n.y_var_ready, 1)


def norm_out_scalar(nc, act, n, y):
    act.wait_ge(n.y_scale_ready, 3)
    for t in range(NT):
        nc.scalar.activation(n.yn[:, t, :], y(t), ACT.Identity, bias=n.ynm[:, t:t + 1],
                             scale=n.yrstd[:, t:t + 1]).then_inc(n.yn_ready, 1)


def norm_out_pool(nc, pool, n, eps):
    pool.wait_ge(n.y_var_ready, 1)
    nc.gpsimd.tensor_scalar(n.yrstd[:, :], n.ymv[:, :, 1], EPS, None, ALU.add)
    nc.gpsimd.tensor_scalar(n.ynm[:, :], n.ymv[:, :, 0], -1.0, None, ALU.mult).then_inc(n.y_scale_ready, 1)
    pool.wait_ge(n.y_scale_ready, 1)
    nc.gpsimd.tensor_tensor(n.yrstd[:, :], n.yrstd[:, :], eps.minus_half[:, 0:NT], ALU.pow)\
        .then_inc(n.y_scale_ready, 1)
    pool.wait_ge(n.y_scale_ready, 2)
    nc.gpsimd.tensor_tensor(n.ynm[:, :], n.ynm[:, :], n.yrstd[:, :], ALU.mult).then_inc(n.y_scale_ready, 1)
    pool.wait_ge(n.xr_in, 16)
    for t in range(NT):
        pool.wait_ge(n.yn_ready, t + 1)
        nc.gpsimd.tensor_tensor(n.yn[:, t, :], n.yn[:, t, :], n.xr[:, t, :], ALU.add).then_inc(n.x_out, 1)


def norm_out_store(sp, n, dst, b):
    sp.wait_ge(n.x_out, NT)
    sp.dma_start(rows(dst)[b], n.yn[:, :, :]).then_inc(n.x_stored, 16)
    sp.wait_ge(n.x_stored, 16)


def load_rows(sp, n, src, b):
    sp.dma_start(n.xr[:, :, :], rows(src)[(b + NB - 1) & (NB - 1)]).then_inc(n.xr_in, 16)
    sp.dma_start(n.x[:, :, :], rows(src)[(b + 1) & (NB - 1)]).then_inc(n.x_in, 16)


def last_norm(nc, sc, n, src, dst, c, y, dch):
    with nc.Block() as block:
        @block.sync
        def _(sp):
            sp.dma_start(n.xr[:, :, :], rows(src)[NB - 1]).then_inc(n.xr_in, 16)
            norm_out_store(sp, n, dst, NB - 1)

        @block.vector
        def _(dve):
            norm_out_vector(nc, dve, n, Chain(dve, dch).link, y)

        @block.scalar
        def _(act):
            norm_out_scalar(nc, act, n, y)

        @block.gpsimd
        def _(pool):
            norm_out_pool(nc, pool, n, c)
    sc.clear()


def first_norm(nc, sc, n, src, c, xT_ps, dch, y):
    with nc.Block() as block:
        @block.sync
        def _(sp):
            sp.dma_start(n.x[:, :, :], rows(src)[0]).then_inc(n.x_in, 16)

        @block.vector
        def _(dve):
            link = Chain(dve, dch).link
            for t in range(NT):
                last = nc.vector.memset(y(t), 0.0)
            link(last)
            norm_in_vector(nc, dve, n, link)

        @block.gpsimd
        def _(pool):
            norm_in_pool(nc, pool, n, c)

        @block.tensor
        def _(pe):
            norm_in_tensor(nc, pe, n, xT_ps, c.ident)

        @block.scalar
        def _(act):
            norm_in_evacuate(nc, act, n, xT_ps)
    sc.clear()


class Consts:
    pass


def constants(nc, ctx):
    c = Consts()
    c.ident = ctx.enter_context(nc.sbuf_tensor("ident", [P, P], F32))
    c.minus_half = ctx.enter_context(nc.sbuf_tensor("minus_half", [P, 64], F32))
    c.ident16 = ctx.enter_context(nc.sbuf_tensor("ident16", [P, P], BF16))
    c.causal16 = ctx.enter_context(nc.sbuf_tensor("causal16", [P, P], BF16))
    c.causal16T = ctx.enter_context(nc.sbuf_tensor("causal16T", [P, P], BF16))
    c.gathered = ctx.enter_context(nc.semaphore("gathered"))
    c.added = ctx.enter_context(nc.semaphore("added"))
    c.iota8 = ctx.enter_context(nc.sbuf_tensor("iota8", [P, 8], F32))
    const_done = ctx.enter_context(nc.semaphore("const_done"))
    with nc.Block() as block:
        @block.gpsimd
        def _(pool):
            nc.gpsimd.memset(c.ident[:, :], 0.0)
            nc.gpsimd.memset(c.ident16[:, :], 0.0)
            nc.gpsimd.memset(c.causal16[:, :], 0.0)
            nc.gpsimd.memset(c.causal16T[:, :], 0.0)
            nc.gpsimd.iota(c.iota8[:, :], [[1, 8]], base=0, channel_multiplier=0,
                           allow_small_or_imprecise_dtypes=True)
            nc.gpsimd.memset(c.minus_half[:, :], -0.5).then_inc(const_done, 1)
            pool.wait_ge(const_done, 1)
            for ident in (c.ident, c.ident16):
                nc.gpsimd.affine_select(out=ident[:, :], in_=ident[:, :], compare_op=ALU.not_equal, fill=1.0,
                                        base=0, pattern=[[-1, P]], channel_multiplier=1).then_inc(const_done, 1)
            nc.gpsimd.affine_select(out=c.causal16[:, :], in_=c.causal16[:, :], compare_op=ALU.is_ge, fill=MASKED,
                                    base=0, pattern=[[-1, P]], channel_multiplier=1).then_inc(const_done, 1)
            nc.gpsimd.affine_select(out=c.causal16T[:, :], in_=c.causal16T[:, :], compare_op=ALU.is_ge, fill=MASKED,
                                    base=0, pattern=[[1, P]], channel_multiplier=-1).then_inc(const_done, 1)
            pool.wait_ge(const_done, 5)
    return c


def stage_tanh_mlp(nc, w, src, dst, c):
    with Scope(nc, "mlp") as sc:
        n = Norm(sc)
        wt = [sc.sb(f"w{i}", [P, KD, D]) for i in range(3)]
        bias = sc.sb("bias", [P, D])
        hT = [sc.sb(f"hT{i}", [P, KD, L]) for i in range(2)]
        y = sc.sb("y", [P, NT, D])
        pA = [sc.ps(f"pA{k}", [P, L]) for k in range(KD)]
        pB = [sc.ps(f"pB{k}", [P, L]) for k in range(KD)]
        pY = sc.ps("pY", [P, NT, D])
        w_in = sc.sem("w_in")
        with nc.Block() as block:
            @block.sync
            def _(sp):
                for i, name in enumerate(("L0_ffn_weight", "L0_ffn_aux_weight1", "L0_ffn_aux_weight2")):
                    sp.dma_start(wt[i][:, :, :], w[name].rearrange("(k p) d -> p k d", p=P)).then_inc(w_in, 16)
                sp.dma_start(bias[:, :], w["L0_ffn_bias"][None, :].to_broadcast([P, D])).then_inc(w_in, 16)
                sp.wait_ge(w_in, 64)
        h_ps = sc.sem("h_ps")
        h_ready = sc.sem("h_ready")
        yb_ready = sc.sem("yb_ready")
        y_ready = sc.sem("y_ready")
        dch = sc.sem("dch")
        first_norm(nc, sc, n, src, c, pA, dch, lambda t: y[:, t, :])
        with nc.Fori(0, NB) as b:
            with nc.Block() as block:
                @block.sync
                def _(sp):
                    load_rows(sp, n, src, b)
                    norm_out_store(sp, n, dst, (b + NB - 1) & (NB - 1))

                @block.vector
                def _(dve):
                    link = Chain(dve, dch).link
                    norm_out_vector(nc, dve, n, link, lambda t: y[:, t, :])
                    norm_in_vector(nc, dve, n, link)
                    dve.wait_ge(h_ps, 3)
                    dve.wait_ge(n.yn_ready, NT)
                    for t in range(NT):
                        nc.vector.tensor_tensor(y[:, t, :], pY[:, t, :], bias[:, :], ALU.add).then_inc(yb_ready, 1)

                @block.scalar
                def _(act):
                    for i, ps in enumerate((pB, pA)):
                        act.wait_ge(h_ps, i + 1)
                        for k in range(KD):
                            nc.scalar.activation(hT[i][:, k, :], ps[k][:, :], ACT.Copy).then_inc(h_ready, 1)
                    norm_out_scalar(nc, act, n, lambda t: y[:, t, :])
                    act.wait_ge(yb_ready, NT)
                    nc.scalar.activation(y[:, :, :], y[:, :, :], ACT.Tanh).then_inc(y_ready, 1)
                    norm_in_evacuate(nc, act, n, pA)

                @block.tensor
                def _(pe):
                    for i, (a, ps) in enumerate(((n.xnT, pB), (hT[0], pA))):
                        if i == 1:
                            pe.wait_ge(h_ready, KD)
                        for m in range(KD):
                            for k in range(KD):
                                last = nc.tensor.matmul(ps[m][:, :], wt[i][:, k, m * P:(m + 1) * P], a[:, k, :],
                                                        start=(k == 0), stop=(k == KD - 1))
                        last.then_inc(h_ps, 1)
                    pe.wait_ge(h_ready, 2 * KD)
                    for t in range(NT):
                        for k in range(KD):
                            last = nc.tensor.matmul(pY[:, t, :], hT[1][:, k, t * P:(t + 1) * P], wt[2][:, k, :],
                                                    start=(k == 0), stop=(k == KD - 1))
                    last.then_inc(h_ps, 1)
                    norm_in_tensor(nc, pe, n, pA, c.ident)

                @block.gpsimd
                def _(pool):
                    norm_out_pool(nc, pool, n, c)
                    norm_in_pool(nc, pool, n, c)
            sc.clear()
        last_norm(nc, sc, n, src, dst, c, lambda t: y[:, t, :], dch)


def stage_int_swiglu(nc, w, src, dst, c):
    H = w["L2_ffn_w_gate"].shape[1]
    JH = H // P
    scale = float(np.float32(1.0 / 127.0))
    with Scope(nc, "isw") as sc:
        n = Norm(sc)
        raw = sc.sb("raw", [P, KD * H], I32)
        wg = sc.sb("wg", [P, KD, H])
        wu = sc.sb("wu", [P, KD, H])
        wd = sc.sb("wd", [P, JH, D])
        g = sc.sb("g", [P, 2, L])
        hT = sc.sb("hT", [P, JH, L])
        pX = [sc.ps(f"pX{k}", [P, L]) for k in range(KD)]
        pG = [sc.ps(f"pG{k}", [P, L]) for k in range(2)]
        pU = [sc.ps(f"pU{k}", [P, L]) for k in range(2)]
        pY = sc.ps("pY", [P, NT, D])
        w_in, w_ready = sc.sem("w_in"), sc.sem("w_ready")
        gu_ps, g_ready, h_ready, y_ps, dch = (sc.sem(s) for s in ("gu_ps", "g_ready", "h_ready", "y_ps", "dch"))
        sources = ((wg, w["L2_ffn_w_gate"]), (wu, w["L2_ffn_w_up"]), (wd, w["L2_ffn_w_down"]))
        with nc.Block() as block:
            @block.sync
            def _(sp):
                for i, (t, a) in enumerate(sources):
                    if i:
                        sp.wait_ge(w_ready, i)
                    sp.dma_start(raw[:, :].rearrange("p (k d) -> p k d", d=a.shape[1]),
                                 a.rearrange("(k p) d -> p k d", p=P)).then_inc(w_in, 16)

            @block.vector
            def _(dve):
                for i, (t, a) in enumerate(sources):
                    dve.wait_ge(w_in, 16 * (i + 1))
                    nc.vector.tensor_scalar(t[:, :, :].rearrange("p k d -> p (k d)"), raw[:, :], scale, None,
                                            ALU.mult).then_inc(w_ready, 1)
                dve.wait_ge(w_ready, 3)
        sc.clear()
        first_norm(nc, sc, n, src, c, pX, dch, lambda t: pY[:, t, :])
        with nc.Fori(0, NB) as b:
            with nc.Block() as block:
                @block.sync
                def _(sp):
                    load_rows(sp, n, src, b)
                    norm_out_store(sp, n, dst, (b + NB - 1) & (NB - 1))

                @block.vector
                def _(dve):
                    link = Chain(dve, dch).link
                    norm_out_vector(nc, dve, n, link, lambda t: pY[:, t, :])
                    for j in range(JH):
                        dve.wait_ge(g_ready, j + 1)
                        nc.vector.tensor_tensor(hT[:, j, :], g[:, j % 2, :], pU[j % 2][:, :], ALU.mult)\
                            .then_inc(h_ready, 1)
                    norm_in_vector(nc, dve, n, link)

                @block.scalar
                def _(act):
                    norm_out_scalar(nc, act, n, lambda t: pY[:, t, :])
                    for j in range(JH):
                        act.wait_ge(gu_ps, j + 1)
                        if j >= 2:
                            act.wait_ge(h_ready, j - 1)
                        nc.scalar.activation(g[:, j % 2, :], pG[j % 2][:, :], ACT.Silu).then_inc(g_ready, 1)
                    norm_in_evacuate(nc, act, n, pX)

                @block.tensor
                def _(pe):

                    def down(j):
                        if j == 0:
                            pe.wait_ge(n.yn_ready, NT)
                        pe.wait_ge(h_ready, j + 1)
                        for t in range(NT):
                            last = nc.tensor.matmul(pY[:, t, :], hT[:, j, t * P:(t + 1) * P], wd[:, j, :],
                                                    start=(j == 0 and t % 2 == 0), stop=(j == JH - 1),
                                                    skip_group_check=True)
                        return last

                    for j in range(JH):
                        if j >= 2:
                            pe.wait_ge(h_ready, j - 1)
                        for wt, ps in ((wg, pG), (wu, pU)):
                            for k in range(KD):
                                last = nc.tensor.matmul(ps[j % 2][:, :], wt[:, k, j * P:(j + 1) * P], n.xnT[:, k, :],
                                                        start=(k == 0), stop=(k == KD - 1))
                        last.then_inc(gu_ps, 1)
                        if j >= 1:
                            down(j - 1)
                    down(JH - 1).then_inc(y_ps, 1)
                    norm_in_tensor(nc, pe, n, pX, c.ident)

                @block.gpsimd
                def _(pool):
                    norm_out_pool(nc, pool, n, c)
                    norm_in_pool(nc, pool, n, c)
            sc.clear()
        last_norm(nc, sc, n, src, dst, c, lambda t: pY[:, t, :], dch)


def stage_moe_top2(nc, w, src, dst, c):
    E, H = w["L3_ffn_w1"].shape[0], w["L3_ffn_w1"].shape[2]
    TOP = 2
    JH = H // P
    NE = E + 1
    units = [(e, j) for e in range(NE) for j in range(JH)]
    with Scope(nc, "top2") as sc:
        n = Norm(sc)
        w1 = sc.sb("w1", [P, NE * KD, H])
        w3 = sc.sb("w3", [P, NE * KD, H])
        w2 = sc.sb("w2", [P, NE * JH, D])
        wr = sc.sb("wr", [P, KD, E])
        g = sc.sb("g", [P, 2, L])
        hT = sc.sb("hT", [P, 2, L])
        acc = sc.sb("acc", [P, NT, D])
        sub = sc.sb("sub", [P, NT, E])
        prob = sc.sb("prob", [P, NT, E])
        best = sc.sb("best", [P, NT, 8])
        best_i = sc.sb("best_i", [P, NT, 8], U32)
        best_f = sc.sb("best_f", [P, NT, 8])
        cw = sc.sb("cw", [P, NT, E])
        red = sc.sb("red", [P, NT])
        pG = [sc.ps(f"pG{k}", [P, L]) for k in range(2)]
        pU = [sc.ps(f"pU{k}", [P, L]) for k in range(2)]
        pY = [sc.ps(f"pY{k}", [P, NT, D]) for k in range(2)]
        pX = pU
        pR = pG[0][:, 0:NT * E].rearrange("p (t e) -> p t e", e=E)
        w_in = sc.sem("w_in")
        gu_ps, g_ready, h_ready, y_ps, dch, r_ps, sub_ready, exp_ready, acc_ready = (
            sc.sem(s) for s in ("gu_ps", "g_ready", "h_ready", "y_ps", "dch", "r_ps", "sub_ready", "exp_ready",
                                "acc_ready"))
        with nc.Block() as block:
            @block.sync
            def _(sp):
                sp.dma_start(wr[:, :, :], w["L3_ffn_w_router"].rearrange("(k p) e -> p k e", p=P)).then_inc(w_in, 16)
                for t, many, one, k in ((w1, "L3_ffn_w1", "L3_ffn_ws1", KD), (w3, "L3_ffn_w3", "L3_ffn_ws3", KD),
                                        (w2, "L3_ffn_w2", "L3_ffn_ws2", JH)):
                    for e in range(E):
                        sp.dma_start(t[:, e * k:(e + 1) * k, :],
                                     w[many][e].rearrange("(k p) h -> p k h", p=P)).then_inc(w_in, 16)
                    sp.dma_start(t[:, E * k:, :], w[one].rearrange("(k p) h -> p k h", p=P)).then_inc(w_in, 16)
                sp.wait_ge(w_in, 16 * (3 * NE + 1))
        first_norm(nc, sc, n, src, c, pX, dch, lambda t: acc[:, t, :])
        with nc.Fori(0, NB) as b:
            with nc.Block() as block:
                @block.sync
                def _(sp):
                    load_rows(sp, n, src, b)
                    norm_out_store(sp, n, dst, (b + NB - 1) & (NB - 1))

                @block.vector
                def _(dve):
                    link = Chain(dve, dch).link
                    norm_out_vector(nc, dve, n, link, lambda t: acc[:, t, :])
                    dve.wait_ge(r_ps, 1)
                    link(nc.vector.tensor_reduce(red[:, :], pR, AX.X, ALU.max))
                    nc.vector.tensor_tensor(sub[:, :, :], pR, red[:, :].unsqueeze(2).to_broadcast([P, NT, E]),
                                            ALU.subtract).then_inc(sub_ready, 1)
                    dve.wait_ge(exp_ready, 1)
                    link(nc.vector.tensor_reduce(red[:, :], sub[:, :, :], AX.X, ALU.add))
                    link(nc.vector.reciprocal(red[:, :], red[:, :]))
                    link(nc.vector.tensor_tensor(prob[:, :, :], sub[:, :, :],
                                                 red[:, :].unsqueeze(2).to_broadcast([P, NT, E]), ALU.mult))
                    for t in range(NT):
                        last = nc.vector.max(best[:, t, :], prob[:, t, :])
                    link(last)
                    for t in range(NT):
                        last = nc.vector.max_index(best_i[:, t, :], best[:, t, :], prob[:, t, :])
                    link(last)
                    link(nc.vector.tensor_copy(best_f[:, :, :], best_i[:, :, :]))
                    for t in range(NT):
                        last = nc.vector.tensor_scalar(cw[:, t, :], c.iota8[:, :], best_f[:, t, 0:1], None, ALU.is_equal)
                    link(last)
                    for t in range(NT):
                        last = nc.vector.scalar_tensor_tensor(cw[:, t, :], c.iota8[:, :], best_f[:, t, 1:2], cw[:, t, :],
                                                              ALU.is_equal, ALU.add)
                    link(last)
                    link(nc.vector.scalar_tensor_tensor(cw[:, :, :], prob[:, :, :], TOP / (TOP + 1.0), cw[:, :, :],
                                                        ALU.mult, ALU.mult))

                    def add_expert(e):
                        dve.wait_ge(y_ps, e + 1)
                        if e == 0:
                            dve.wait_ge(n.yn_ready, NT)
                        if e:
                            dve.wait_ge(acc_ready, e)
                        for t in range(NT):
                            if e == 0:
                                last = nc.vector.tensor_scalar(acc[:, t, :], pY[0][:, t, :], cw[:, t, 0:1], None,
                                                               ALU.mult)
                            else:
                                weight = cw[:, t, e:e + 1] if e < E else 1.0 / (TOP + 1.0)
                                last = nc.vector.scalar_tensor_tensor(acc[:, t, :], pY[e % 2][:, t, :], weight,
                                                                      acc[:, t, :], ALU.mult, ALU.add)
                        last.then_inc(acc_ready, 1)

                    for u, (e, j) in enumerate(units):
                        dve.wait_ge(g_ready, u + 1)
                        if u >= 2:
                            dve.wait_ge(gu_ps, u + 1)
                        nc.vector.tensor_tensor(hT[:, u % 2, :], g[:, u % 2, :], pU[u % 2][:, :], ALU.mult)\
                            .then_inc(h_ready, 1)
                        if j == 1 and e >= 1:
                            add_expert(e - 1)
                    norm_in_vector(nc, dve, n, link)
                    add_expert(E)
                    dve.wait_ge(acc_ready, NE)

                @block.scalar
                def _(act):
                    act.wait_ge(sub_ready, 1)
                    nc.scalar.activation(sub[:, :, :], sub[:, :, :], ACT.Exp).then_inc(exp_ready, 1)
                    norm_out_scalar(nc, act, n, lambda t: acc[:, t, :])
                    for u in range(len(units)):
                        act.wait_ge(gu_ps, u + 1)
                        if u >= 2:
                            act.wait_ge(h_ready, u - 1)
                        nc.scalar.activation(g[:, u % 2, :], pG[u % 2][:, :], ACT.Silu).then_inc(g_ready, 1)
                    norm_in_evacuate(nc, act, n, pX)

                @block.tensor
                def _(pe):
                    for t in range(NT):
                        for k in range(KD):
                            last = nc.tensor.matmul(pR[:, t, :], n.xnT[:, k, t * P:(t + 1) * P], wr[:, k, :],
                                                    start=(k == 0), stop=(k == KD - 1))
                    last.then_inc(r_ps, 1)

                    def down(u):
                        e, j = units[u]
                        pe.wait_ge(h_ready, u + 1)
                        if j == 0 and e >= 2:
                            pe.wait_ge(acc_ready, e - 1)
                        for t in range(NT):
                            last = nc.tensor.matmul(pY[e % 2][:, t, :], hT[:, u % 2, t * P:(t + 1) * P],
                                                    w2[:, e * JH + j, :], start=(j == 0 and t % 2 == 0),
                                                    stop=(j == JH - 1), skip_group_check=True)
                        if j == JH - 1:
                            last.then_inc(y_ps, 1)

                    for u, (e, j) in enumerate(units):
                        if u == 0:
                            pe.wait_ge(sub_ready, 1)
                        if u >= 2:
                            pe.wait_ge(h_ready, u - 1)
                        for wt, ps in ((w1, pG), (w3, pU)):
                            for k in range(KD):
                                last = nc.tensor.matmul(ps[u % 2][:, :], wt[:, e * KD + k, j * P:(j + 1) * P],
                                                        n.xnT[:, k, :], start=(k == 0), stop=(k == KD - 1))
                        last.then_inc(gu_ps, 1)
                        if u >= 1:
                            down(u - 1)
                    down(len(units) - 1)
                    norm_in_tensor(nc, pe, n, pX, c.ident)

                @block.gpsimd
                def _(pool):
                    norm_out_pool(nc, pool, n, c)
                    norm_in_pool(nc, pool, n, c)
            sc.clear()
        last_norm(nc, sc, n, src, dst, c, lambda t: acc[:, t, :], dch)


def stage_mqa(nc, w, src, dst, c):
    DH = w["L1_attn_Wkv"].shape[1] // 2
    H = w["L1_attn_Wq"].shape[1] // DH
    SCALE = float(np.float32(1.0 / np.sqrt(DH)))
    units = [(h, q) for h in range(H) for q in range(NT)]
    with Scope(nc, "mqa") as sc:
        n = Norm(sc)
        wq = sc.sb("wq", [P, KD, H * DH])
        wkv = sc.sb("wkv", [P, KD, 2 * DH])
        wo = sc.sb("wo", [P, H, D])
        bq = sc.sb("bq", [P, H])
        bk = sc.sb("bk", [P, 1])
        bv = sc.sb("bv", [P, DH])
        peT = sc.sb("peT", [P, L])
        qT = sc.sb("qT", [P, H, L])
        kT = sc.sb("kT", [P, L])
        v = sc.sb("v", [P, NT, DH])
        prob = sc.sb("prob", [P, 3, L])
        probT = sc.sb("probT", [P, 2, NT, L])
        oT = sc.sb("oT", [P, H, L])
        nmax = sc.sb("nmax", [P, len(units)])
        rsum = sc.sb("rsum", [P, len(units)])
        rinv = sc.sb("rinv", [P, len(units)])
        pS = [sc.ps(f"pS{k}", [P, L]) for k in range(2)]
        pT = [sc.ps(f"pT{k}", [P, L]) for k in range(2)]
        pO = [sc.ps(f"pO{k}", [P, L]) for k in range(2)]
        pY = sc.ps("pY", [P, NT, D])
        w_in = sc.sem("w_in")
        (proj_ps, proj_used, k_sum, s_ps, max_ready, exp_ready, inv_ready, prob_ready, t_ps, t_used, o_ps, o_used, y_ps,
         dch) = (sc.sem(s) for s in ("proj_ps", "proj_used", "k_sum", "s_ps", "max_ready", "exp_ready", "inv_ready",
                                     "prob_ready", "t_ps", "t_used", "o_ps", "o_used", "y_ps", "dch"))
        with nc.Block() as block:
            @block.sync
            def _(sp):
                sp.dma_start(wq[:, :, :], w["L1_attn_Wq"].rearrange("(k p) d -> p k d", p=P)).then_inc(w_in, 16)
                sp.dma_start(wkv[:, :, :], w["L1_attn_Wkv"].rearrange("(k p) d -> p k d", p=P)).then_inc(w_in, 16)
                sp.dma_start(wo[:, :, :], w["L1_attn_Wo"].rearrange("(h p) d -> p h d", p=P)).then_inc(w_in, 16)
                with nc.allow_non_contiguous_dma(reason="biases, a few values each"):
                    sp.dma_start(bq[:, :], w["L1_attn_bq"].rearrange("(h p) -> p h", p=P)).then_inc(w_in, 16)
                    sp.dma_start(bk[:, :], w["L1_attn_bkv"].rearrange("(a p) -> p a", p=P)[:, 0:1]).then_inc(w_in, 16)
                sp.dma_start(bv[:, :], w["L1_attn_bkv"][None, DH:].to_broadcast([P, DH])).then_inc(w_in, 16)
                sp.dma_start(peT[:, :], w["positions"]).then_inc(w_in, 16)
                sp.wait_ge(w_in, 16 * 7)
        first_norm(nc, sc, n, src, c, pT, dch, lambda t: pY[:, t, :])
        with nc.Fori(0, NB) as b:
            with nc.Block() as block:
                @block.sync
                def _(sp):
                    load_rows(sp, n, src, b)
                    norm_out_store(sp, n, dst, (b + NB - 1) & (NB - 1))

                @block.vector
                def _(dve):
                    link = Chain(dve, dch).link
                    norm_out_vector(nc, dve, n, link, lambda t: pY[:, t, :])
                    for i in range(H + 1):
                        dve.wait_ge(proj_ps, i + 1)
                        out, bias = (kT[:, :], bk[:, 0:1]) if i == 0 else (qT[:, i - 1, :], bq[:, i - 1:i])
                        nc.vector.scalar_tensor_tensor(out, pO[i % 2][:, :], bias, peT[:, :], ALU.add, ALU.add)\
                            .then_inc(proj_used, 1)
                        if i == 1:
                            dve.wait_ge(proj_used, 1)
                            nc.vector.tensor_scalar(kT[:, :], kT[:, :], SCALE, None, ALU.mult).then_inc(k_sum, 1)
                    dve.wait_ge(proj_ps, H + 2)
                    nc.vector.tensor_tensor(v[:, :, :], pT[0][:, :].rearrange("p (t d) -> p t d", d=DH),
                                            bv[:, :].unsqueeze(1).to_broadcast([P, NT, DH]), ALU.add)\
                        .then_inc(proj_used, 1)

                    def neg_max(u):
                        dve.wait_ge(s_ps, u + 1)
                        nc.vector.tensor_reduce(nmax[:, u:u + 1], pS[u % 2][:, 0:(units[u][1] + 1) * P], AX.X, ALU.max,
                                                negate=True).then_inc(max_ready, 1)

                    def inverse(u):
                        dve.wait_ge(exp_ready, u + 1)
                        nc.vector.reciprocal(rinv[:, u:u + 1], rsum[:, u:u + 1]).then_inc(inv_ready, 1)

                    def evacuate(u):
                        h, q = units[u]
                        dve.wait_ge(t_ps, u + 1)
                        if h >= 2:
                            dve.wait_ge(o_ps, h - 1)
                        nc.vector.tensor_copy(probT[:, h % 2, 0:q + 1, q * P:(q + 1) * P],
                                              pT[u % 2][:, 0:(q + 1) * P].rearrange("p (k q) -> p k q", q=P))\
                            .then_inc(t_used, 1)

                    for u in range(len(units) + 2):
                        if u < len(units):
                            neg_max(u)
                        if 1 <= u <= len(units):
                            inverse(u - 1)
                        if u >= 2:
                            evacuate(u - 2)
                    norm_in_vector(nc, dve, n, link)

                @block.scalar
                def _(act):
                    norm_out_scalar(nc, act, n, lambda t: pY[:, t, :])

                    def output(h):
                        act.wait_ge(o_ps, h + 1)
                        nc.scalar.activation(oT[:, h, :], pO[h % 2][:, :], ACT.Copy).then_inc(o_used, 1)

                    for u, (h, q) in enumerate(units):
                        act.wait_ge(max_ready, u + 1)
                        if u >= 3:
                            act.wait_ge(t_ps, u - 2)
                        nc.scalar.activation(prob[:, u % 3, 0:(q + 1) * P], pS[u % 2][:, 0:(q + 1) * P], ACT.Exp,
                                             bias=nmax[:, u:u + 1], accum_out=rsum[:, u:u + 1]).then_inc(exp_ready, 1)
                        if q == NT - 1 and h >= 2:
                            output(h - 2)
                    output(H - 2)
                    output(H - 1)
                    norm_in_evacuate(nc, act, n, pT)

                @block.tensor
                def _(pe):
                    for i in range(H + 1):
                        if i >= 2:
                            pe.wait_ge(proj_used, i - 1)
                        for k in range(KD):
                            wt = wkv[:, k, 0:DH] if i == 0 else wq[:, k, (i - 1) * DH:i * DH]
                            last = nc.tensor.matmul(pO[i % 2][:, :], wt, n.xnT[:, k, :], start=(k == 0), stop=(k == KD - 1))
                        last.then_inc(proj_ps, 1)
                    for t in range(NT):
                        for k in range(KD):
                            last = nc.tensor.matmul(pT[0][:, t * DH:(t + 1) * DH], n.xnT[:, k, t * P:(t + 1) * P],
                                                    wkv[:, k, DH:], start=(k == 0), stop=(k == KD - 1))
                    last.then_inc(proj_ps, 1)
                    pe.wait_ge(proj_used, H + 2)
                    pe.wait_ge(k_sum, 1)

                    def scores(u):
                        h, q = units[u]
                        if u >= 2:
                            pe.wait_ge(exp_ready, u - 1)
                        nc.tensor.matmul(pS[u % 2][:, 0:(q + 1) * P], qT[:, h, q * P:(q + 1) * P], kT[:, 0:(q + 1) * P],
                                         start=True, stop=False, skip_group_check=True)
                        nc.tensor.matmul(pS[u % 2][:, q * P:(q + 1) * P], c.ident16[:, :], c.causal16[:, :],
                                         start=False, stop=True, skip_group_check=True).then_inc(s_ps, 1)

                    def turn(u):
                        pe.wait_ge(prob_ready, u + 1)
                        if u >= 2:
                            pe.wait_ge(t_used, u - 1)
                        for k in range(units[u][1] + 1):
                            last = nc.tensor.transpose(pT[u % 2][:, k * P:(k + 1) * P], prob[:, u % 3, k * P:(k + 1) * P],
                                                       c.ident[:, :])
                        last.then_inc(t_ps, 1)

                    def weigh(h):
                        pe.wait_ge(t_used, NT * (h + 1))
                        if h >= 2:
                            pe.wait_ge(o_used, h - 1)
                        for k in range(NT):
                            last = nc.tensor.matmul(pO[h % 2][:, k * P:], v[:, k, :], probT[:, h % 2, k, k * P:],
                                                    start=(k == 0), stop=(k == NT - 1), skip_group_check=True)
                        last.then_inc(o_ps, 1)

                    for u in range(len(units) + 3):
                        if u < len(units):
                            scores(u)
                        if 2 <= u < len(units) + 2:
                            turn(u - 2)
                        if u >= 3 and (u - 3) % NT == NT - 1:
                            weigh((u - 3) // NT)
                    pe.wait_ge(o_used, H)
                    pe.wait_ge(n.yn_ready, NT)
                    for t in range(NT):
                        for h in range(H):
                            last = nc.tensor.matmul(pY[:, t, :], oT[:, h, t * P:(t + 1) * P], wo[:, h, :],
                                                    start=(h == 0), stop=(h == H - 1))
                    last.then_inc(y_ps, 1)
                    norm_in_tensor(nc, pe, n, pT, c.ident)

                @block.gpsimd
                def _(pool):
                    norm_out_pool(nc, pool, n, c)
                    for u, (h, q) in enumerate(units):
                        pool.wait_ge(inv_ready, u + 1)
                        nc.gpsimd.tensor_scalar(prob[:, u % 3, 0:(q + 1) * P], prob[:, u % 3, 0:(q + 1) * P],
                                                rinv[:, u:u + 1], 1.0, ALU.mult, ALU.mult).then_inc(prob_ready, 1)
                    norm_in_pool(nc, pool, n, c)
            sc.clear()
        last_norm(nc, sc, n, src, dst, c, lambda t: pY[:, t, :], dch)


def stage_silu_mha(nc, w, src, dst, c):
    H = w["L2_attn_q_scale"].shape[0]
    DH = D // H
    SLOTS = {"q": "hhmhlm", "k": "hmhlhm"}
    EPS_LEN = 1e-6
    HP = 2
    BUF = 3
    VW = DH + 1
    HEADS = [HP * (L // (P * (q + 1))) for q in range(NT)]
    units = [(q, h) for q in range(NT) for h in range(0, H, HEADS[q])]
    last_unit = [sum(H // n for n in HEADS[:q + 1]) for q in range(NT)]
    KS = 6 * DH
    with Scope(nc, "mha") as sc:
        n = Norm(sc)
        wt = {s: sc.sb("w" + s, [P, KD, D]) for s in "qkvo"}
        hs = sc.sb("hs", [P, 2, H])
        r = sc.sb("r", [P, 2, NT * D])
        sq = sc.sb("sq", [P, 2, NT * D])
        mid = sc.sb("mid", [P, 2, NT * D], BF16)
        ss = sc.sb("ss", [P, 2, NT, H])
        ln = sc.sb("ln", [P, 2, NT, H])
        stack = sc.sb("stack", [P, 2, NT, H, P], BF16)
        qkT = sc.sb("qkT", [P, 2, H, L], BF16)
        v = sc.sb("v", [P, NT, H, VW])
        nmax = sc.sb("nmax", [P, NT, 2, H], F32)
        nmax16 = sc.sb("nmax16", [P, NT, 2 * H], BF16)
        sel = sc.sb("sel", [P, H, P], BF16)
        prob = sc.sb("prob", [P, BUF, HP, L])
        o = sc.sb("o", [P, NT, D])
        oT = sc.sb("oT", [P, KD, L])
        rinv = sc.sb("rinv", [P, NT, H])
        pS = [sc.ps(f"pS{k}", [P, HP, L]) for k in range(BUF)]
        pO = [sc.ps(f"pO{k}", [P, L]) for k in range(2)]
        pY = [pS[0], pS[1]]
        (w_in, row_ps, row_ready, sq_ready, ss_ready, len_ready, scaled, high_ready, mid_ready, mid_placed, low_ready,
         nmT_act, nmT_dve, stT_ps, stT_act, stT_dve, a_ps,
         max_ready, nm_ready, nmT_ps, s_ps, exp_ready, o_ps, o_ready, oT_ps, oT_ready, y_ps, dch, pz) = (
            sc.sem(s) for s in ("w_in", "row_ps", "row_ready", "sq_ready", "ss_ready", "len_ready", "scaled",
                                "high_ready", "mid_ready", "mid_placed", "low_ready", "nmT_act", "nmT_dve", "stT_ps", "stT_act", "stT_dve", "a_ps", "max_ready", "nm_ready",
                                "nmT_ps", "s_ps", "exp_ready", "o_ps", "o_ready", "oT_ps", "oT_ready",
                                "y_ps", "dch", "pz"))

        def by_head(a):
            return a.rearrange("p (t h d) -> p (t h) d", h=H, d=DH)

        def pT_bank(g):
            return pS[g % 4 // 2][:, g % 2, :].bitcast(BF16)

        def mixed(qa, qb):
            a, b = [u for u in units if u[0] == qa], [u for u in units if u[0] == qb]
            out = []
            for i in range(max(len(a), len(b))):
                out += [("max",) + u for u in a[i:i + 1]] + [("weight",) + u for u in b[i:i + 1]]
            return out

        jobs = [("max",) + u for u in units if u[0] < 2] + [("turn", 0, 0)] + mixed(2, 0) + [("turn", 1, 0)]
        jobs += mixed(3, 1) + [("turn", 2, 0)] + [("weight",) + u for u in units if u[0] == 2] + [("turn", 3, 0)]
        jobs += [("weight",) + u for u in units if u[0] == 3]

        def by_unit(a, q):
            return a.rearrange("p a l -> p (a l)").rearrange("p (n m) -> p n m", n=HEADS[q])[:, :, 0:(q + 1) * P]

        def slot_of(i, slot):
            return stack[:, i, :, :, slot * DH:(slot + 1) * DH].rearrange("p t h d -> p (t h) d")

        def nmT_ps_of(j):
            return pS[j % BUF][KS:, 0, 0:P // 2].bitcast(BF16)

        def nmT_copy(eng, j, q):
            psum, out = nmT_ps_of(j).unsqueeze(1).to_broadcast([2 * H, H, P]), qkT[KS:, 0, :, q * P:(q + 1) * P]
            if eng is nc.vector:
                nc.vector.tensor_copy(out, psum).then_inc(nmT_dve, 1)
            else:
                nc.scalar.activation(out, psum, ACT.Copy).then_inc(nmT_act, 1)

        def stT(g):
            return pT_bank(g).rearrange("p (a l) -> p a l", a=2)

        def y_of(t):
            return pY[t // 2][:, 0, (t % 2) * D:(t % 2 + 1) * D]

        with nc.Block() as block:
            @block.sync
            def _(sp):
                for s in "qkvo":
                    sp.dma_start(wt[s][:, :, :], w["L2_attn_W" + s].rearrange("(k p) d -> p k d", p=P)).then_inc(w_in, 16)
                for i, s in enumerate("qk"):
                    sp.dma_start(hs[:, i, :], w[f"L2_attn_{s}_scale"][None, :].to_broadcast([P, H])).then_inc(w_in, 16)
                sp.wait_ge(w_in, 16 * 6)

            @block.gpsimd
            def _(pool):
                nc.gpsimd.memset(stack[:, :, :, :, :], 0.0)
                nc.gpsimd.memset(v[:, :, :, :], 1.0)
                nc.gpsimd.memset(sel[:, :, :], 0.0).then_inc(pz, 1)
                pool.wait_ge(pz, 1)
                for i in range(2):
                    nc.gpsimd.affine_select(out=sel[:, :, :], in_=sel[:, :, :], compare_op=ALU.not_equal, fill=1.0,
                                            base=-KS - i * H, pattern=[[-1, H], [0, P]], channel_multiplier=1)\
                        .then_inc(pz, 1)
                    pool.wait_ge(pz, 2 + i)
                for t in range(NT):
                    nc.gpsimd.tensor_copy(qkT[KS:, 1, :, t * P:(t + 1) * P], sel[KS:, :, :]).then_inc(pz, 1)
                pool.wait_ge(pz, 3 + NT)
        sc.clear()
        first_norm(nc, sc, n, src, c, pO, dch, y_of)
        with nc.Fori(0, NB) as b:
            with nc.Block() as block:
                @block.sync
                def _(sp):
                    load_rows(sp, n, src, b)
                    norm_out_store(sp, n, dst, (b + NB - 1) & (NB - 1))

                @block.vector
                def _(dve):
                    link = Chain(dve, dch).link
                    norm_out_vector(nc, dve, n, link, y_of)
                    flat = lambda a: a[:, :, :, :].rearrange("p s t h -> p (s t h)")
                    for i in range(2):
                        dve.wait_ge(sq_ready, i + 1)
                        nc.vector.tensor_reduce(ss[:, i, :, :].rearrange("p t h -> p (t h)"), by_head(sq[:, i, :]), AX.X,
                                                ALU.add).then_inc(ss_ready, 1)
                    dve.wait_ge(len_ready, 1)
                    link(nc.vector.tensor_scalar(flat(ss), flat(ln), EPS_LEN, None, ALU.add))
                    link(nc.vector.reciprocal(flat(ss), flat(ss)))
                    link(nc.vector.tensor_tensor(flat(ss), flat(ss), flat(ln), ALU.mult))
                    for i in range(2):
                        last = nc.vector.tensor_tensor(ss[:, i, :, :], ss[:, i, :, :],
                                                       hs[:, i, :].unsqueeze(1).to_broadcast([P, NT, H]), ALU.mult)
                    link(last)
                    for i in range(2):
                        fac = ss[:, i, :, :].rearrange("p t h -> p (t h)").unsqueeze(2).to_broadcast([P, NT * H, DH])
                        last = nc.vector.tensor_tensor(by_head(r[:, i, :]), by_head(r[:, i, :]), fac, ALU.mult)
                        last.then_inc(scaled, 1)
                    for i in range(2):
                        dve.wait_ge(high_ready, 3 * i + 1)
                        first = SLOTS["qk"[i]].index("h")
                        link(nc.vector.tensor_tensor(by_head(sq[:, i, :]), by_head(r[:, i, :]), slot_of(i, first),
                                                     ALU.subtract))
                        nc.vector.tensor_copy(mid[:, i, :], sq[:, i, :]).then_inc(mid_ready, 1)
                        dve.wait_ge(mid_ready, i + 1)
                        nc.vector.tensor_tensor(slot_of(i, SLOTS["qk"[i]].index("l")), by_head(sq[:, i, :]),
                                                by_head(mid[:, i, :]), ALU.subtract).then_inc(low_ready, 1)
                    for g in range(1, H, 2):
                        dve.wait_ge(stT_ps, g + 1)
                        nc.vector.tensor_copy(qkT[0:KS, g // (H // 2), g % (H // 2) * 2:g % (H // 2) * 2 + 2, :],
                                              stT(g)[0:KS]).then_inc(stT_dve, 1)
                    def parts_of_max(q):
                        dve.wait_ge(max_ready, last_unit[q])
                        link(nc.vector.tensor_copy(nmax16[:, q, 0:H], nmax[:, q, 0, :]))
                        nc.vector.tensor_tensor(nmax16[:, q, H:], nmax[:, q, 0, :], nmax16[:, q, 0:H], ALU.subtract)\
                            .then_inc(nm_ready, 1)

                    def output(q):
                        dve.wait_ge(o_ps, last_unit[q])
                        po = pO[q % 2][:, 0:H * VW].rearrange("p (h d) -> p h d", d=VW)
                        link(nc.vector.reciprocal(rinv[:, q, :], po[:, :, DH]))
                        nc.vector.tensor_tensor(o[:, q, :].rearrange("p (h d) -> p h d", d=DH), po[:, :, 0:DH],
                                                rinv[:, q, :].unsqueeze(2).to_broadcast([P, H, DH]), ALU.mult)\
                            .then_inc(o_ready, 1)

                    maxima = turns = 0
                    for j, (kind, q, h) in enumerate(jobs):
                        if kind == "max":
                            maxima += 1
                            dve.wait_ge(a_ps, maxima)
                            nc.vector.tensor_reduce(nmax[:, q, 0, h:h + HEADS[q]], by_unit(pS[j % BUF][:, :, :], q), AX.X,
                                                    ALU.max, negate=True).then_inc(max_ready, 1)
                            if maxima in last_unit:
                                parts_of_max(q)
                        elif kind == "turn":
                            turns += 1
                            if q == 3:
                                output(0)
                                output(1)
                            if q % 2:
                                dve.wait_ge(nmT_ps, turns)
                                nmT_copy(nc.vector, j, q)
                    output(2)
                    output(3)
                    norm_in_vector(nc, dve, n, link)

                @block.scalar
                def _(act):
                    for i in range(3):
                        for t in range(NT):
                            act.wait_ge(row_ps, NT * i + t + 1)
                            out = v[:, t, :, 0:DH] if i == 2 else \
                                r[:, i, t * D:(t + 1) * D].rearrange("p (h d) -> p h d", d=DH)
                            nc.scalar.activation(out, pO[t % 2][:, 0:D].rearrange("p (h d) -> p h d", d=DH), ACT.Silu)\
                                .then_inc(row_ready, 1)
                        if i < 2:
                            act.wait_ge(row_ready, NT * (i + 1))
                            nc.scalar.activation(sq[:, i, :], r[:, i, :], ACT.Square).then_inc(sq_ready, 1)
                    norm_out_scalar(nc, act, n, y_of)
                    act.wait_ge(ss_ready, 2)
                    nc.scalar.activation(ln[:, :, :, :], ss[:, :, :, :], ACT.Sqrt).then_inc(len_ready, 1)
                    for i in range(2):
                        act.wait_ge(scaled, i + 1)
                        for slot in (m for m in range(6) if SLOTS["qk"[i]][m] == "h"):
                            nc.scalar.activation(slot_of(i, slot), by_head(r[:, i, :]), ACT.Copy).then_inc(high_ready, 1)
                    for g in range(0, H, 2):
                        act.wait_ge(stT_ps, g + 1)
                        nc.scalar.activation(qkT[0:KS, g // (H // 2), g % (H // 2) * 2:g % (H // 2) * 2 + 2, :],
                                             stT(g)[0:KS], ACT.Copy).then_inc(stT_act, 1)
                    weights = turns = 0
                    for j, (kind, q, h) in enumerate(jobs):
                        if kind == "turn":
                            turns += 1
                            if q % 2 == 0:
                                act.wait_ge(nmT_ps, turns)
                                nmT_copy(nc.scalar, j, q)
                        elif kind == "weight":
                            weights += 1
                            act.wait_ge(s_ps, weights)
                            if weights > BUF:
                                act.wait_ge(o_ps, weights - BUF)
                            nc.scalar.activation(by_unit(prob[:, (weights - 1) % BUF, :, :], q),
                                                 by_unit(pS[j % BUF][:, :, :], q), ACT.Exp).then_inc(exp_ready, 1)
                    for k in range(KD):
                        act.wait_ge(oT_ps, k + 1)
                        nc.scalar.activation(oT[:, k, :], pO[k][:, :], ACT.Copy).then_inc(oT_ready, 1)
                    norm_in_evacuate(nc, act, n, pO)

                @block.tensor
                def _(pe):
                    for i, s in enumerate("qkv"):
                        for t in range(NT):
                            if NT * i + t >= 2:
                                pe.wait_ge(row_ready, NT * i + t - 1)
                            for k in range(KD):
                                last = nc.tensor.matmul(pO[t % 2][:, 0:D], n.xnT[:, k, t * P:(t + 1) * P], wt[s][:, k, :],
                                                        start=(k == 0), stop=(k == KD - 1))
                            last.then_inc(row_ps, 1)
                    pe.wait_ge(n.yn_ready, NT)
                    for g in range(H):
                        i, h2 = g // (H // 2), g % (H // 2) * 2
                        pe.wait_ge(high_ready, 3 * (i + 1))
                        pe.wait_ge(mid_placed, 2 * (i + 1))
                        pe.wait_ge(low_ready, i + 1)
                        if g >= 4:
                            pe.wait_ge(stT_dve if g % 2 else stT_act, (g - 4) // 2 + 1)
                        out = pT_bank(g)
                        for a in range(2):
                            for t in range(NT):
                                at = a * L + t * P
                                last = nc.tensor.transpose(out[:, at:at + P], stack[:, i, t, h2 + a, :], c.ident16[:, :])
                        last.then_inc(stT_ps, 1)
                    pe.wait_ge(stT_dve, H // 2)
                    pe.wait_ge(stT_act, H // 2)
                    def maximum_scores(j, q, h):
                        out = by_unit(pS[j % BUF][:, :, :], q)
                        for a in range(HEADS[q]):
                            nc.tensor.matmul(out[:, a, :], qkT[0:KS, 0, h + a, q * P:(q + 1) * P],
                                             qkT[0:KS, 1, h + a, 0:(q + 1) * P], start=(a % (HEADS[q] // HP) == 0),
                                             stop=False, skip_group_check=True)
                            last = nc.tensor.matmul(out[:, a, q * P:(q + 1) * P], c.ident16[:, :], c.causal16[:, :],
                                                    start=False, stop=True, skip_group_check=True)
                        last.then_inc(a_ps, 1)

                    def turn_maxima(j, q):
                        pe.wait_ge(nm_ready, q + 1)
                        nc.tensor.transpose(nmT_ps_of(j), nmax16[:, q, :], c.ident16[:, :]).then_inc(nmT_ps, 1)

                    def weight_scores(j, q, h):
                        if h == 0:
                            pe.wait_ge(nmT_dve if q % 2 else nmT_act, q // 2 + 1)
                        out = by_unit(pS[j % BUF][:, :, :], q)
                        for a in range(HEADS[q]):
                            for k in range(q + 1):
                                nc.tensor.matmul(out[:, a, k * P:(k + 1) * P], qkT[:, 1, h + a, k * P:(k + 1) * P],
                                                 qkT[:, 0, h + a, q * P:(q + 1) * P],
                                                 start=(k == 0 and a % (HEADS[q] // HP) == 0), stop=False,
                                                 skip_group_check=True)
                            last = nc.tensor.matmul(out[:, a, q * P:(q + 1) * P], c.ident16[:, :], c.causal16T[:, :],
                                                    start=False, stop=True, skip_group_check=True)
                        last.then_inc(s_ps, 1)

                    def weigh(u):
                        q, h = units[u]
                        pe.wait_ge(exp_ready, u + 1)
                        if h == 0 and q >= 2:
                            pe.wait_ge(o_ready, q - 1)
                        weights = by_unit(prob[:, u % BUF, :, :], q)
                        for a in range(HEADS[q]):
                            for k in range(q + 1):
                                last = nc.tensor.matmul(pO[q % 2][:, (h + a) * VW:(h + a + 1) * VW],
                                                        weights[:, a, k * P:(k + 1) * P], v[:, k, h + a, :],
                                                        start=(k == 0), stop=(k == q))
                        last.then_inc(o_ps, 1)

                    def wait_buffer(j):
                        kind, q, _ = jobs[j]
                        count = sum(1 for job in jobs[:j + 1] if job[0] == kind)
                        if kind == "max":
                            pe.wait_ge(max_ready, count)
                        elif kind == "weight":
                            pe.wait_ge(exp_ready, count)
                        else:
                            pe.wait_ge(nmT_dve if q % 2 else nmT_act, q // 2 + 1)

                    pe.wait_ge(row_ready, 3 * NT)
                    weights = 0
                    for j, (kind, q, h) in enumerate(jobs):
                        if j >= BUF:
                            wait_buffer(j - BUF)
                        if kind == "max":
                            maximum_scores(j, q, h)
                        elif kind == "turn":
                            turn_maxima(j, q)
                        else:
                            weight_scores(j, q, h)
                            weights += 1
                            if weights > 2:
                                weigh(weights - 3)
                    weigh(len(units) - 2)
                    weigh(len(units) - 1)
                    pe.wait_ge(o_ready, NT)
                    for k in range(KD):
                        for t in range(NT):
                            last = nc.tensor.transpose(pO[k][:, t * P:(t + 1) * P], o[:, t, k * P:(k + 1) * P],
                                                       c.ident[:, :])
                        last.then_inc(oT_ps, 1)
                    pe.wait_ge(oT_ready, KD)
                    for t in range(NT):
                        for k in range(KD):
                            last = nc.tensor.matmul(y_of(t), oT[:, k, t * P:(t + 1) * P], wt["o"][:, k, :],
                                                    start=(k == 0), stop=(k == KD - 1))
                    last.then_inc(y_ps, 1)
                    norm_in_tensor(nc, pe, n, pO, c.ident)

                @block.gpsimd
                def _(pool):
                    norm_out_pool(nc, pool, n, c)
                    for i in range(2):
                        pool.wait_ge(mid_ready, i + 1)
                        for slot in (m for m in range(6) if SLOTS["qk"[i]][m] == "m"):
                            nc.gpsimd.tensor_copy(slot_of(i, slot), by_head(mid[:, i, :])).then_inc(mid_placed, 1)
                    norm_in_pool(nc, pool, n, c)
            sc.clear()
        last_norm(nc, sc, n, src, dst, c, y_of, dch)


def stage_mamba(nc, w, src, dst, c):
    DI, NS = w["L3_attn_A_log"].shape
    R = w["L3_attn_W_dt"].shape[0]
    CONV = w["L3_attn_W_conv"].shape[2]
    CT = DI // P
    BC = 2 * NS
    X = R + BC
    units = [(ct, s) for ct in range(CT) for s in range(NS)]
    with Scope(nc, "mamba") as sc:
        n = Norm(sc)
        w_in_t = sc.sb("w_in_t", [P, KD, 2 * DI])
        w_conv = sc.sb("w_conv", [P, CT, CONV])
        b_conv = sc.sb("b_conv", [P, CT])
        w_x = sc.sb("w_x", [P, CT, X])
        w_dt = sc.sb("w_dt", [X, DI])
        b_dt = sc.sb("b_dt", [P, CT])
        a_neg = sc.sb("a_neg", [P, CT, NS])
        d_skip = sc.sb("d_skip", [P, CT])
        w_out = sc.sb("w_out", [P, CT, D])
        sel = sc.sb("sel", [3 * BC, BC, P], BF16)
        parts = sc.sb("parts", [3 * BC, L], BF16)
        rest = sc.sb("rest", [BC, L])
        mid = sc.sb("mid", [BC, L], BF16)
        xc = sc.sb("xc", [P, CT, CONV - 1 + L])
        conv = sc.sb("conv", [P, CT, L])
        u_t = sc.sb("u_t", [P, CT, L])
        res = sc.sb("res", [P, CT, L])
        xdbl = sc.sb("xdbl", [X, L])
        delta = sc.sb("delta", [P, CT, L])
        e_t = sc.sb("e_t", [P, CT, L])
        bc = sc.sb("bc", [P, 2 * NS, L])
        dA = sc.sb("dA", [P, 3, L])
        dB = sc.sb("dB", [P, 3, L])
        h_t = sc.sb("h_t", [P, 3, L])
        hC = sc.sb("hC", [P, 3, L])
        pA = sc.ps("pA", [P, CT, L])
        pS = [sc.ps(f"pS{k}", [P, L]) for k in range(2)]
        pY = sc.ps("pY", [P, NT, D])
        (w_in, pz, xr_ps, xr_used, conv_ready, u_ready, xd_ps, xd_ready, dt_ps, z_ready, soft_ready, delta_ready, du_ready,
         bc_ps, c_ready, b_ready, parts_ready, da_ready, db_ready, scan_ready, hc_ready, s_ps, s_sum, y_ready, y_ps, dch) = (
            sc.sem(s) for s in ("w_in", "pz", "xr_ps", "xr_used", "conv_ready", "u_ready", "xd_ps", "xd_ready", "dt_ps",
                                "z_ready", "soft_ready", "delta_ready", "du_ready", "bc_ps", "c_ready", "b_ready", "parts_ready", "da_ready",
                                "db_ready", "scan_ready", "hc_ready", "s_ps", "s_sum", "y_ready", "y_ps", "dch"))
        ln1 = conv
        with nc.Block() as block:
            @block.sync
            def _(sp):
                with nc.allow_non_contiguous_dma(reason="per-channel parameters, a few values each"):
                    sp.dma_start(w_in_t[:, :, :], w["L3_attn_W_in"].rearrange("(k p) d -> p k d", p=P)).then_inc(w_in, 16)
                    sp.dma_start(w_conv[:, :, :], w["L3_attn_W_conv"].rearrange("(c p) a j -> p c (a j)", p=P))\
                        .then_inc(w_in, 16)
                    xproj = w["L3_attn_W_xproj"].rearrange("(c p) e -> p c e", p=P)
                    sp.dma_start(w_x[:, :, 0:BC], xproj[:, :, R:]).then_inc(w_in, 16)
                    sp.dma_start(w_x[:, :, BC:], xproj[:, :, 0:R]).then_inc(w_in, 16)
                    sp.dma_start(w_dt[BC:X, :], w["L3_attn_W_dt"]).then_inc(w_in, 16)
                    sp.dma_start(a_neg[:, :, :], w["L3_attn_A_log"].rearrange("(c p) s -> p c s", p=P)).then_inc(w_in, 16)
                    sp.dma_start(w_out[:, :, :], w["L3_attn_W_out"].rearrange("(c p) d -> p c d", p=P)).then_inc(w_in, 16)
                    for t, name in ((b_conv, "b_conv"), (b_dt, "b_dt"), (d_skip, "D")):
                        sp.dma_start(t[:, :], w["L3_attn_" + name].rearrange("(c p) -> p c", p=P)).then_inc(w_in, 16)
                sp.wait_ge(w_in, 16 * 10)

            @block.scalar
            def _(act):
                act.wait_ge(w_in, 16 * 10)
                nc.scalar.activation(a_neg[:, :, :], a_neg[:, :, :], ACT.Exp).then_inc(u_ready, 1)

            @block.gpsimd
            def _(pool):
                nc.gpsimd.memset(xc[:, :, :], 0.0).then_inc(pz, 1)
                nc.gpsimd.memset(sel[:, :, :], 0.0).then_inc(pz, 1)
                pool.wait_ge(pz, 2)
                for i in range(3):
                    part = sel[BC * i:BC * (i + 1), :, :]
                    nc.gpsimd.affine_select(out=part, in_=part, compare_op=ALU.not_equal, fill=1.0,
                                            base=0, pattern=[[-1, BC], [0, P]], channel_multiplier=1).then_inc(pz, 1)
                pool.wait_ge(pz, 5)
                pool.wait_ge(u_ready, 1)
                nc.gpsimd.tensor_scalar(a_neg[:, :, :].rearrange("p c s -> p (c s)"),
                                        a_neg[:, :, :].rearrange("p c s -> p (c s)"), -1.0, None, ALU.mult)\
                    .then_inc(pz, 1)
                pool.wait_ge(pz, 6)
        sc.clear()
        first_norm(nc, sc, n, src, c, pS, dch, lambda t: pY[:, t, :])
        with nc.Fori(0, NB) as b:
            with nc.Block() as block:
                @block.sync
                def _(sp):
                    load_rows(sp, n, src, b)
                    norm_out_store(sp, n, dst, (b + NB - 1) & (NB - 1))

                @block.vector
                def _(dve):
                    link = Chain(dve, dch).link
                    norm_out_vector(nc, dve, n, link, lambda t: pY[:, t, :])
                    for j in range(CONV):
                        for ct in range(CT):
                            if j == 0:
                                dve.wait_ge(xr_used, ct + 1)
                                last = nc.vector.tensor_scalar(conv[:, ct, :], xc[:, ct, 0:L], w_conv[:, ct, 0:1], None,
                                                               ALU.mult)
                            else:
                                last = nc.vector.scalar_tensor_tensor(conv[:, ct, :], xc[:, ct, j:j + L],
                                                                      w_conv[:, ct, j:j + 1], conv[:, ct, :],
                                                                      ALU.mult, ALU.add)
                            if j == CONV - 1:
                                last.then_inc(conv_ready, 1)
                        if j < CONV - 1:
                            link(last)
                    dve.wait_ge(xd_ready, 1)
                    link(nc.vector.tensor_copy(parts[0:BC, :], xdbl[0:BC, :]))
                    link(nc.vector.tensor_tensor(rest[:, :], xdbl[0:BC, :], parts[0:BC, :], ALU.subtract))
                    link(nc.vector.tensor_copy(mid[:, :], rest[:, :]))
                    nc.vector.tensor_copy(parts[BC:2 * BC, :], mid[:, :])
                    link(nc.vector.tensor_tensor(rest[:, :], rest[:, :], mid[:, :], ALU.subtract))
                    nc.vector.tensor_copy(parts[2 * BC:, :], rest[:, :]).then_inc(parts_ready, 1)
                    for ct in range(CT):
                        dve.wait_ge(dt_ps, ct + 1)
                        last = nc.vector.tensor_scalar(delta[:, ct, :], pA[:, ct, :], b_dt[:, ct:ct + 1], None, ALU.add)
                        last.then_inc(z_ready, 1)
                    for i in range(NS):
                        dve.wait_ge(bc_ps, i + 1)
                        nc.vector.tensor_copy(bc[:, i, :], pA[:, i % CT, :]).then_inc(b_ready, 1)
                    dve.wait_ge(soft_ready, 3)
                    dve.wait_ge(u_ready, CT)
                    for ct in range(CT):
                        nc.vector.scalar_tensor_tensor(xc[:, ct, CONV - 1:], e_t[:, ct, :], -0.5, e_t[:, ct, :],
                                                       ALU.mult, ALU.mult)
                        last = nc.vector.tensor_tensor(ln1[:, ct, :], ln1[:, ct, :], e_t[:, ct, :], ALU.min)
                    link(last)
                    for ct in range(CT):
                        last = nc.vector.tensor_tensor(xc[:, ct, CONV - 1:], xc[:, ct, CONV - 1:], e_t[:, ct, :], ALU.add)
                    link(last)
                    for ct in range(CT):
                        last = nc.vector.tensor_tensor(ln1[:, ct, :], ln1[:, ct, :], xc[:, ct, CONV - 1:], ALU.max)
                    link(last)
                    for ct in range(CT):
                        last = nc.vector.scalar_tensor_tensor(delta[:, ct, :], delta[:, ct, :], 0.0, ln1[:, ct, :],
                                                              ALU.max, ALU.add)
                        last.then_inc(delta_ready, 1)
                    dve.wait_ge(delta_ready, CT)
                    dve.wait_ge(soft_ready, 3)
                    for ct in range(CT):
                        nc.vector.tensor_tensor(e_t[:, ct, :], delta[:, ct, :], u_t[:, ct, :], ALU.mult)\
                            .then_inc(du_ready, 1)

                    def state_in(u):
                        ct, s = units[u]
                        if u == 0:
                            dve.wait_ge(du_ready, CT)
                            dve.wait_ge(b_ready, NS)
                            dve.wait_ge(c_ready, NS)
                        if u >= 3:
                            dve.wait_ge(scan_ready, u - 2)
                        nc.vector.tensor_tensor(dB[:, u % 3, :], e_t[:, ct, :], bc[:, s, :], ALU.mult)\
                            .then_inc(db_ready, 1)

                    def finish(ct):
                        dve.wait_ge(s_ps, ct + 1)
                        nc.vector.scalar_tensor_tensor(u_t[:, ct, :], u_t[:, ct, :], d_skip[:, ct:ct + 1],
                                                       pS[ct % 2][:, :], ALU.mult, ALU.add).then_inc(s_sum, 1)

                    state_in(0)
                    for u, (ct, s) in enumerate(units):
                        if u + 1 < len(units):
                            state_in(u + 1)
                        dve.wait_ge(da_ready, u + 1)
                        dve.wait_ge(db_ready, u + 1)
                        if u >= 3:
                            dve.wait_ge(hc_ready, u - 2)
                        nc.vector.tensor_tensor_scan(h_t[:, u % 3, :], dA[:, u % 3, :], dB[:, u % 3, :], 0.0,
                                                     ALU.mult, ALU.add).then_inc(scan_ready, 1)
                        if s == 3 and ct >= 1:
                            finish(ct - 1)
                    finish(CT - 1)
                    norm_in_vector(nc, dve, n, link)

                @block.scalar
                def _(act):
                    for i in range(2 * CT):
                        act.wait_ge(xr_ps, i + 1)
                        if i < CT:
                            nc.scalar.activation(xc[:, i, CONV - 1:], pA[:, i % CT, :], ACT.Copy).then_inc(xr_used, 1)
                        else:
                            nc.scalar.activation(res[:, i - CT, :], pA[:, i % CT, :], ACT.Silu).then_inc(xr_used, 1)
                    norm_out_scalar(nc, act, n, lambda t: pY[:, t, :])
                    for ct in range(CT):
                        act.wait_ge(conv_ready, ct + 1)
                        nc.scalar.activation(u_t[:, ct, :], conv[:, ct, :], ACT.Silu, bias=b_conv[:, ct:ct + 1])\
                            .then_inc(u_ready, 1)
                    act.wait_ge(xd_ps, 1)
                    nc.scalar.activation(xdbl[:, :], pS[0][0:X, :], ACT.Copy).then_inc(xd_ready, 1)
                    act.wait_ge(z_ready, CT)
                    nc.scalar.activation(e_t[:, :, :], delta[:, :, :], ACT.Abs).then_inc(soft_ready, 1)
                    act.wait_ge(soft_ready, 1)
                    nc.scalar.activation(e_t[:, :, :], e_t[:, :, :], ACT.Exp, scale=-1.0).then_inc(soft_ready, 1)
                    act.wait_ge(soft_ready, 2)
                    act.wait_ge(u_ready, CT)
                    nc.scalar.activation(ln1[:, :, :], e_t[:, :, :], ACT.Ln, bias=1.0).then_inc(soft_ready, 1)
                    for i in range(NS, BC):
                        act.wait_ge(bc_ps, i + 1)
                        nc.scalar.activation(bc[:, i, :], pA[:, i % CT, :], ACT.Copy).then_inc(c_ready, 1)
                    act.wait_ge(delta_ready, CT)
                    for u, (ct, s) in enumerate(units):
                        if u >= 3:
                            act.wait_ge(scan_ready, u - 2)
                        nc.scalar.activation(dA[:, u % 3, :], delta[:, ct, :], ACT.Exp, scale=a_neg[:, ct, s:s + 1])\
                            .then_inc(da_ready, 1)
                    norm_in_evacuate(nc, act, n, pS)

                @block.tensor
                def _(pe):
                    for i in range(2 * CT):
                        if i >= CT:
                            pe.wait_ge(xr_used, i - CT + 1)
                        for k in range(KD):
                            last = nc.tensor.matmul(pA[:, i % CT, :], w_in_t[:, k, i * P:(i + 1) * P], n.xnT[:, k, :],
                                                    start=(k == 0), stop=(k == KD - 1))
                        last.then_inc(xr_ps, 1)
                    for ct in range(CT):
                        pe.wait_ge(u_ready, ct + 1)
                        last = nc.tensor.matmul(pS[0][0:X, :], w_x[:, ct, :], u_t[:, ct, :], start=(ct == 0),
                                                stop=(ct == CT - 1))
                    last.then_inc(xd_ps, 1)
                    pe.wait_ge(xd_ready, 1)
                    pe.wait_ge(xr_used, 2 * CT)
                    for ct in range(CT):
                        nc.tensor.matmul(pA[:, ct, :], w_dt[BC:X, ct * P:(ct + 1) * P], xdbl[BC:X, :], start=True, stop=True)\
                            .then_inc(dt_ps, 1)
                    pe.wait_ge(parts_ready, 1)
                    for i in range(BC):
                        if i < CT:
                            pe.wait_ge(z_ready, i + 1)
                        else:
                            pe.wait_ge(b_ready if i - CT < NS else c_ready, (i - CT) % NS + 1)
                        nc.tensor.matmul(pA[:, i % CT, :], sel[:, i, :], parts[:, :], start=True, stop=True)\
                            .then_inc(bc_ps, 1)
                    for u, (ct, s) in enumerate(units):
                        if s == 0 and ct >= 2:
                            pe.wait_ge(s_sum, ct - 1)
                        pe.wait_ge(hc_ready, u + 1)
                        last = nc.tensor.matmul(pS[ct % 2][:, :], c.ident[:, :], hC[:, u % 3, :], start=(s == 0),
                                                stop=(s == NS - 1))
                        last.then_inc(bc_ps, 1)
                        if s == NS - 1:
                            last = None
                            pe.wait_ge(bc_ps, 2 * NS + u + 1)
                            pe.sem_inc(s_ps, 1)
                    pe.wait_ge(n.yn_ready, NT)
                    for ct in range(CT):
                        pe.wait_ge(y_ready, ct + 1)
                    for t in range(NT):
                        for ct in range(CT):
                            last = nc.tensor.matmul(pY[:, t, :], res[:, ct, t * P:(t + 1) * P], w_out[:, ct, :],
                                                    start=(ct == 0), stop=(ct == CT - 1))
                    last.then_inc(y_ps, 1)
                    norm_in_tensor(nc, pe, n, pS, c.ident)

                @block.gpsimd
                def _(pool):
                    norm_out_pool(nc, pool, n, c)
                    def state_out(u):
                        ct, s = units[u]
                        pool.wait_ge(scan_ready, u + 1)
                        if u == 0:
                            pool.wait_ge(c_ready, NS)
                            pool.wait_ge(b_ready, NS)
                        if u >= 3:
                            pool.wait_ge(bc_ps, 2 * NS + u - 2)
                        nc.gpsimd.tensor_tensor(hC[:, u % 3, :], h_t[:, u % 3, :], bc[:, NS + s, :], ALU.mult)\
                            .then_inc(hc_ready, 1)

                    def gate(ct):
                        pool.wait_ge(s_sum, ct + 1)
                        nc.gpsimd.tensor_tensor(res[:, ct, :], res[:, ct, :], u_t[:, ct, :], ALU.mult)\
                            .then_inc(y_ready, 1)

                    for u in range(len(units)):
                        state_out(u)
                        if u >= 8 and (u - 8) % NS == NS - 1:
                            gate((u - 8) // NS)
                    gate(CT - 1)
                    norm_in_pool(nc, pool, n, c)
            sc.clear()
        last_norm(nc, sc, n, src, dst, c, lambda t: pY[:, t, :], dch)


def stage_expert_choice(nc, w, src, dst, c):
    E, S, _, M = w["L1_ffn_W1"].shape
    K = w["L1_ffn_W2"].shape[3]
    T = NB * L
    CAP = int(1.5 * T / E)
    assert CAP == P and D == 2 * P and M == 2 * P
    GE = 4
    MT = M // P
    TAKEN = -3.0e38
    normed = nc.dram_tensor("normed", [T, D], F32, kind="Internal").ap()
    logit_d = nc.dram_tensor("router_logits", [E, T], F32, kind="Internal").ap()
    moe_sum = nc.dram_tensor("moe_sum", [T, D], F32, kind="Internal").ap()

    with Scope(nc, "route") as sc:
        n = Norm(sc)
        wr = sc.sb("wr", [P, KD, E])
        lg = sc.sb("lg", [E, L])
        zero = sc.sb("zero", [P, NT, D])
        pX = [sc.ps(f"pX{k}", [P, L]) for k in range(KD)]
        pL = sc.ps("pL", [E, L])
        w_in, z_ready, lg_ps, lg_ready, stored, dch = (
            sc.sem(s) for s in ("w_in", "z_ready", "lg_ps", "lg_ready", "stored", "dch"))
        with nc.Block() as block:
            @block.sync
            def _(sp):
                sp.dma_start(wr[:, :, :], w["L1_ffn_Wr"].rearrange("(k p) e -> p k e", p=P)).then_inc(w_in, 16)
                sp.wait_ge(w_in, 16)

            @block.vector
            def _(dve):
                nc.vector.memset(zero[:, :, :], 0.0).then_inc(z_ready, 1)
                dve.wait_ge(z_ready, 1)
        sc.clear()
        with nc.Fori(0, NB) as b:
            with nc.Block() as block:
                @block.sync
                def _(sp):
                    sp.dma_start(n.x[:, :, :], rows(src)[b]).then_inc(n.x_in, 16)
                    sp.dma_start(moe_sum.rearrange("(b t p) d -> b p t d", t=NT, p=P)[b], zero[:, :, :])\
                        .then_inc(stored, 16)
                    sp.wait_ge(n.xn_ready, NT)
                    sp.dma_start(normed.rearrange("(b t p) d -> b p t d", t=NT, p=P)[b], n.xn[:, :, :])\
                        .then_inc(stored, 16)
                    sp.wait_ge(lg_ready, 1)
                    sp.dma_start(logit_d.rearrange("e (b l) -> b e l", l=L)[b], lg[:, :]).then_inc(stored, 16)
                    sp.wait_ge(stored, 48)

                @block.vector
                def _(dve):
                    norm_in_vector(nc, dve, n, Chain(dve, dch).link)

                @block.scalar
                def _(act):
                    norm_in_evacuate(nc, act, n, pX)
                    act.wait_ge(lg_ps, 1)
                    nc.scalar.activation(lg[:, :], pL[:, :], ACT.Copy).then_inc(lg_ready, 1)

                @block.tensor
                def _(pe):
                    norm_in_tensor(nc, pe, n, pX, c.ident)
                    pe.wait_ge(n.xnT_ready, KD)
                    for k in range(KD):
                        last = nc.tensor.matmul(pL[:, :], wr[:, k, :], n.xnT[:, k, :], start=(k == 0), stop=(k == KD - 1))
                    last.then_inc(lg_ps, 1)

                @block.gpsimd
                def _(pool):
                    norm_in_pool(nc, pool, n, c)
            sc.clear()

    with Scope(nc, "expert") as sc:
        lg = sc.sb("lg", [E, T])
        vals = sc.sb("vals", [E, CAP])
        idx = sc.sb("idx", [E, CAP], U32)
        idx_f = sc.sb("idx_f", [E, CAP])
        nmax = sc.sb("nmax", [E, 1])
        rsum = sc.sb("rsum", [E, 1])
        idxT = sc.sb("idxT", [P, E], U32)
        wgtT = sc.sb("wgtT", [P, E])
        ES = E * S // 2
        b1r = sc.sb("b1r", [ES, 2, M])
        b1T = sc.sb("b1T", [P, E * S, MT])
        ones = sc.sb("ones", [1, P])
        w1 = [sc.sb(f"w1_{g}", [P, GE, S, 2, M]) for g in range(2)]
        w2 = [sc.sb(f"w2_{g}", [P, GE, S, 2, K]) for g in range(2)]
        b2 = [sc.sb(f"b2_{g}", [1, GE, S * K]) for g in range(2)]
        xg = [sc.sb(f"xg_{g}", [P, GE, D]) for g in range(2)]
        col = [sc.sb(f"col_{g}", [P, GE], U32) for g in range(2)]
        xgT = sc.sb("xgT", [P, 2, KD, P])
        hT = sc.sb("hT", [P, 2, S * MT, P])
        y = sc.sb("y", [P, 2, D])
        pX = [sc.ps(f"pX{k}", [P, L]) for k in range(2)]
        pH = [sc.ps(f"pH{k}", [P, S * MT, P]) for k in range(2)]
        pY = [sc.ps(f"pY{k}", [P, L]) for k in range(2)]
        (lg_in, b1_in, w_in, dch, max_ready, exp_ready, wgt_ready, t_ps, t_ready, col_ready, x_ps, x_ready, h_ps, hb_ready,
         h_ready, y_ps, y_ready, one_ready) = (
            sc.sem(s) for s in ("lg_in", "b1_in", "w_in", "dch", "max_ready", "exp_ready", "wgt_ready", "t_ps",
                                "t_ready", "col_ready", "x_ps", "x_ready", "h_ps", "hb_ready", "h_ready", "y_ps",
                                "y_ready", "one_ready"))

        def load_group(sp, g, e0):
            for j in range(GE):
                sp.dma_start(w1[g][:, j, :, :, :].rearrange("p s k m -> p s (k m)"),
                             w["L1_ffn_W1"][bass.ds(e0 + j, 1)].rearrange("e s (p k) m -> p (e s) (k m)", k=2))\
                    .then_inc(w_in, 16)
                sp.dma_start(w2[g][:, j, :, :, :].rearrange("p s k m -> p s (k m)"),
                             w["L1_ffn_W2"][bass.ds(e0 + j, 1)].rearrange("e s (p k) m -> p (e s) (k m)", k=2))\
                    .then_inc(w_in, 16)
            sp.dma_start(b2[g][:, :, :], w["L1_ffn_b2"].rearrange("(a e) s k -> a e (s k)", a=1)[:, bass.ds(e0, GE), :])\
                .then_inc(w_in, 16)

        LOADS = 16 * (2 * GE + 1)

        def gather_group(pool, g):
            for j in range(GE):
                pool.indirect_dma_start(out=xg[g][:, j, :], out_offset=None, in_=normed,
                                        in_offset=bass.IndirectOffsetOnAxis(ap=col[g][:, j:j + 1], axis=0))\
                    .then_inc(c.gathered, 16)

        with nc.Block() as block:
            @block.sync
            def _(sp):
                sp.dma_start(lg[:, :], logit_d).then_inc(lg_in, 16)
                sp.dma_start(b1r[:, :, :], w["L1_ffn_b1"].rearrange("(a e) s m -> (e s) a m", a=2)).then_inc(b1_in, 16)
                load_group(sp, 0, 0)
                sp.wait_ge(w_in, LOADS)

            @block.vector
            def _(dve):
                link = Chain(dve, dch).link
                nc.vector.memset(ones[:, :], 1.0).then_inc(one_ready, 1)
                dve.wait_ge(lg_in, 16)
                for i in range(CAP // 8):
                    eight = slice(8 * i, 8 * i + 8)
                    link(nc.vector.max(vals[:, eight], lg[:, :]))
                    link(nc.vector.max_index(idx[:, eight], vals[:, eight], lg[:, :]))
                    link(nc.vector.match_replace(lg[:, :], vals[:, eight], lg[:, :], TAKEN))
                link(nc.vector.tensor_copy(idx_f[:, :], idx[:, :]))
                nc.vector.tensor_scalar(nmax[:, :], vals[:, 0:1], -1.0, None, ALU.mult).then_inc(max_ready, 1)
                dve.wait_ge(exp_ready, 1)
                link(nc.vector.reciprocal(rsum[:, :], rsum[:, :]))
                nc.vector.tensor_scalar(vals[:, :], vals[:, :], rsum[:, 0:1], None, ALU.mult).then_inc(wgt_ready, 1)
                dve.wait_ge(t_ps, 1)
                nc.vector.tensor_copy(b1T[:, :, :].rearrange("p (a e) k -> p a k e", a=2),
                                      pX[1][:, 0:2 * MT * ES].rearrange("p (a k e) -> p a k e", a=2, k=MT))\
                    .then_inc(t_ready, 1)
                dve.wait_ge(t_ps, 2)
                link(nc.vector.tensor_copy(idxT[:, :], pX[0][:, 0:E]))
                nc.vector.tensor_copy(wgtT[:, :], pX[0][:, E:2 * E]).then_inc(t_ready, 1)
                nc.vector.tensor_copy(col[0][:, :], idxT[:, 0:GE]).then_inc(col_ready, 1)
                dve.wait_ge(t_ready, 2)

            @block.scalar
            def _(act):
                act.wait_ge(max_ready, 1)
                nc.scalar.activation(vals[:, :], vals[:, :], ACT.Exp, bias=nmax[:, 0:1], accum_out=rsum[:, 0:1])\
                    .then_inc(exp_ready, 1)

            @block.tensor
            def _(pe):
                pe.wait_ge(b1_in, 16)
                for a in range(2):
                    for k in range(MT):
                        at = (a * MT + k) * ES
                        last = nc.tensor.transpose(pX[1][:, at:at + ES], b1r[:, a, k::MT], c.ident[0:ES, 0:ES])
                last.then_inc(t_ps, 1)
                pe.wait_ge(wgt_ready, 1)
                nc.tensor.transpose(pX[0][:, 0:E], idx_f[:, :], c.ident[0:E, 0:E])
                nc.tensor.transpose(pX[0][:, E:2 * E], vals[:, :], c.ident[0:E, 0:E]).then_inc(t_ps, 1)

            @block.gpsimd
            def _(pool):
                pool.wait_ge(col_ready, 1)
                gather_group(pool, 0)
                pool.wait_ge(c.gathered, 16 * GE)
        sc.clear()

        def half(g, e0, more):
            with nc.Block() as block:
                @block.sync
                def _(sp):
                    if more:
                        load_group(sp, 1 - g, e0 + GE)
                        sp.wait_ge(w_in, LOADS)

                @block.vector
                def _(dve):
                    if more:
                        nc.vector.tensor_copy(col[1 - g][:, :], idxT[:, bass.ds(e0 + GE, GE)]).then_inc(col_ready, 1)

                    def add_b1(j):
                        dve.wait_ge(h_ps, j + 1)
                        if j >= 2:
                            dve.wait_ge(y_ps, j - 1)
                        bias = b1T[:, bass.ds((e0 + j) * S, S), :].rearrange("p s k -> p (s k)")
                        nc.vector.tensor_tensor(hT[:, j % 2, :, :], pH[j % 2][:, :, :],
                                                bias.unsqueeze(2).to_broadcast([P, S * MT, P]), ALU.add)\
                            .then_inc(hb_ready, 1)

                    def weigh(j):
                        dve.wait_ge(y_ps, j + 1)
                        if j:
                            dve.wait_ge(c.added, (e0 + j) * 16)
                        nc.vector.tensor_tensor(y[:, j % 2, :], pY[j % 2][:, 0:D],
                                                wgtT[:, bass.ds(e0 + j, 1)].to_broadcast([P, D]), ALU.mult)\
                            .then_inc(y_ready, 1)

                    for j in range(GE + 1):
                        if j < GE:
                            add_b1(j)
                        if j >= 1:
                            weigh(j - 1)

                @block.scalar
                def _(act):
                    def turned(j):
                        act.wait_ge(x_ps, j + 1)
                        if j >= 2:
                            act.wait_ge(h_ps, j - 1)
                        nc.scalar.activation(xgT[:, j % 2, :, :].rearrange("p k t -> p (k t)"), pX[j % 2][:, 0:D], ACT.Copy)\
                            .then_inc(x_ready, 1)

                    turned(0)
                    for j in range(GE):
                        if j + 1 < GE:
                            turned(j + 1)
                        act.wait_ge(hb_ready, j + 1)
                        nc.scalar.activation(hT[:, j % 2, :, :], hT[:, j % 2, :, :], ACT.Gelu).then_inc(h_ready, 1)

                @block.tensor
                def _(pe):
                    def turn(j):
                        if j >= 2:
                            pe.wait_ge(x_ready, j - 1)
                        for k in range(KD):
                            last = nc.tensor.transpose(pX[j % 2][:, k * P:(k + 1) * P], xg[g][:, j, k::KD], c.ident[:, :])
                        last.then_inc(x_ps, 1)

                    def hidden(j):
                        pe.wait_ge(x_ready, j + 1)
                        if j >= 2:
                            pe.wait_ge(hb_ready, j - 1)
                        for s in range(S):
                            for m in range(MT):
                                for k in range(KD):
                                    last = nc.tensor.matmul(pH[j % 2][:, s * MT + m, :], w1[g][:, j, s, k, m::MT],
                                                            xgT[:, j % 2, k, :], start=(k == 0), stop=(k == KD - 1))
                        last.then_inc(h_ps, 1)

                    def output(j):
                        pe.wait_ge(h_ready, j + 1)
                        if j >= 2:
                            pe.wait_ge(y_ready, j - 1)
                        nc.tensor.matmul(pY[j % 2][:, 0:D], ones[:, :], b2[g][:, j, :], start=True, stop=False,
                                         skip_group_check=True)
                        for s in range(S):
                            for m in range(MT):
                                last = nc.tensor.matmul(pY[j % 2][:, s * K:(s + 1) * K], hT[:, j % 2, s * MT + m, :],
                                                        w2[g][:, j, s, m, :], start=False, stop=(m == MT - 1),
                                                        skip_group_check=True)
                        last.then_inc(y_ps, 1)

                    turn(0)
                    for j in range(GE + 1):
                        if j + 1 < GE:
                            turn(j + 1)
                        if j < GE:
                            hidden(j)
                        if j >= 1:
                            output(j - 1)

                @block.gpsimd
                def _(pool):
                    if more:
                        pool.wait_ge(col_ready, 1)
                        gather_group(pool, 1 - g)
                    for j in range(GE):
                        pool.wait_ge(y_ready, j + 1)
                        pool.indirect_dma_start(out=moe_sum, in_=y[:, j % 2, :], in_offset=None,
                                                out_offset=bass.IndirectOffsetOnAxis(ap=col[g][:, j:j + 1], axis=0),
                                                compute_op=ALU.add).then_inc(c.added, 16)
                    pool.wait_ge(c.added, (e0 + GE) * 16)
                    if more:
                        pool.wait_ge(c.gathered, (e0 + 2 * GE) * 16)
            sc.clear()

        with nc.Fori(0, E // (2 * GE) - 1) as i:
            half(0, i * (2 * GE), True)
            half(1, i * (2 * GE) + GE, True)
        half(0, E - 2 * GE, True)
        half(1, E - GE, False)

    with Scope(nc, "moe_out") as sc:
        n = Norm(sc)
        y = sc.sb("y", [P, NT, D])
        y_in, dch = sc.sem("y_in"), sc.sem("dch")
        with nc.Fori(0, NB) as b:
            with nc.Block() as block:
                @block.sync
                def _(sp):
                    sp.dma_start(y[:, :, :], moe_sum.rearrange("(b t p) d -> b p t d", t=NT, p=P)[b]).then_inc(y_in, 16)
                    sp.dma_start(n.xr[:, :, :], rows(src)[b]).then_inc(n.xr_in, 16)
                    norm_out_store(sp, n, dst, b)

                @block.vector
                def _(dve):
                    dve.wait_ge(y_in, 16)
                    norm_out_vector(nc, dve, n, Chain(dve, dch).link, lambda t: y[:, t, :])

                @block.scalar
                def _(act):
                    norm_out_scalar(nc, act, n, lambda t: y[:, t, :])

                @block.gpsimd
                def _(pool):
                    norm_out_pool(nc, pool, n, c)
            sc.clear()


def stage_delta(nc, w, src, dst, c):
    H = w["L0_attn_Wb"].shape[1]
    DH = D // H
    CONV = w["L0_attn_conv_q"].shape[1]
    TAPS = [w["L0_attn_fir_" + f].shape[2] for f in "sml"]
    PAST = max(TAPS) - 1
    NG = w["L0_attn_gate_w"].shape[2]
    CH = 32
    NC = P // CH
    PE_TAPS = 12
    POOL_TAPS = 38
    PRODS = 3
    PRODS_OF_TILE = 9
    LEVELS = 4
    with Scope(nc, "delta") as sc:
        n = Norm(sc)
        wt = {s: sc.sb("w" + s, [P, KD, D]) for s in "qkvo"}
        wg = sc.sb("wg", [P, KD, H * NG + H])
        wconv = {s: sc.sb("wconv" + s, [P, KD, CONV]) for s in "qkv"}
        fir = {f: sc.sb("fir" + f, [P, KD, k]) for f, k in zip("sml", TAPS)}
        diag = sc.sb("diag", [P, KD, PE_TAPS, P])
        masks = sc.sb("masks", [P, LEVELS + 3, P])
        gate_b = sc.sb("gate_b", [P, H, NG])
        itemp = sc.sb("itemp", [P, H])
        geps = sc.sb("geps", [P, H])
        gscale = sc.sb("gscale", [P, H])
        norm_w = sc.sb("norm_w", [P, 1])
        xc = {s: sc.sb("xc" + s, [P, KD, CONV - 1 + L]) for s in "qkv"}
        cT = {s: sc.sb("c" + s, [P, KD, (PAST if s == "v" else 0) + L]) for s in "qkv"}
        r = {s: sc.sb("r" + s, [P, NT, D]) for s in "qkv"}
        kb = sc.sb("kb", [P, NT, D])
        vb = sc.sb("vb", [P, NT, D])
        sq = sc.sb("sq", [P, NT, D])
        ss = {s: sc.sb("ss" + s, [P, NT * H]) for s in "qko"}
        beta = sc.sb("beta", [P, NT, H])
        gl = sc.sb("gl", [P, NT, H, NG])
        gred = sc.sb("gred", [P, NT * H])
        hT = {s: sc.sb("hT" + s, [DH, H, L]) for s in ("q", "k", "kb")}
        facc = {f: sc.sb("facc_" + f, [P, KD, L]) for f in ("s", "m", "l", "l_pe", "l_pool")}
        prod = sc.sb("prod", [P, PRODS, KD, L])
        GT = sc.sb("GT", [P, H, P])
        Tm = sc.sb("Tm", [P, H, P])
        TT = sc.sb("TT", [P, H, P])
        X = sc.sb("X", [P, H, P])
        attnT = sc.sb("attnT", [P, 2, H, P])
        u_t = sc.sb("u_t", [P, D])
        ua = sc.sb("ua", [P, D])
        wT = sc.sb("wT", [DH, H, P])
        S = sc.sb("S", [DH, D])
        do = sc.sb("do", [P, NT, D])
        o = sc.sb("o", [P, NT, D])
        oT = sc.sb("oT", [P, KD, L])
        pb = [sc.ps(f"pb{k}", [P, L]) for k in range(6)]
        pY = sc.ps("pY", [P, NT, D])
        turned = (pb[0], pb[1], pb[3], pb[4])
        pW, pS, pF = pY[:, 0, :], pY[0:DH, 1, :], pY[:, 2:4, :]
        NAMES = ("w_in", "zeroed", "proj_ps", "xc_ready", "conv_ready", "c_ready", "gate_ps", "beta_ready", "gate_sub",
                 "gate_exp", "row_ps", "row_ready", "sq_ready", "ss_ready", "ilen_ready", "rows_ready", "firp_ps",
                 "firp_ready", "hT_ps", "hT_ready", "g_ps", "gt_ready", "t_ready", "x_ps", "x_masked", "tx_ps",
                 "attn_ready", "uw_ps", "uw_ready", "ws_ps", "ua_ready", "ks_ps", "s_ready", "do_ps", "do_ready",
                 "s_zero", "fir_done", "fir_ps", "fir_used", "o_sq", "o_ss", "o_ilen", "o_ready", "oT_ps", "oT_ready",
                 "y_ps", "dch", "pch", "setup", "pool_taps_done", "prod_ready",
                 "prod_used")
        z = {name: sc.sem(name) for name in NAMES}

        def xc_out(s, k):
            return facc[{"q": "s", "k": "m", "v": "l"}[s]][:, k, :]

        def xc_silu(s, k):
            return cT[s][:, k, (PAST if s == "v" else 0):]

        def hd(a):
            return a[:, :, :].rearrange("p t (h d) -> p (t h) d", d=DH)

        def per_head(a):
            return a.unsqueeze(2).to_broadcast([P, NT * H, DH])

        with nc.Block() as block:
            @block.sync
            def _(sp):
                def load(out, in_):
                    sp.dma_start(out, in_).then_inc(z["w_in"], 16)

                for s in "qkvo":
                    load(wt[s][:, :, :], w["L0_attn_W" + s].rearrange("(k p) d -> p k d", p=P))
                with nc.allow_non_contiguous_dma(reason="small weights"):
                    for h in range(H):
                        load(wg[:, :, h * NG:(h + 1) * NG], w["L0_attn_gate_w"][h].rearrange("(k p) g -> p k g", p=P))
                    load(wg[:, :, H * NG:], w["L0_attn_Wb"].rearrange("(k p) h -> p k h", p=P))
                    for s in "qkv":
                        load(wconv[s][:, :, :], w["L0_attn_conv_" + s].rearrange("(k p) j -> p k j", p=P))
                    for f in "sml":
                        load(fir[f][:, :, :], w["L0_attn_fir_" + f].rearrange("(k h) d j -> (h d) k j", k=KD))
                load(masks[:, :, :], w["chunk_masks"])
                load(gate_b[:, :, :], w["L0_attn_gate_b"][None, :, :].to_broadcast([P, H, NG]))
                for t, name in ((itemp, "log_temp"), (geps, "eps_param")):
                    load(t[:, :], w["L0_attn_" + name].rearrange("h a -> a h").to_broadcast([P, H]))
                with nc.allow_non_contiguous_dma(reason="a weight for each partition"):
                    for i in range(P // DH):
                        load(norm_w[i * DH:(i + 1) * DH, :], w["L0_attn_norm_w"].rearrange("(d a) -> d a", a=1))
                sp.wait_ge(z["w_in"], 16 * (4 + H + 1 + 3 + 3 + 1 + 1 + 2 + P // DH))

            @block.scalar
            def _(act):
                act.wait_ge(z["w_in"], 16 * (4 + H + 1 + 3 + 3 + 1 + 1 + 2 + P // DH))
                nc.scalar.activation(itemp[:, :], itemp[:, :], ACT.Exp, scale=-1.0).then_inc(z["setup"], 1)
                act.wait_ge(z["setup"], 1)

            @block.vector
            def _(dve):
                link = Chain(dve, z["dch"]).link
                dve.wait_ge(z["w_in"], 16 * (4 + H + 1 + 3 + 3 + 1 + 1 + 2 + P // DH))
                for k in range(KD):
                    link(nc.vector.tensor_scalar(wt["o"][:, k, :], wt["o"][:, k, :], norm_w[:, 0:1], None, ALU.mult))
                link(nc.vector.tensor_scalar(geps[:, :], geps[:, :], 0.0, 0.2, ALU.max, ALU.min))
                link(nc.vector.tensor_scalar(gscale[:, :], geps[:, :], -float(NG), 1.0, ALU.mult, ALU.add))
                for k in range(KD):
                    for j in range(PE_TAPS):
                        last = nc.vector.tensor_scalar(diag[:, k, j, :], c.ident[:, :], fir["l"][:, k, j:j + 1], None,
                                                       ALU.mult)
                link(last)

            @block.gpsimd
            def _(pool):
                for s in "qkv":
                    nc.gpsimd.memset(xc[s][:, :, :], 0.0)
                nc.gpsimd.memset(cT["v"][:, :, :], 0.0).then_inc(z["zeroed"], 1)
                pool.wait_ge(z["zeroed"], 1)
        sc.clear()
        first_norm(nc, sc, n, src, c, pb, z["dch"], lambda t: pY[:, t, :])
        with nc.Fori(0, NB) as b:
            with nc.Block() as block:
                @block.sync
                def _(sp):
                    load_rows(sp, n, src, b)
                    norm_out_store(sp, n, dst, (b + NB - 1) & (NB - 1))

                @block.vector
                def _(dve):
                    link = Chain(dve, z["dch"]).link
                    norm_out_vector(nc, dve, n, link, lambda t: pY[:, t, :])
                    for i, s in enumerate("qkv"):
                        for j in range(CONV):
                            for k in range(KD):
                                if j == 0:
                                    dve.wait_ge(z["xc_ready"], KD * i + k + 1)
                                    last = nc.vector.tensor_scalar(xc_out(s, k), xc[s][:, k, 0:L], wconv[s][:, k, 0:1],
                                                                   None, ALU.mult)
                                else:
                                    last = nc.vector.scalar_tensor_tensor(xc_out(s, k), xc[s][:, k, j:j + L],
                                                                          wconv[s][:, k, j:j + 1], xc_out(s, k),
                                                                          ALU.mult, ALU.add)
                            if j < CONV - 1:
                                link(last)
                        last.then_inc(z["conv_ready"], 1)
                    flat = gl[:, :, :, :].rearrange("p t h g -> p (t h) g")
                    gps = pb[5][:, 0:NT * (NG + 1) * H].rearrange("p (t x) -> p t x", t=NT)
                    dve.wait_ge(z["gate_ps"], 1)
                    dve.wait_ge(z["beta_ready"], 1)
                    for t in range(NT):
                        last = nc.vector.tensor_tensor(gl[:, t, :, :], gps[:, t, 0:H * NG].rearrange("p (h g) -> p h g", g=NG),
                                                       gate_b[:, :, :], ALU.add)
                    link(last)
                    for t in range(NT):
                        last = nc.vector.tensor_tensor(gl[:, t, :, :], gl[:, t, :, :],
                                                       itemp[:, :].unsqueeze(2).to_broadcast([P, H, NG]), ALU.mult)
                    link(last)
                    link(nc.vector.tensor_reduce(gred[:, :], flat, AX.X, ALU.max))
                    nc.vector.tensor_tensor(flat, flat, gred[:, :].unsqueeze(2).to_broadcast([P, NT * H, NG]),
                                            ALU.subtract).then_inc(z["gate_sub"], 1)
                    for i, s in enumerate("qk"):
                        dve.wait_ge(z["sq_ready"], i + 1)
                        nc.vector.tensor_reduce(ss[s][:, :], hd(sq), AX.X, ALU.add).then_inc(z["ss_ready"], 1)
                    for i, s in enumerate("qk"):
                        dve.wait_ge(z["ilen_ready"], 2 * i + 2)
                        last = nc.vector.tensor_tensor(hd(r[s]), hd(r[s]), per_head(ss[s][:, :]), ALU.mult)
                        last.then_inc(z["rows_ready"], 1)
                    bflat = beta[:, :, :].rearrange("p t h -> p (t h)")
                    dve.wait_ge(z["rows_ready"], 2)
                    nc.vector.tensor_tensor(hd(kb), hd(r["k"]), per_head(bflat), ALU.mult).then_inc(z["rows_ready"], 1)
                    dve.wait_ge(z["row_ready"], 6)
                    nc.vector.tensor_tensor(hd(vb), hd(r["v"]), per_head(bflat), ALU.mult).then_inc(z["rows_ready"], 1)
                    dve.wait_ge(z["gate_exp"], 1)
                    link(nc.vector.tensor_reduce(gred[:, :], flat, AX.X, ALU.add))
                    link(nc.vector.reciprocal(gred[:, :], gred[:, :]))
                    link(nc.vector.tensor_tensor(flat, flat, gred[:, :].unsqueeze(2).to_broadcast([P, NT * H, NG]), ALU.mult))
                    for t in range(NT):
                        last = nc.vector.tensor_tensor(gl[:, t, :, :], gl[:, t, :, :],
                                                       gscale[:, :].unsqueeze(2).to_broadcast([P, H, NG]), ALU.mult)
                    link(last)
                    for t in range(NT):
                        last = nc.vector.tensor_tensor(gl[:, t, :, :], gl[:, t, :, :],
                                                       geps[:, :].unsqueeze(2).to_broadcast([P, H, NG]), ALU.add)
                    last.then_inc(z["gate_sub"], 1)

                    def tap(f, k, j, first):
                        at = PAST - (TAPS["sml".index(f)] - 1) + j
                        v_in, acc, wj = cT["v"][:, k, at:at + L], facc[f][:, k, :], fir[f][:, k, j:j + 1]
                        if first:
                            return nc.vector.tensor_scalar(acc, v_in, wj, None, ALU.mult)
                        return nc.vector.scalar_tensor_tensor(acc, v_in, wj, acc, ALU.mult, ALU.add)

                    steps = [(f, j) for f in "sm" for j in range(TAPS["sml".index(f)])]
                    steps += [("l", j) for j in range(PE_TAPS + POOL_TAPS, TAPS[2])]
                    done = [0]

                    def taps(count):
                        for _ in range(count):
                            if done[0] == len(steps):
                                return
                            f, j = steps[done[0]]
                            for k in range(KD):
                                last = tap(f, k, j, j in (0, PE_TAPS + POOL_TAPS))
                            done[0] += 1
                            link(last)

                    def all_heads(a):
                        return a.unsqueeze(1).to_broadcast([P, H, P])

                    def bank(i):
                        return pb[i][:, :].rearrange("p (h j) -> p h j", h=H)

                    def inverse_start(t):
                        dve.wait_ge(z["g_ps"], t + 1)
                        nc.vector.tensor_tensor(Tm[:, :, :], bank(0), all_heads(masks[:, 0, :]), ALU.mult)
                        dve.wait_ge(z["gt_ready"], t + 1)
                        link(nc.vector.tensor_tensor(TT[:, :, :], bank(1), all_heads(masks[:, 1, :]), ALU.mult))
                        nc.vector.tensor_tensor(Tm[:, :, :], Tm[:, :, :], all_heads(c.ident[:, :]), ALU.add)
                        nc.vector.tensor_tensor(TT[:, :, :], TT[:, :, :], all_heads(c.ident[:, :]), ALU.add)\
                            .then_inc(z["t_ready"], 1)
                        nc.vector.tensor_tensor(attnT[:, t % 2, :, :], bank(2), all_heads(masks[:, 6, :]), ALU.mult)\
                            .then_inc(z["attn_ready"], 1)

                    def level_mask(t, lv):
                        dve.wait_ge(z["x_ps"], LEVELS * t + lv + 1)
                        nc.vector.tensor_tensor(X[:, :, :], bank(0), all_heads(masks[:, 2 + lv, :]), ALU.mult)\
                            .then_inc(z["x_masked"], 1)

                    def level_subtract(t, lv):
                        dve.wait_ge(z["tx_ps"], LEVELS * t + lv + 1)
                        if lv < LEVELS - 1:
                            nc.vector.tensor_tensor(Tm[:, :, :], Tm[:, :, :], bank(1), ALU.subtract)
                        nc.vector.tensor_tensor(TT[:, :, :], TT[:, :, :], bank(2), ALU.subtract)\
                            .then_inc(z["t_ready"], 1)

                    def gated_rows(i):
                        f, t2 = i // 2, i % 2
                        if i == 0:
                            dve.wait_ge(z["gate_sub"], 2)
                        dve.wait_ge(z["fir_ps"], i + 1)
                        for t in (2 * t2, 2 * t2 + 1):
                            fp = turned[i % 3][:, (t % 2) * D:(t % 2 + 1) * D].rearrange("p (h d) -> p h d", d=DH)
                            out = (sq if f else o)[:, t, :].rearrange("p (h d) -> p h d", d=DH)
                            last = nc.vector.tensor_tensor(out, fp, gl[:, t, :, f:f + 1].to_broadcast([P, H, DH]), ALU.mult)
                        last.then_inc(z["fir_used"], 1)
                        if f:
                            dve.wait_ge(z["fir_used"], i + 1)
                            link(nc.vector.tensor_tensor(o[:, 2 * t2:2 * t2 + 2, :], o[:, 2 * t2:2 * t2 + 2, :],
                                                         sq[:, 2 * t2:2 * t2 + 2, :], ALU.add))

                    taps(7)
                    inverse_start(0)
                    for lv in range(LEVELS):
                        level_mask(0, lv)
                        level_subtract(0, lv)
                        taps(1)
                    for t in range(NT):
                        if t + 1 < NT:
                            taps(2)
                            inverse_start(t + 1)
                        else:
                            taps(len(steps))
                            nc.vector.engine_nop().then_inc(z["fir_done"], 1)
                        for i in range(NC):
                            at = NC * t + i
                            lanes = slice(i * CH, (i + 1) * CH)
                            dve.wait_ge(z["ws_ps"], at + 1)
                            dve.wait_ge(z["uw_ready"], 2 * t + 2)
                            nc.vector.tensor_tensor(ua[lanes, :], u_t[lanes, :], pW[lanes, :], ALU.subtract)\
                                .then_inc(z["ua_ready"], 1)
                            if t + 1 < NT:
                                level_mask(t + 1, i)
                            dve.wait_ge(z["ks_ps"], at + 1)
                            if at == 0:
                                dve.wait_ge(z["s_zero"], 1)
                            nc.vector.tensor_tensor(S[:, :], S[:, :], pS, ALU.add).then_inc(z["s_ready"], 1)
                            if t + 1 < NT:
                                level_subtract(t + 1, i)
                                taps(1)
                            elif i < NC - 1:
                                gated_rows(2 * i)
                                gated_rows(2 * i + 1)
                    dve.wait_ge(z["o_ready"], 1)
                    nc.vector.tensor_tensor(o[:, :, :], o[:, :, :], do[:, :, :], ALU.add).then_inc(z["o_ready"], 1)
                    dve.wait_ge(z["o_sq"], 1)
                    nc.vector.tensor_reduce(ss["o"][:, :], hd(sq), AX.X, ALU.add).then_inc(z["o_ss"], 1)
                    dve.wait_ge(z["o_ilen"], 2)
                    nc.vector.tensor_tensor(hd(o), hd(o), per_head(ss["o"][:, :]), ALU.mult).then_inc(z["o_ready"], 1)
                    norm_in_vector(nc, dve, n, link)

                @block.scalar
                def _(act):
                    for i, s in enumerate("qkv"):
                        for k in range(KD):
                            act.wait_ge(z["proj_ps"], KD * i + k + 1)
                            nc.scalar.activation(xc[s][:, k, CONV - 1:], pb[2 + k][:, :], ACT.Copy).then_inc(z["xc_ready"], 1)
                    norm_out_scalar(nc, act, n, lambda t: pY[:, t, :])
                    for i, s in enumerate("qkv"):
                        act.wait_ge(z["conv_ready"], i + 1)
                        for k in range(KD):
                            nc.scalar.activation(xc_silu(s, k), xc_out(s, k), ACT.Silu).then_inc(z["c_ready"], 1)
                    act.wait_ge(z["gate_ps"], 1)
                    gps = pb[5][:, 0:NT * (NG + 1) * H].rearrange("p (t x) -> p t x", t=NT)
                    nc.scalar.activation(beta[:, :, :], gps[:, :, H * NG:], ACT.Sigmoid).then_inc(z["beta_ready"], 1)
                    for i in range(6):
                        act.wait_ge(z["row_ps"], i + 1)
                        s, t2 = "qkv"[i // 2], i % 2
                        nc.scalar.activation(r[s][:, 2 * t2:2 * t2 + 2, :].rearrange("p t d -> p (t d)"),
                                             turned[i % 4][:, :], ACT.Copy).then_inc(z["row_ready"], 1)
                    for i, s in enumerate("qk"):
                        act.wait_ge(z["row_ready"], 2 * (i + 1))
                        if i:
                            act.wait_ge(z["ss_ready"], 1)
                        nc.scalar.activation(sq[:, :, :], r[s][:, :, :], ACT.Square).then_inc(z["sq_ready"], 1)
                    act.wait_ge(z["gate_sub"], 1)
                    nc.scalar.activation(gl[:, :, :, :], gl[:, :, :, :], ACT.Exp).then_inc(z["gate_exp"], 1)
                    for i in range(3 * H):
                        act.wait_ge(z["hT_ps"], i + 1)
                        nc.scalar.activation(hT[("q", "k", "kb")[i // H]][:, i % H, :], turned[i % 4][0:DH, :], ACT.Copy)\
                            .then_inc(z["hT_ready"], 1)
                    def gt_copy(t):
                        act.wait_ge(z["g_ps"], t + 1)
                        nc.scalar.activation(GT[:, :, :].rearrange("p h j -> p (h j)"), pb[1][:, :], ACT.Copy)\
                            .then_inc(z["gt_ready"], 1)

                    made = [0]

                    def products(count):
                        for _ in range(count):
                            m = made[0]
                            if m > PRODS:
                                act.wait_ge(z["prod_used"], m - PRODS)
                            j = PE_TAPS + m
                            for k in range(KD):
                                nc.scalar.activation(prod[:, m % PRODS, k, :] if m else facc["l_pool"][:, k, :],
                                                     cT["v"][:, k, j:j + L], ACT.Copy, scale=fir["l"][:, k, j:j + 1])\
                                    .then_inc(z["prod_ready"], 1)
                            made[0] += 1

                    act.wait_ge(z["c_ready"], 3 * KD)
                    gt_copy(0)
                    products(POOL_TAPS - (NT - 1) * PRODS_OF_TILE)
                    for t in range(NT):
                        act.wait_ge(z["uw_ps"], t + 1)
                        nc.scalar.activation(u_t[:, :], pb[3][:, 0:D], ACT.Copy).then_inc(z["uw_ready"], 1)
                        nc.scalar.activation(wT[:, :, :].rearrange("p h j -> p (h j)"), pb[4][0:DH, :], ACT.Copy)\
                            .then_inc(z["uw_ready"], 1)
                        if t + 1 < NT:
                            gt_copy(t + 1)
                            products(PRODS_OF_TILE)
                        act.wait_ge(z["do_ps"], t + 1)
                        nc.scalar.activation(do[:, t, :], pb[5][:, 0:D], ACT.Copy).then_inc(z["do_ready"], 1)
                        if t % 2 == 0:
                            act.wait_ge(z["firp_ps"], t // 2 + 1)
                            nc.scalar.activation(facc["l_pe"][:, t // 2, :].rearrange("p (a d) -> p a d", a=2), pF,
                                                 ACT.Copy).then_inc(z["firp_ready"], 1)
                    act.wait_ge(z["o_ready"], 2)
                    nc.scalar.activation(sq[:, :, :], o[:, :, :], ACT.Square).then_inc(z["o_sq"], 1)
                    for k in range(KD):
                        act.wait_ge(z["oT_ps"], k + 1)
                        nc.scalar.activation(oT[:, k, :], pb[k][:, :], ACT.Copy).then_inc(z["oT_ready"], 1)
                    norm_in_evacuate(nc, act, n, pb)

                @block.tensor
                def _(pe):
                    for i, s in enumerate("qkv"):
                        for m in range(KD):
                            if i:
                                pe.wait_ge(z["xc_ready"], KD * (i - 1) + m + 1)
                            for k in range(KD):
                                last = nc.tensor.matmul(pb[2 + m][:, :], wt[s][:, k, m * P:(m + 1) * P], n.xnT[:, k, :],
                                                        start=(k == 0), stop=(k == KD - 1))
                            last.then_inc(z["proj_ps"], 1)
                    NGH = H * (NG + 1)
                    for t in range(NT):
                        for k in range(KD):
                            last = nc.tensor.matmul(pb[5][:, t * NGH:(t + 1) * NGH], n.xnT[:, k, t * P:(t + 1) * P],
                                                    wg[:, k, :], start=(k == 0), stop=(k == KD - 1))
                    last.then_inc(z["gate_ps"], 1)
                    for i in range(6):
                        s, t2 = "qkv"[i // 2], i % 2
                        past = PAST if s == "v" else 0
                        pe.wait_ge(z["c_ready"], KD * (i // 2) + KD)
                        if i >= 4:
                            pe.wait_ge(z["row_ready"], i - 3)
                        for t in (2 * t2, 2 * t2 + 1):
                            for k in range(KD):
                                at = (t % 2) * D + k * P
                                last = nc.tensor.transpose(turned[i % 4][:, at:at + P],
                                                           cT[s][:, k, past + t * P:past + (t + 1) * P], c.ident[:, :])
                        last.then_inc(z["row_ps"], 1)
                    pe.wait_ge(z["row_ready"], 6)
                    for i in range(3 * H):
                        rows_of, done = ((r["q"], 1), (r["k"], 2), (kb, 3))[i // H]
                        pe.wait_ge(z["rows_ready"], done)
                        if i >= 4:
                            pe.wait_ge(z["hT_ready"], i - 3)
                        for t in range(NT):
                            last = nc.tensor.transpose(turned[i % 4][0:DH, t * P:(t + 1) * P],
                                                       rows_of[:, t, (i % H) * DH:(i % H + 1) * DH], c.ident[:, :])
                        last.then_inc(z["hT_ps"], 1)
                    pe.wait_ge(z["hT_ready"], 3 * H)
                    pe.wait_ge(z["rows_ready"], 4)
                    pe.wait_ge(n.yn_ready, NT)
                    pe.wait_ge(z["s_zero"], 1)
                    pe.wait_ge(z["beta_ready"], 1)
                    pe.wait_ge(z["gate_sub"], 1)

                    def inverse_start(t):
                        tok = slice(t * P, (t + 1) * P)
                        if t:
                            pe.wait_ge(z["t_ready"], (LEVELS + 1) * t)
                        for h in range(H):
                            out = slice(h * P, (h + 1) * P)
                            q, k, kbh = (hT[s][:, h, tok] for s in ("q", "k", "kb"))
                            nc.tensor.matmul(pb[0][:, out], kbh, k, start=True, stop=True)
                            nc.tensor.matmul(pb[1][:, out], k, kbh, start=True, stop=True)
                            last = nc.tensor.matmul(pb[2][:, out], k, q, start=True, stop=True)
                        last.then_inc(z["g_ps"], 1)

                    def level_cross(t, lv):
                        pe.wait_ge(z["t_ready"], (LEVELS + 1) * t + lv + 1)
                        if lv == 0:
                            pe.wait_ge(z["gt_ready"], t + 1)
                            pe.wait_ge(z["attn_ready"], t + 1)
                        for h in range(H):
                            last = nc.tensor.matmul(pb[0][:, h * P:(h + 1) * P], GT[:, h, :], Tm[:, h, :],
                                                    start=True, stop=True)
                        last.then_inc(z["x_ps"], 1)

                    def level_join(t, lv):
                        pe.wait_ge(z["x_masked"], LEVELS * t + lv + 1)
                        for h in range(H):
                            if lv < LEVELS - 1:
                                nc.tensor.matmul(pb[1][:, h * P:(h + 1) * P], TT[:, h, :], X[:, h, :],
                                                 start=True, stop=True)
                            last = nc.tensor.matmul(pb[2][:, h * P:(h + 1) * P], X[:, h, :], TT[:, h, :],
                                                    start=True, stop=True)
                        last.then_inc(z["tx_ps"], 1)

                    def fir_taps(at):
                        half = NT * NC // KD
                        k, i = at // half, at % half
                        if k and i == 0:
                            pe.wait_ge(z["firp_ready"], k)
                        for j in range(i * PE_TAPS // half, (i + 1) * PE_TAPS // half):
                            last = nc.tensor.matmul(pF, diag[:, k, j, :],
                                                    cT["v"][:, k, j:j + L].rearrange("p (a d) -> p a d", a=2),
                                                    start=(j == 0), stop=(j == PE_TAPS - 1), skip_group_check=True)
                        if i == half - 1:
                            last.then_inc(z["firp_ps"], 1)

                    def filter_rows(i):
                        parts = (("s",), ("m",), ("l", "l_pe", "l_pool"))[i // 2]
                        t2 = i % 2
                        if i == 0:
                            pe.wait_ge(z["fir_done"], 1)
                        if i == 4:
                            pe.wait_ge(z["firp_ready"], KD)
                            pe.wait_ge(z["pool_taps_done"], 1)
                        if i >= 3:
                            pe.wait_ge(z["fir_used"], i - 2)
                        for t in (2 * t2, 2 * t2 + 1):
                            for k in range(KD):
                                at = (t % 2) * D + k * P
                                for part in parts:
                                    last = nc.tensor.matmul(turned[i % 3][:, at:at + P],
                                                            facc[part][:, k, t * P:(t + 1) * P],
                                                            c.ident[:, :], start=(part == parts[0]),
                                                            stop=(part == parts[-1]))
                        last.then_inc(z["fir_ps"], 1)

                    inverse_start(0)
                    for lv in range(LEVELS):
                        level_cross(0, lv)
                        level_join(0, lv)
                        fir_taps(lv)
                    for t in range(NT):
                        pe.wait_ge(z["t_ready"], (LEVELS + 1) * (t + 1))
                        for h in range(H):
                            cols = slice(h * DH, (h + 1) * DH)
                            nc.tensor.matmul(pb[3][:, cols], TT[:, h, :], vb[:, t, cols], start=True, stop=True)
                            last = nc.tensor.matmul(pb[4][0:DH, h * P:(h + 1) * P], kb[:, t, cols], TT[:, h, :],
                                                    start=True, stop=True)
                        last.then_inc(z["uw_ps"], 1)
                        if t + 1 < NT:
                            inverse_start(t + 1)
                        pe.wait_ge(z["uw_ready"], 2 * t + 2)
                        for i in range(NC):
                            at = NC * t + i
                            lanes = slice(i * CH, (i + 1) * CH)
                            if at:
                                pe.wait_ge(z["s_ready"], at)
                            for h in range(H):
                                cols = slice(h * DH, (h + 1) * DH)
                                last = nc.tensor.matmul(pW[lanes, cols], wT[:, h, lanes], S[:, cols], start=True, stop=True)
                            last.then_inc(z["ws_ps"], 1)
                            if t + 1 < NT:
                                level_cross(t + 1, i)
                            if t and i == 0:
                                pe.wait_ge(z["do_ready"], t)
                            for h in range(H):
                                cols = slice(h * DH, (h + 1) * DH)
                                nc.tensor.matmul(pb[5][lanes, cols], hT["q"][:, h, t * P + i * CH:t * P + (i + 1) * CH],
                                                 S[:, cols], start=(h == 0), stop=False, skip_group_check=True)
                            pe.wait_ge(z["ua_ready"], at + 1)
                            for h in range(H):
                                cols = slice(h * DH, (h + 1) * DH)
                                last = nc.tensor.matmul(pS[:, cols], r["k"][lanes, t, cols], ua[lanes, cols],
                                                        start=True, stop=True)
                            last.then_inc(z["ks_ps"], 1)
                            if t + 1 < NT:
                                level_join(t + 1, i)
                                fir_taps(LEVELS + at)
                            elif i < NC - 1:
                                filter_rows(2 * i)
                                filter_rows(2 * i + 1)
                        for h in range(H):
                            cols = slice(h * DH, (h + 1) * DH)
                            last = nc.tensor.matmul(pb[5][:, cols], attnT[:, t % 2, h, :], ua[:, cols], start=False,
                                                    stop=True, skip_group_check=True)
                        last.then_inc(z["do_ps"], 1)
                    pe.wait_ge(z["o_ready"], 3)
                    for k in range(KD):
                        for t in range(NT):
                            last = nc.tensor.transpose(pb[k][:, t * P:(t + 1) * P], o[:, t, k * P:(k + 1) * P], c.ident[:, :])
                        last.then_inc(z["oT_ps"], 1)
                    pe.wait_ge(z["oT_ready"], KD)
                    pe.wait_ge(z["s_ready"], NT * NC)
                    for t in range(NT):
                        for k in range(KD):
                            last = nc.tensor.matmul(pY[:, t, :], oT[:, k, t * P:(t + 1) * P], wt["o"][:, k, :],
                                                    start=(k == 0), stop=(k == KD - 1))
                    last.then_inc(z["y_ps"], 1)
                    norm_in_tensor(nc, pe, n, pb, c.ident)

                @block.gpsimd
                def _(pool):
                    norm_out_pool(nc, pool, n, c)
                    link = Chain(pool, z["pch"]).link
                    nc.gpsimd.memset(S[:, :], 0.0).then_inc(z["s_zero"], 1)
                    for i, s in enumerate("qk"):
                        pool.wait_ge(z["ss_ready"], i + 1)
                        nc.gpsimd.tensor_scalar(ss[s][:, :], ss[s][:, :], 1e-6, None, ALU.add).then_inc(z["ilen_ready"], 1)
                        pool.wait_ge(z["ilen_ready"], 2 * i + 1)
                        nc.gpsimd.tensor_tensor(ss[s][:, :], ss[s][:, :], c.minus_half[:, 0:NT * H], ALU.pow)\
                            .then_inc(z["ilen_ready"], 1)
                    for m in range(1, POOL_TAPS):
                        pool.wait_ge(z["prod_ready"], KD * (m + 1))
                        if m > 1:
                            pool.wait_ge(z["prod_used"], m - 1)
                        nc.gpsimd.tensor_tensor(facc["l_pool"][:, :, :], facc["l_pool"][:, :, :],
                                                prod[:, m % PRODS, :, :], ALU.add).then_inc(z["prod_used"], 1)
                    pool.wait_ge(z["prod_used"], POOL_TAPS - 1)
                    nc.gpsimd.engine_nop().then_inc(z["pool_taps_done"], 1)
                    pool.wait_ge(z["gate_sub"], 2)
                    pool.wait_ge(z["rows_ready"], 4)

                    def gated(a, t, g):
                        a3 = a[:, t, :].rearrange("p (h d) -> p h d", d=DH)
                        return nc.gpsimd.tensor_tensor(a3, a3, gl[:, t, :, g:g + 1].to_broadcast([P, H, DH]), ALU.mult)

                    for t in range(NT):
                        last = gated(r["v"], t, 4)
                    link(last)
                    for t in range(NT):
                        pool.wait_ge(z["do_ready"], t + 1)
                        link(gated(do, t, 3))
                        last = nc.gpsimd.tensor_tensor(do[:, t, :], do[:, t, :], r["v"][:, t, :], ALU.add)
                    last.then_inc(z["o_ready"], 1)
                    pool.wait_ge(z["o_ss"], 1)
                    nc.gpsimd.tensor_scalar(ss["o"][:, :], ss["o"][:, :], 1.0 / DH, 1e-5, ALU.mult, ALU.add)\
                        .then_inc(z["o_ilen"], 1)
                    pool.wait_ge(z["o_ilen"], 1)
                    nc.gpsimd.tensor_tensor(ss["o"][:, :], ss["o"][:, :], c.minus_half[:, 0:NT * H], ALU.pow)\
                        .then_inc(z["o_ilen"], 1)
                    norm_in_pool(nc, pool, n, c)
            sc.clear()
        last_norm(nc, sc, n, src, dst, c, lambda t: pY[:, t, :], z["dch"])


_TRANSPOSED = ("L2_ffn_w_gate", "L2_ffn_w_up", "L2_ffn_w_down", "L2_attn_Wq", "L2_attn_Wk", "L2_attn_Wv", "L2_attn_Wo",
               "L3_attn_W_in", "L3_attn_W_xproj", "L3_attn_W_dt", "L3_attn_W_out", "L1_ffn_Wr",
               "L0_attn_Wq", "L0_attn_Wk", "L0_attn_Wv", "L0_attn_Wo", "L0_attn_Wb", "L0_attn_gate_w")


def positions(tokens, d):
    pos = np.arange(tokens, dtype=np.float32)[None, :]
    freq = np.exp((-np.log(10000.0) * np.arange(0, d, 2) / d).astype(np.float32)).astype(np.float32)
    out = np.zeros((d, tokens), np.float32)
    out[0::2] = np.sin(freq[:, None] * pos)
    out[1::2] = np.cos(freq[:, None] * pos)
    return out


def chunk_masks(chunk):
    i, j = np.arange(P)[:, None], np.arange(P)[None, :]

    def lower(s):
        return ((i // (2 * s) == j // (2 * s)) & (i // s % 2 == 1) & (j // s % 2 == 0)).astype(np.float32)

    s, m = 2, [-lower(1), -lower(1).T]
    while s < chunk:
        m.append(lower(s))
        s *= 2
    m.append(((i // chunk == j // chunk) & (i <= j)).astype(np.float32))
    return np.ascontiguousarray(np.stack(m, 1))


def build(nc, w, out):
    ctx = ExitStack()
    with ctx:
        c = constants(nc, ctx)
        stages = {0: stage_delta, 1: stage_tanh_mlp, 2: stage_mqa, 3: stage_expert_choice, 4: stage_silu_mha, 5: stage_int_swiglu, 6: stage_mamba, 7: stage_moe_top2}
        res = [nc.dram_tensor(f"residual{i}", [NB, L, D], F32, kind="Internal").ap() for i in range(2)]
        src = w["L0_attn_hidden_states"]
        for s in STAGES:
            dst = out if s == STAGES[-1] else res[s % 2]
            stages[s](nc, w, src, dst, c)
            src = dst


def kernel(**inputs):
    import numpy as _np
    import concourse.bacc as _bacc
    from concourse import mybir as _mybir
    from concourse.bass_utils import run_bass_kernel_spmd as _run

    nc = _bacc.Bacc("TRN2", target_bir_lowering=False, num_devices=1)
    arrays, w = {}, {}
    for name, v in inputs.items():
        a = _np.asarray(v)
        if name in _TRANSPOSED:
            a = _np.swapaxes(a, -1, -2)
        a = _np.ascontiguousarray(a)
        arrays["in_" + name] = a
        w[name] = nc.dram_tensor("in_" + name, a.shape, _mybir.dt.from_np(a.dtype), kind="ExternalInput").ap()
    constants_of_shapes = {"positions": positions(L, P), "chunk_masks": chunk_masks(32)}
    for name, a in constants_of_shapes.items():
        arrays[name] = a
        w[name] = nc.dram_tensor(name, a.shape, _mybir.dt.float32, kind="ExternalInput").ap()
    out = nc.dram_tensor("out_0", (NB, L, D), _mybir.dt.float32, kind="ExternalOutput").ap()
    build(nc, w, out)
    r = _run(nc, [arrays], core_ids=[0])
    return r.results[0]["out_0"]
```
